# Optimizing a Trainium2 kernel written in Bass

```python
import numpy as np
import jax
import jax.numpy as jnp

def _softmax(x, axis=-1):
    return jax.nn.softmax(x, axis=axis)

def _gelu(x):
    return jax.nn.gelu(x, approximate=True)

def _silu(x):
    return jax.nn.silu(x)

def _sigmoid(x):
    return jax.nn.sigmoid(x)

def _layernorm(x, axis=-1, eps=1e-05):
    m = jnp.mean(x, axis=axis, keepdims=True)
    v = jnp.var(x, axis=axis, keepdims=True)
    return (x - m) / jnp.sqrt(v + eps)

def _scatter_add(tgt, idx, src, axis=0):
    return tgt.at[idx].add(src)

def _segment_sum(src, seg, n):
    return jax.ops.segment_sum(src, seg, n)
kernel_name = 'mk_gnn_ffn_d2_gnn_r32_1ab6b6'

def setup_inputs(seed: int=0):
    np.random.seed(seed)
    _w = jnp.asarray

    def _rec_inputs():
        import jax
        import jax.numpy as jnp
        _gk = jax.random.key(seed)
        x = -0.000364 + 1 * jax.random.normal(jax.random.fold_in(_gk, 1), (625, 768), jnp.float32)
        src = jax.random.randint(jax.random.fold_in(_gk, 2), (10000,), 0, 625, jnp.int32)
        dst = jax.random.randint(jax.random.fold_in(_gk, 3), (10000,), 0, 625, jnp.int32)
        _o = jnp.argsort(dst, stable=True)
        src = src[_o]
        dst = dst[_o]
        return (x, src, dst)
    x, src, dst = _rec_inputs()

    def _L0_gnn_setup():
        import jax, jax.numpy as jnp
        import numpy as np
        N, E, DIM, HEADS = (625, 10000, 768, 8)
        HD = DIM // HEADS
        EPS = 1e-05

        def layer_norm(x, w, b):
            mu = jnp.mean(x, axis=-1, keepdims=True)
            var = jnp.var(x, axis=-1, keepdims=True)
            return (x - mu) * jax.lax.rsqrt(var + EPS) * w + b

        def gatv2(x, src, dst, Ws, bs, Wd, bd, attn):
            H, D = attn.shape
            fs = (x @ Ws + bs).reshape(-1, H, D)
            fd = (x @ Wd + bd).reshape(-1, H, D)
            e = jax.nn.leaky_relu(fs[src] + fd[dst], 0.2)
            logits = jnp.einsum('ehd,hd->eh', e, attn)
            m = jax.ops.segment_max(logits, dst, num_segments=N)
            ex = jnp.exp(logits - m[dst])
            denom = jax.ops.segment_sum(ex, dst, num_segments=N)
            alpha = ex / denom[dst]
            out = jax.ops.segment_sum(alpha[:, :, None] * fs[src], dst, num_segments=N)
            return jax.nn.elu(out)
        key = jax.random.key(seed)
        ks = jax.random.split(key, 10)
        s = 1.0 / np.sqrt(DIM)
        return {'x': jax.random.normal(ks[0], (N, DIM), jnp.float32), 'src': jax.random.randint(ks[1], (E,), 0, N, jnp.int32), 'dst': jax.random.randint(ks[2], (E,), 0, N, jnp.int32), 'W1s': jax.random.normal(ks[3], (DIM, DIM), jnp.float32) * s, 'b1s': jnp.zeros((DIM,), jnp.float32), 'W1d': jax.random.normal(ks[4], (DIM, DIM), jnp.float32) * s, 'b1d': jnp.zeros((DIM,), jnp.float32), 'attn1': jax.random.normal(ks[5], (HEADS, HD), jnp.float32) * s, 'ln1_w': jnp.ones((DIM,), jnp.float32), 'ln1_b': jnp.zeros((DIM,), jnp.float32), 'Wos': jax.random.normal(ks[6], (DIM, DIM), jnp.float32) * s, 'bos': jnp.zeros((DIM,), jnp.float32), 'Wod': jax.random.normal(ks[7], (DIM, DIM), jnp.float32) * s, 'bod': jnp.zeros((DIM,), jnp.float32), 'attno': jax.random.normal(ks[8], (1, DIM), jnp.float32) * s, 'lno_w': jnp.ones((DIM,), jnp.float32), 'lno_b': jnp.zeros((DIM,), jnp.float32)}
    _L0_gnn_all = _L0_gnn_setup()
    _L0_gnn_in = {k: v for k, v in _L0_gnn_all.items() if k in ('W1s', 'b1s', 'W1d', 'b1d', 'attn1', 'ln1_w', 'ln1_b', 'Wos', 'bos', 'Wod', 'bod', 'attno', 'lno_w', 'lno_b')}
    del _L0_gnn_all

    def _L0_ffn_setup():
        import jax, jax.numpy as jnp
        import numpy as np
        KNN = 16
        BN_EPS = 1e-05

        def _swiglu(z, w1, w2, w3):
            return jax.nn.silu(z @ w1.T) * (z @ w3.T) @ w2.T
        key = jax.random.key(seed)
        ks = jax.random.split(key, 12)
        B, T, D = (1, 64, 768)
        H, N, KD = (4, 800, 128)
        HID_A, HID_S = (44, 1024)
        inp = {'x': jax.random.normal(ks[0], (B, T, D), jnp.float32), 'wq': jax.random.normal(ks[1], (H * KD, D), jnp.float32) * (1.0 / np.sqrt(D)), 'bq': jax.random.normal(ks[2], (H * KD,), jnp.float32) * 0.02, 'bn_gamma': jnp.ones((H * KD,), jnp.float32), 'bn_beta': jnp.zeros((H * KD,), jnp.float32), 'bn_mean': jnp.zeros((H * KD,), jnp.float32), 'bn_var': jnp.ones((H * KD,), jnp.float32), 'keys': jax.random.uniform(ks[3], (H, N, KD), jnp.float32, -1.0 / np.sqrt(KD), 1.0 / np.sqrt(KD)), 'w_down_tab': jax.random.normal(ks[4], (N, 1), jnp.float32) * 0.02, 'w_up_tab': jax.random.normal(ks[5], (N, 1), jnp.float32) * 0.02, 'a_w1': jax.random.normal(ks[6], (HID_A, KNN), jnp.float32) * (1.0 / np.sqrt(KNN)), 'a_w2': jax.random.normal(ks[7], (KNN, HID_A), jnp.float32) * (1.0 / np.sqrt(HID_A)), 'a_w3': jax.random.normal(ks[8], (HID_A, KNN), jnp.float32) * (1.0 / np.sqrt(KNN)), 's_w1': jax.random.normal(ks[9], (HID_S, D), jnp.float32) * (1.0 / np.sqrt(D)), 's_w2': jax.random.normal(ks[10], (D, HID_S), jnp.float32) * (1.0 / np.sqrt(HID_S)), 's_w3': jax.random.normal(ks[11], (HID_S, D), jnp.float32) * (1.0 / np.sqrt(D))}
        return inp
    _L0_ffn_all = _L0_ffn_setup()
    _L0_ffn_in = {k: v for k, v in _L0_ffn_all.items() if k in ('wq', 'bq', 'bn_gamma', 'bn_beta', 'bn_mean', 'bn_var', 'keys', 'w_down_tab', 'w_up_tab', 'a_w1', 'a_w2', 'a_w3', 's_w1', 's_w2', 's_w3')}
    del _L0_ffn_all

    def _L1_gnn_setup():
        import jax, jax.numpy as jnp
        import numpy as np
        N_NODES = 10000
        N_EDGES = 3125
        DIM = 768
        NEG_SLOPE = 0.2

        def gat_conv(x, src, dst, W, att_src, att_dst, bias, num_nodes):
            h = x @ W
            a_s = h @ att_src
            a_d = h @ att_dst
            e = jax.nn.leaky_relu(a_s[src] + a_d[dst], NEG_SLOPE)
            m = jax.ops.segment_max(e, dst, num_segments=num_nodes)
            e = jnp.exp(e - m[dst])
            denom = jax.ops.segment_sum(e, dst, num_segments=num_nodes)
            alpha = e / denom[dst]
            msg = alpha[:, None] * h[src]
            out = jax.ops.segment_sum(msg, dst, num_segments=num_nodes)
            return out + bias
        key = jax.random.key(seed)
        ks = jax.random.split(key, 12)
        s = 1.0 / np.sqrt(DIM)
        inp = {'x': jax.random.normal(ks[0], (N_NODES, DIM), dtype=jnp.float32), 'edge_index': jax.random.randint(ks[1], (2, N_EDGES), 0, N_NODES, dtype=jnp.int64), 'W1': jax.random.normal(ks[2], (DIM, DIM), dtype=jnp.float32) * s, 'att_src1': jax.random.normal(ks[3], (DIM,), dtype=jnp.float32) * s, 'att_dst1': jax.random.normal(ks[4], (DIM,), dtype=jnp.float32) * s, 'b1': jnp.zeros((DIM,), dtype=jnp.float32), 'W2': jax.random.normal(ks[5], (DIM, DIM), dtype=jnp.float32) * s, 'att_src2': jax.random.normal(ks[6], (DIM,), dtype=jnp.float32) * s, 'att_dst2': jax.random.normal(ks[7], (DIM,), dtype=jnp.float32) * s, 'b2': jnp.zeros((DIM,), dtype=jnp.float32)}
        return inp
    _L1_gnn_all = _L1_gnn_setup()
    _L1_gnn_in = {k: v for k, v in _L1_gnn_all.items() if k in ('W1', 'att_src1', 'att_dst1', 'b1', 'W2', 'att_src2', 'att_dst2', 'b2')}
    del _L1_gnn_all

    def _L1_ffn_setup():
        import jax, jax.numpy as jnp
        import numpy as np
        G, E = (4, 8)
        KG, KE = (2, 2)
        D, M = (768, 96)
        SCALE = 0.02

        def _combine_weights(xf, Wg, bg, Wge, bge):
            N = xf.shape[0]
            glog = xf @ Wg + bg
            gtop, gidx = jax.lax.top_k(glog, KG)
            ggate = jax.nn.softmax(gtop, axis=-1)
            elog_all = jnp.einsum('nd,gde->nge', xf, Wge) + bge
            elog = jnp.take_along_axis(elog_all, gidx[:, :, None], axis=1)
            etop, eidx = jax.lax.top_k(elog, KE)
            egate = jax.nn.softmax(etop, axis=-1)
            w = ggate[:, :, None] * egate
            flat = gidx[:, :, None] * E + eidx
            comb = jnp.zeros((N, G * E), xf.dtype).at[jnp.arange(N)[:, None, None], flat].add(w)
            return comb
        key = jax.random.key(seed)
        ks = jax.random.split(key, 8)
        x = jax.random.normal(ks[0], (1, 512, D), jnp.float32)
        Wg = jax.random.normal(ks[1], (D, G), jnp.float32) * SCALE
        bg = jnp.zeros((G,), jnp.float32)
        Wge = jax.random.normal(ks[2], (G, D, E), jnp.float32) * SCALE
        bge = jnp.zeros((G, E), jnp.float32)
        W1 = jax.random.normal(ks[3], (G * E, D, M), jnp.float32) * SCALE
        b1 = jnp.zeros((G * E, M), jnp.float32)
        W2 = jax.random.normal(ks[4], (G * E, M, D), jnp.float32) * SCALE
        b2 = jnp.zeros((G * E, D), jnp.float32)
        return {'x': x, 'Wg': Wg, 'bg': bg, 'Wge': Wge, 'bge': bge, 'W1': W1, 'b1': b1, 'W2': W2, 'b2': b2}
    _L1_ffn_all = _L1_ffn_setup()
    _L1_ffn_in = {k: v for k, v in _L1_ffn_all.items() if k in ('Wg', 'bg', 'Wge', 'bge', 'W1', 'b1', 'W2', 'b2')}
    del _L1_ffn_all
    return {'x': x, 'src': src, 'dst': dst, 'L0_gnn_W1s': _L0_gnn_in['W1s'], 'L0_gnn_b1s': _L0_gnn_in['b1s'], 'L0_gnn_W1d': _L0_gnn_in['W1d'], 'L0_gnn_b1d': _L0_gnn_in['b1d'], 'L0_gnn_attn1': _L0_gnn_in['attn1'], 'L0_gnn_ln1_w': _L0_gnn_in['ln1_w'], 'L0_gnn_ln1_b': _L0_gnn_in['ln1_b'], 'L0_gnn_Wos': _L0_gnn_in['Wos'], 'L0_gnn_bos': _L0_gnn_in['bos'], 'L0_gnn_Wod': _L0_gnn_in['Wod'], 'L0_gnn_bod': _L0_gnn_in['bod'], 'L0_gnn_attno': _L0_gnn_in['attno'], 'L0_gnn_lno_w': _L0_gnn_in['lno_w'], 'L0_gnn_lno_b': _L0_gnn_in['lno_b'], 'L0_ffn_wq': _L0_ffn_in['wq'], 'L0_ffn_bq': _L0_ffn_in['bq'], 'L0_ffn_bn_gamma': _L0_ffn_in['bn_gamma'], 'L0_ffn_bn_beta': _L0_ffn_in['bn_beta'], 'L0_ffn_bn_mean': _L0_ffn_in['bn_mean'], 'L0_ffn_bn_var': _L0_ffn_in['bn_var'], 'L0_ffn_keys': _L0_ffn_in['keys'], 'L0_ffn_w_down_tab': _L0_ffn_in['w_down_tab'], 'L0_ffn_w_up_tab': _L0_ffn_in['w_up_tab'], 'L0_ffn_a_w1': _L0_ffn_in['a_w1'], 'L0_ffn_a_w2': _L0_ffn_in['a_w2'], 'L0_ffn_a_w3': _L0_ffn_in['a_w3'], 'L0_ffn_s_w1': _L0_ffn_in['s_w1'], 'L0_ffn_s_w2': _L0_ffn_in['s_w2'], 'L0_ffn_s_w3': _L0_ffn_in['s_w3'], 'L1_gnn_W1': _L1_gnn_in['W1'], 'L1_gnn_att_src1': _L1_gnn_in['att_src1'], 'L1_gnn_att_dst1': _L1_gnn_in['att_dst1'], 'L1_gnn_b1': _L1_gnn_in['b1'], 'L1_gnn_W2': _L1_gnn_in['W2'], 'L1_gnn_att_src2': _L1_gnn_in['att_src2'], 'L1_gnn_att_dst2': _L1_gnn_in['att_dst2'], 'L1_gnn_b2': _L1_gnn_in['b2'], 'L1_ffn_Wg': _L1_ffn_in['Wg'], 'L1_ffn_bg': _L1_ffn_in['bg'], 'L1_ffn_Wge': _L1_ffn_in['Wge'], 'L1_ffn_bge': _L1_ffn_in['bge'], 'L1_ffn_W1': _L1_ffn_in['W1'], 'L1_ffn_b1': _L1_ffn_in['b1'], 'L1_ffn_W2': _L1_ffn_in['W2'], 'L1_ffn_b2': _L1_ffn_in['b2']}

def reference(x, src, dst, L0_gnn_W1s, L0_gnn_b1s, L0_gnn_W1d, L0_gnn_b1d, L0_gnn_attn1, L0_gnn_ln1_w, L0_gnn_ln1_b, L0_gnn_Wos, L0_gnn_bos, L0_gnn_Wod, L0_gnn_bod, L0_gnn_attno, L0_gnn_lno_w, L0_gnn_lno_b, L0_ffn_wq, L0_ffn_bq, L0_ffn_bn_gamma, L0_ffn_bn_beta, L0_ffn_bn_mean, L0_ffn_bn_var, L0_ffn_keys, L0_ffn_w_down_tab, L0_ffn_w_up_tab, L0_ffn_a_w1, L0_ffn_a_w2, L0_ffn_a_w3, L0_ffn_s_w1, L0_ffn_s_w2, L0_ffn_s_w3, L1_gnn_W1, L1_gnn_att_src1, L1_gnn_att_dst1, L1_gnn_b1, L1_gnn_W2, L1_gnn_att_src2, L1_gnn_att_dst2, L1_gnn_b2, L1_ffn_Wg, L1_ffn_bg, L1_ffn_Wge, L1_ffn_bge, L1_ffn_W1, L1_ffn_b1, L1_ffn_W2, L1_ffn_b2):
    import jax
    import jax.numpy as jnp

    def _L0_gnn_ref(x, src, dst, W1s, b1s, W1d, b1d, attn1, ln1_w, ln1_b, Wos, bos, Wod, bod, attno, lno_w, lno_b):
        import jax, jax.numpy as jnp
        import numpy as np
        N, E, DIM, HEADS = (625, 10000, 768, 8)
        HD = DIM // HEADS
        EPS = 1e-05

        def layer_norm(x, w, b):
            mu = jnp.mean(x, axis=-1, keepdims=True)
            var = jnp.var(x, axis=-1, keepdims=True)
            return (x - mu) * jax.lax.rsqrt(var + EPS) * w + b

        def gatv2(x, src, dst, Ws, bs, Wd, bd, attn):
            H, D = attn.shape
            fs = (x @ Ws + bs).reshape(-1, H, D)
            fd = (x @ Wd + bd).reshape(-1, H, D)
            e = jax.nn.leaky_relu(fs[src] + fd[dst], 0.2)
            logits = jnp.einsum('ehd,hd->eh', e, attn)
            m = jax.ops.segment_max(logits, dst, num_segments=N)
            ex = jnp.exp(logits - m[dst])
            denom = jax.ops.segment_sum(ex, dst, num_segments=N)
            alpha = ex / denom[dst]
            out = jax.ops.segment_sum(alpha[:, :, None] * fs[src], dst, num_segments=N)
            return jax.nn.elu(out)
        h = gatv2(x, src, dst, W1s, b1s, W1d, b1d, attn1).reshape(N, DIM)
        h = layer_norm(h + x, ln1_w, ln1_b)
        out = gatv2(h, src, dst, Wos, bos, Wod, bod, attno).reshape(N, DIM)
        return layer_norm(out, lno_w, lno_b)

    def _L0_ffn_ref(x, wq, bq, bn_gamma, bn_beta, bn_mean, bn_var, keys, w_down_tab, w_up_tab, a_w1, a_w2, a_w3, s_w1, s_w2, s_w3):
        import jax, jax.numpy as jnp
        import numpy as np
        KNN = 16
        BN_EPS = 1e-05

        def _swiglu(z, w1, w2, w3):
            return jax.nn.silu(z @ w1.T) * (z @ w3.T) @ w2.T
        B, T, D = x.shape
        H, N, KD = keys.shape
        identity = x
        q = x.reshape(-1, D) @ wq.T + bq
        q = (q - bn_mean) * jax.lax.rsqrt(bn_var + BN_EPS) * bn_gamma + bn_beta
        q = q.reshape(-1, H, KD)
        scores = jnp.einsum('bhk,hnk->bhn', q, keys)
        top_s, top_i = jax.lax.top_k(scores, KNN)
        gates = jax.nn.softmax(top_s, axis=-1)
        idx = top_i.reshape(B, T, H, KNN)
        gates = gates.reshape(B, T, H, KNN)
        w_down = w_down_tab[idx, 0]
        w_up = w_up_tab[idx, 0]
        xd = jnp.sum(x, axis=-1)[:, :, None, None] * w_down
        h = _swiglu(xd, a_w1, a_w2, a_w3)
        h = h * gates
        comb = jnp.sum(h * w_up, axis=(2, 3))[:, :, None]
        out = comb + _swiglu(identity, s_w1, s_w2, s_w3)
        return out

    def _L1_gnn_ref(x, edge_index, W1, att_src1, att_dst1, b1, W2, att_src2, att_dst2, b2):
        import jax, jax.numpy as jnp
        import numpy as np
        N_NODES = 10000
        N_EDGES = 3125
        DIM = 768
        NEG_SLOPE = 0.2

        def gat_conv(x, src, dst, W, att_src, att_dst, bias, num_nodes):
            h = x @ W
            a_s = h @ att_src
            a_d = h @ att_dst
            e = jax.nn.leaky_relu(a_s[src] + a_d[dst], NEG_SLOPE)
            m = jax.ops.segment_max(e, dst, num_segments=num_nodes)
            e = jnp.exp(e - m[dst])
            denom = jax.ops.segment_sum(e, dst, num_segments=num_nodes)
            alpha = e / denom[dst]
            msg = alpha[:, None] * h[src]
            out = jax.ops.segment_sum(msg, dst, num_segments=num_nodes)
            return out + bias
        n = x.shape[0]
        loops = jnp.arange(n, dtype=edge_index.dtype)
        src = jnp.concatenate([edge_index[0], loops])
        dst = jnp.concatenate([edge_index[1], loops])
        h = gat_conv(x, src, dst, W1, att_src1, att_dst1, b1, n)
        h = jax.nn.relu(h)
        out = gat_conv(h, src, dst, W2, att_src2, att_dst2, b2, n)
        return out

    def _L1_ffn_ref(x, Wg, bg, Wge, bge, W1, b1, W2, b2):
        import jax, jax.numpy as jnp
        import numpy as np
        G, E = (4, 8)
        KG, KE = (2, 2)
        D, M = (768, 96)
        SCALE = 0.02

        def _combine_weights(xf, Wg, bg, Wge, bge):
            N = xf.shape[0]
            glog = xf @ Wg + bg
            gtop, gidx = jax.lax.top_k(glog, KG)
            ggate = jax.nn.softmax(gtop, axis=-1)
            elog_all = jnp.einsum('nd,gde->nge', xf, Wge) + bge
            elog = jnp.take_along_axis(elog_all, gidx[:, :, None], axis=1)
            etop, eidx = jax.lax.top_k(elog, KE)
            egate = jax.nn.softmax(etop, axis=-1)
            w = ggate[:, :, None] * egate
            flat = gidx[:, :, None] * E + eidx
            comb = jnp.zeros((N, G * E), xf.dtype).at[jnp.arange(N)[:, None, None], flat].add(w)
            return comb
        shp = x.shape
        xf = x.reshape(-1, D)
        comb = _combine_weights(xf, Wg, bg, Wge, bge)
        h = jax.nn.gelu(jnp.einsum('nd,edm->nem', xf, W1) + b1, approximate=False)
        y = jnp.einsum('nem,emd->ned', h, W2) + b2
        out = jnp.einsum('ne,ned->nd', comb, y)
        return out.reshape(shp)
    edge_index = jnp.stack([src, dst])
    x = x + _L0_gnn_ref(_layernorm(x, axis=-1), src, dst, L0_gnn_W1s, L0_gnn_b1s, L0_gnn_W1d, L0_gnn_b1d, L0_gnn_attn1, L0_gnn_ln1_w, L0_gnn_ln1_b, L0_gnn_Wos, L0_gnn_bos, L0_gnn_Wod, L0_gnn_bod, L0_gnn_attno, L0_gnn_lno_w, L0_gnn_lno_b)
    x = x + _L0_ffn_ref(_layernorm(x, axis=-1)[None], L0_ffn_wq, L0_ffn_bq, L0_ffn_bn_gamma, L0_ffn_bn_beta, L0_ffn_bn_mean, L0_ffn_bn_var, L0_ffn_keys, L0_ffn_w_down_tab, L0_ffn_w_up_tab, L0_ffn_a_w1, L0_ffn_a_w2, L0_ffn_a_w3, L0_ffn_s_w1, L0_ffn_s_w2, L0_ffn_s_w3)[0]
    x = x + _L1_gnn_ref(_layernorm(x, axis=-1), edge_index, L1_gnn_W1, L1_gnn_att_src1, L1_gnn_att_dst1, L1_gnn_b1, L1_gnn_W2, L1_gnn_att_src2, L1_gnn_att_dst2, L1_gnn_b2)
    x = x + _L1_ffn_ref(_layernorm(x, axis=-1)[None], L1_ffn_Wg, L1_ffn_bg, L1_ffn_Wge, L1_ffn_bge, L1_ffn_W1, L1_ffn_b1, L1_ffn_W2, L1_ffn_b2)[0]
    return x

_drawn_inputs = setup_inputs


def setup_inputs(seed=0):
    import zlib

    import numpy as np

    out = dict(_drawn_inputs(seed))
    spreads = {'L0_gnn_b1s': (0.0, 0.1),
     'L0_gnn_b1d': (0.0, 0.8),
     'L0_gnn_ln1_w': (1.0, 0.2),
     'L0_gnn_ln1_b': (0.0, 0.1),
     'L0_gnn_bos': (0.0, 0.1),
     'L0_gnn_bod': (0.0, 0.421),
     'L0_gnn_lno_w': (1.0, 0.2),
     'L0_gnn_lno_b': (0.0, 0.1),
     'L0_ffn_bn_gamma': (1.0, 0.2),
     'L0_ffn_bn_beta': (0.0, 0.1),
     'L0_ffn_bn_mean': (0.0, 0.1),
     'L0_ffn_bn_var': (1.0, 0.2),
     'L1_gnn_b1': (0.0, 0.1),
     'L1_gnn_b2': (0.0, 0.1),
     'L1_ffn_bg': (0.0, 0.733),
     'L1_ffn_bge': (0.0, 0.533),
     'L1_ffn_b1': (0.0, 0.8),
     'L1_ffn_b2': (0.0, 0.1)}
    factors = {'L0_gnn_W1d': 2.98,
     'L1_gnn_att_dst1': 8.0,
     'L1_gnn_att_src2': 7.007,
     'L1_gnn_att_dst2': 8.0,
     'L1_ffn_W1': 2.826}
    for name, (base, spread) in spreads.items():
        noise = np.random.default_rng([zlib.crc32(name.encode()), seed]).standard_normal(out[name].shape)
        drawn = base * np.exp(spread * noise) if base else spread * noise
        out[name] = jnp.asarray(drawn.astype(out[name].dtype))
    for name, factor in factors.items():
        out[name] = (out[name] * factor).astype(out[name].dtype)
    return out
```

```python
from contextlib import ExitStack

import numpy as np
import concourse.bass as bass
from concourse import mybir

F32 = mybir.dt.float32
BF16 = mybir.dt.bfloat16
FP16 = mybir.dt.float16
U32 = mybir.dt.uint32
ALU = mybir.AluOpType
ACT = mybir.ActivationFunctionType
AX = mybir.AxisListType.X

N, E, D = 625, 10000, 768
P = 125
TT = N // P
ET = E // P
KC = D // 128
HALF = D // 2
RING = 5
EG = ET // RING
BODY = 2 * RING
LAG = 11
HEADS = 8
TROWS = 128 * 3052
FILLW = 1526
KNN, PH, NKEY = 16, 4, 800
HK = PH * KNN
HIDA = 44
HIDS = 1024
EXP, MH = 32, 96
XH = EXP * MH
XC = XH // 128
NEG = -1.0e30
EPS = 1e-5
NPS = 3


def emit(nc, a, out):
    ctx = ExitStack()
    with ctx:
        arena = ctx.enter_context(nc.sbuf_tensor("arena", [128, 52900], F32))
        DB = [ctx.enter_context(nc.psum_tensor(f"DB{i}", [128, 1024], F32)) for i in range(4)]
        ACC = DB[3]

        def sem(name):
            return ctx.enter_context(nc.semaphore(name))

        def at(off, n, p=128):
            return arena[0:p, off:off + n]

        def at3(off, x, y, p=128):
            return arena[0:p, off:off + x * y].rearrange("p (x y) -> p x y", x=x)

        XRES = at3(0, TT, D, P)
        XN = at3(3840, TT, D, P)
        XT = at3(7680, KC, N)
        CNT = at3(11520, TT, N, P)
        NODE = at3(14720, TT, D, P)
        HACC = at3(18560, TT, D, P)
        WA = at3(22400, KC, D)
        WB = at3(27008, KC, D)
        BS, BD, LNW, LNB = (at(31616 + D * i, D, P) for i in range(4))
        PT = [at3(34688 + N * i, TT, P, P) for i in range(2)]
        LGS = at3(35938, EG + 1, RING * HEADS, P)
        TB = [at(36640 + 5000 * i, 5000, P) for i in range(2)]
        U = at3(36640, RING, D, P)
        V = at3(36640 + RING * D, RING, D, P)
        ZT = [at3(44320 + 750 * i, KC, P) for i in range(2)]
        OHS = [arena[0:P, 46640 + 313 * i:46640 + 313 * (i + 1)].bitcast(BF16)[:, 0:N] for i in range(2)]
        OHD = [arena[0:P, 47266 + 313 * i:47266 + 313 * (i + 1)].bitcast(BF16)[:, 0:N] for i in range(2)]
        IOTA = arena[0:P, 34688:34688 + 313].bitcast(FP16)[:, 0:N]
        IOTF = at(18560, N, P)
        CXS = arena[0:P, 36640:36640 + 4520].bitcast(BF16).rearrange("p (t n) -> p t n", t=ET)
        CXD = arena[0:P, 41160:41160 + 5000].bitcast(BF16).rearrange("p (t n) -> p t n", t=ET)
        MN = at3(46640, 2, D, P)
        FILL = at(48176, FILLW)
        ATT = at3(49702, KC, HEADS)
        ATC = at(49750, KC)
        IDX = arena[0:P, 49760:49920].bitcast(U32).rearrange("p (a t) -> p a t", a=2)
        TIDX = arena[0:P, 49920:50000].bitcast(U32)
        IDF = at3(50000, 2, ET, P)
        TIF = at(50160, ET, P)
        ATO = at(50240, KC)
        ZERO = arena[0:P, 50250:50570].bitcast(BF16)
        WQ = at3(22400, KC, PH * 128)
        SW2 = at3(25472, 8, D)
        KEYS = at3(14720, PH, NKEY)
        SIL = [at(17920, N), at(51083, N)]
        OHB = at3(18560, HK, 32, P)
        V16, XDV, GAT, WDC, WUC = (at3(20608 + 320 * i, TT, HK, P) for i in range(5))
        GS = at3(31616, 8, N)
        SWR = at3(36616, 8, D)
        SC = [at(42760 + NKEY * i, NKEY, P) for i in range(2)]
        WK = at(44360, NKEY, P)
        OHA = at3(45160, HK, 32, P)
        OHAT = [at3(47208 + 1000 * i, 8, P) for i in range(2)]
        ZG = at3(49208, 2, N, 88)
        XDT = at(50458, N, HK)
        A1 = at(51708, 176, HK)
        A3 = at(51884, 176, HK)
        A2 = at3(52060, 2, HK, 88)
        TBL = at3(52188, 4, 64)
        QT = at3(3840, PH, N)
        SELP = at(6340, 1024, P)
        IDXK = arena[0:P, 7364:7428].bitcast(U32)
        IDA = arena[0:P, 7428:7492].bitcast(U32)
        IDB = arena[0:P, 7492:7556].bitcast(U32)
        IDKF = at3(7556, 1, HK, P)
        BNV = at3(52826, 5, PH)
        BNA = at(52846, PH)
        BNB = at(52850, PH)
        GB = [at(31616 + D * i, D, P) for i in range(6)]
        ASB = at(36224, N, P)
        EB = [at(36864 + 640 * i, N, P) for i in range(2)]
        PG = [at3(38144 + 640 * i, TT, P, P) for i in range(2)]
        DG = at3(39424, TT, P, P)
        MB = at3(40100, TT, N, P)
        JUNK = at(43300, D, P)
        HS = at3(11520, XC, N)
        W2 = at3(26520, XC, D)
        W1R = at3(44952, 4, D)
        SELE = at(48024, XH, EXP)
        B2 = at(51096, D, EXP)
        GT = [at(3840 + N * i, N) for i in range(2)]
        CT = at(5090, N, EXP)
        RT = at3(5720, TT, 36, P)
        RG = at3(5900, TT, 12, P)
        RE = at3(5960, TT * 4, 14, P)
        RGO = at3(6240, TT, 12, P)
        REO = at3(6300, TT * 4, 14, P)
        TOPG = at3(6580, TT, 8, P)
        TOPE = at3(6620, TT * 4, 8, P)
        REPG = at3(6780, TT, 8, P)
        REPE = at3(6820, TT * 4, 8, P)
        GV = at3(6980, TT, 4, P)
        EV = at3(7000, TT * 4, 8, P)
        GSM = at(7160, TT, P)
        ESM = at(7165, TT * 4, P)
        COMB = at3(7185, TT, EXP, P)
        B1C = at(7345, XC)
        BR = at(7370, 36, P)
        WR = at3(51864, KC, 36)
        IDENT = at(52444, P, P)
        IO32 = at(52570, 32, P)
        STATS = at3(52602, TT * 2, 6, P)
        MV = at3(52662, TT, 2, P)
        RSTD = at(52672, TT, P)
        MX = at3(52810, 2, HEADS, P)
        NMX = at3(52686, 2, HEADS, P)
        DEN = at3(52702, 2, HEADS, P)
        RDEN = at(52718, HEADS, P)
        SX = at(52726, TT, P)
        CMB = at(52731, TT, P)
        AS = at(52736, TT, P)
        AD = at(52741, TT, P)
        KM = at3(52746, TT, PH, P)
        KS = at3(52766, TT, PH, P)
        ONES = at(52786, 2, P)
        VARE = at(52788, TT, P)
        EXPN = at(52794, 6)
        BNR = at(52800, PH)
        MBONES = at(43225 + 843, P, P)

        FS = [nc.dram_tensor(f"src_rows{l}", (N, D), F32, kind="Internal").ap() for l in range(2)]
        FD = [nc.dram_tensor(f"dst_rows{l}", (N, D), F32, kind="Internal").ap() for l in range(2)]
        LT = [nc.dram_tensor(f"logits{l}", (TROWS, h), F32, kind="Internal").ap() for l, h in enumerate((HEADS, 1))]

        pe_done = sem("pe_done")
        copied = [sem(f"copied{i}") for i in range(NPS)]
        acc_free = sem("acc_free")
        dve_step, act_step, pool_step = sem("dve_step"), sem("act_step"), sem("pool_step")
        x_in, idx_in, const_in = sem("x_in"), sem("idx_in"), sem("const_in")
        wa_in, wb_in, bias_in, lnp_in, att_in = sem("wa_in"), sem("wb_in"), sem("bias_in"), sem("lnp_in"), sem("att_in")
        filled = sem("filled")
        consts = sem("consts")
        var_ok, rstd_ok = sem("var_ok"), sem("rstd_ok")
        bnv_ok, bnr_ok = sem("bnv_ok"), sem("bnr_ok")
        idx_ok = sem("idx_ok")
        oh_ready, oh_used = sem("oh_ready"), sem("oh_used")
        cx_ready = sem("cx_ready")
        cnt_done, cnt_ok = sem("cnt_done"), sem("cnt_ok")
        feat = sem("feat")
        rows_out = sem("rows_out")
        gath = [sem(f"gath{r}") for r in range(RING)]
        z_sum, z_ready = sem("z_sum"), sem("z_ready")
        zt_done, zt_copied = sem("zt_done"), sem("zt_copied")
        lg_done, lg_copied = sem("lg_done"), sem("lg_copied")
        scattered = sem("scattered")
        tb_in = [sem("tb_in0"), sem("tb_in1")]
        negmax, exped, p_ready, pv_done = (sem(s) for s in ("negmax", "exped", "p_ready", "pv_done"))
        min_ok, expm_ok = sem("min_ok"), sem("expm_ok")
        bn_in, ffn_in, keys_in, sw2_in, peer_in = sem("bn_in"), sem("ffn_in"), sem("keys_in"), sem("sw2_in"), sem("peer_in")
        swr_in = [sem(f"swr_in{i}") for i in range(4)]
        tbl_ok = sem("tbl_ok")
        sc_used, oha_ok = sem("sc_used"), sem("oha_ok")
        kgate, kexp = sem("kgate"), sem("kexp")
        xd_ok, bn_ok = sem("xd_ok"), sem("bn_ok")
        gw_in, gb_in = sem("gw_in"), sem("gb_in")
        diag_ok = sem("diag_ok")
        w1_in = [sem(f"w1_in{i}") for i in range(4)]
        w2_in, xb_in = sem("w2_in"), sem("xb_in")
        sele_ok, rt_ok, rexp, comb_ok = (sem(s) for s in ("sele_ok", "rt_ok", "rexp", "comb_ok"))
        y_out = sem("y_out")
        out_v = out.rearrange("(t p) d -> p t d", p=P)

        G, ngroups = {}, [0]

        def take(name, count):
            G[name] = ngroups[0]
            ngroups[0] += count

        for l in range(2):
            take(f"xT{l}", KC)
            take(f"proj{l}", 2 * TT)
            if l == 0:
                take("cx", 1)
            take(f"pt{l}", TT * (HEADS if l == 0 else 1))
        take("xT2", KC)
        take("q", PH)
        sched = []
        for t in range(TT):
            for h in range(PH):
                s = t * PH + h
                sched.append(("sc", s))
                if s < 16:
                    sched.append(("z", s))
            sched += [("oha", t, 0), ("oha", t, 1)] + [("pick", t, q) for q in range(4)]
        for item in sched:
            take(item, 1)
        take("xd", 1)
        take("peer", 4)
        take("peer_out", 1)
        take("down", TT)
        for l in range(2):
            take(f"xT{3 + l}", KC)
            take(f"h{l}", TT)
            take(f"asb{l}", 1)
            take(f"gt{l}", TT)
        take("xT5", KC)
        take("route", 1)
        take("ct", 1)
        take("exp", 2 * XC)
        take("y", TT)
        accs = {}
        n = 0
        for name in ("gat0", "gat1", "dense0", "dense1"):
            accs[name] = n
            n += TT

        def buf(g):
            return DB[g % NPS]

        def halves(b):
            return b[0:P, :].rearrange("p (a n) -> p a n", a=2)[:, :, 0:HALF]

        def split(ap):
            return ap.rearrange("p (a n) -> p a n", a=2)

        def tiles(b, p=128):
            return b[0:p, 0:640].rearrange("p (t n) -> p t n", t=TT)[:, :, 0:P]

        def nodes(ap):
            return ap.rearrange("p (t n) -> p t n", t=TT)

        def ready(eng, g):
            eng.wait_ge(pe_done, g + 1)

        def read_out(eng, g):
            eng.wait_ge(copied[g % NPS], g // NPS + 1)

        def all_read_out(eng, name, count):
            for g in range(max(0, count - NPS), count):
                read_out(eng, G[name] + g)

        def claim(pe, g):
            if g >= NPS:
                pe.wait_ge(copied[g % NPS], g // NPS)

        def claim_acc(pe, n):
            if n:
                pe.wait_ge(acc_free, n)

        LH = (HEADS, 1)
        PTB = (0, TT * HEADS)

        def cnt_main(i):
            return DB[1 + i // 2][0:P, 512 * (i % 2):512 * (i % 2) + 512] if i < 4 else DB[3][0:P, 0:512]

        def cnt_rest(i):
            return DB[3][0:P, 512 + 113 * i:512 + 113 * (i + 1)]

        block = ctx.enter_context(nc.Block())

        @block.sync
        def _(sp):
            def rows(w):
                return w.rearrange("(c p) n -> p c n", p=128)

            def bcast(v):
                return v.rearrange("(o n) -> o n", o=1).broadcast_to([P, v.shape[0]])

            for t in range(TT):
                sp.dma_start(XRES[:, t, :], a["x"][t * P:(t + 1) * P, :]).then_inc(x_in, 16)
            sp.dma_start(IDX[:, 0, :], a["src"].rearrange("(p t) -> p t", p=P)).then_inc(idx_in, 16)
            sp.dma_start(IDX[:, 1, :], a["dst"].rearrange("(p t) -> p t", p=P)).then_inc(idx_in, 16)
            sp.dma_start(WA, rows(a["W1s"])).then_inc(wa_in, 16)
            sp.dma_start(WB, rows(a["W1d"])).then_inc(wb_in, 16)
            sp.dma_start(BS, bcast(a["b1s"])).then_inc(bias_in, 16)
            sp.dma_start(BD, bcast(a["b1d"])).then_inc(bias_in, 16)
            sp.dma_start(LNW, bcast(a["ln1_w"])).then_inc(lnp_in, 16)
            sp.dma_start(LNB, bcast(a["ln1_b"])).then_inc(lnp_in, 16)
            sp.dma_start(ATC, a["attn1"]).then_inc(att_in, 16)
            sp.dma_start(ATO, a["attno"]).then_inc(att_in, 16)
            sp.wait_ge(consts, 1)
            wide = LT[0].rearrange("(p n) h -> p (n h)", p=128).rearrange("p (a n) -> p a n", a=16)
            sp.dma_start(wide, FILL.unsqueeze(1).to_broadcast([128, 16, FILLW])).then_inc(filled, 16)
            thin = LT[1].rearrange("(p n) h -> p (n h)", p=128).rearrange("p (a n) -> p a n", a=2)
            sp.dma_start(thin, FILL.unsqueeze(1).to_broadcast([128, 2, FILLW])).then_inc(filled, 16)
            for l in range(2):
                for t in range(TT):
                    read_out(sp, G[f"proj{l}"] + 2 * t)
                    read_out(sp, G[f"proj{l}"] + 2 * t + 1)
                    sp.dma_start(FS[l][t * P:(t + 1) * P, :], NODE[:, t, :]).then_inc(rows_out, 16)
                    sp.dma_start(FD[l][t * P:(t + 1) * P, :], HACC[:, t, :]).then_inc(rows_out, 16)
                if l == 0:
                    sp.dma_start(WA, rows(a["Wos"])).then_inc(wa_in, 16)
                    sp.dma_start(WB, rows(a["Wod"])).then_inc(wb_in, 16)
                    sp.dma_start(BS, bcast(a["bos"])).then_inc(bias_in, 16)
                    sp.dma_start(BD, bcast(a["bod"])).then_inc(bias_in, 16)
                else:
                    sp.dma_start(WQ, rows(a["wqT"])).then_inc(ffn_in, 16)
                    sp.dma_start(SW2, rows(a["s_w2T"])).then_inc(sw2_in, 16)
                sp.wait_ge(scattered, 16 * ET * (l + 1))
                w = N * LH[l]
                for i in range(TT):
                    n = TT * l + i
                    if i >= 2:
                        sp.wait_ge(pe_done, G[f"pt{l}"] + LH[l] * (i - 1))
                    sp.dma_start(TB[i % 2][:, 0:w], LT[l][i * P * N:(i + 1) * P * N, :]
                                 .rearrange("(p n) h -> p (n h)", p=P)).then_inc(tb_in[i % 2], 16)
                if l == 0:
                    sp.wait_ge(feat, 2 * TT)
                    sp.dma_start(LNW, bcast(a["lno_w"])).then_inc(lnp_in, 16)
                    sp.dma_start(LNB, bcast(a["lno_b"])).then_inc(lnp_in, 16)
            sp.wait_ge(feat, 3 * TT)
            sp.dma_start(KEYS, a["keysT"].rearrange("h k n -> k h n")).then_inc(keys_in, 16)
            for v, name in enumerate(("bq", "bn_gamma", "bn_beta", "bn_mean", "bn_var")):
                sp.dma_start(BNV[:, v, :], a[name]).then_inc(bn_in, 16)
            sw = [a["s_w1T"], a["s_w3T"]]
            for z in range(16):
                m, which = z // 2, z % 2
                if z >= 8:
                    sp.wait_ge(pe_done, G[("z", 2 * (m - 4) + 1)] + 1)
                sp.dma_start(SWR[:, 2 * (m % 4) + which, :].rearrange("p (c n) -> p c n", c=KC),
                             rows(sw[which])[:, :, m * 128:(m + 1) * 128]).then_inc(swr_in[m % 4], 16)
                if z == 7:
                    sp.wait_ge(tbl_ok, 1)
                    for g in range(PH):
                        for v, name in enumerate(("w_down", "w_up")):
                            sp.dma_start(TBL[32 * g:32 * g + 25, g, 32 * v:32 * v + 32],
                                         a[name].rearrange("(x y) o -> x (y o)", y=32)).then_inc(peer_in, 16)
                        sp.dma_start(A1[KNN * g:KNN * (g + 1), HIDA * g:HIDA * (g + 1)], a["a_w1T"]).then_inc(peer_in, 16)
                        sp.dma_start(A3[KNN * g:KNN * (g + 1), HIDA * g:HIDA * (g + 1)], a["a_w3T"]).then_inc(peer_in, 16)
                        sp.dma_start(A2[HIDA * (g % 2):HIDA * (g % 2 + 1), g // 2, KNN * g:KNN * (g + 1)],
                                     a["a_w2T"]).then_inc(peer_in, 16)
            sp.wait_ge(feat, 4 * TT)
            sp.dma_start(WA, rows(a["G1"])).then_inc(gw_in, 16)
            for i, name in enumerate(("as1", "ad1", "gb1", "as2", "ad2", "gb2")):
                sp.dma_start(GB[i], bcast(a[name])).then_inc(gb_in, 16)
            sp.dma_start(WB, rows(a["G2"])).then_inc(wb_in, 16)
            sp.wait_ge(feat, 6 * TT)
            for m in range(XC):
                if m == 4:
                    sp.dma_start(B2, a["b2"]).then_inc(xb_in, 16)
                    sp.dma_start(WR, a["Wr"].rearrange("p (c n) -> p c n", c=KC)).then_inc(xb_in, 16)
                    all_read_out(sp, "xT5", KC)
                    sp.dma_start(BR, bcast(a["br"])).then_inc(xb_in, 16)
                    sp.dma_start(B1C, a["b1c"]).then_inc(xb_in, 16)
                    for c in range(3):
                        sp.dma_start(W2[:, 8 * c:8 * c + 8, :], rows(a["W2"])[:, 8 * c:8 * c + 8, :]).then_inc(w2_in, 16)
                if m >= 4:
                    sp.wait_ge(pe_done, G["exp"] + 2 * (m - 4) + 1)
                sp.dma_start(W1R[:, m % 4, :].rearrange("p (c n) -> p c n", c=KC),
                             rows(a["W1c"])[:, :, m * 128:(m + 1) * 128]).then_inc(w1_in[m % 4], 16)
            for t in range(TT):
                read_out(sp, G["y"] + t)
                sp.dma_start(out_v[:, t, :], XRES[:, t, :]).then_inc(y_out, 16)
            sp.wait_ge(y_out, 16 * TT)

        @block.gpsimd
        def _(pool):
            steps = [0]

            def link(ins):
                steps[0] += 1
                ins.then_inc(pool_step, 1)
                pool.wait_ge(pool_step, steps[0])

            pool.memset(FILL, NEG).then_inc(consts, 1)
            pool.iota(IOTF, [[1, N]], base=0, channel_multiplier=0, allow_small_or_imprecise_dtypes=True).then_inc(consts, 1)
            pool.iota(IOTA, [[1, N]], base=0, channel_multiplier=0, allow_small_or_imprecise_dtypes=True).then_inc(consts, 1)
            pool.memset(ZERO, 0.0).then_inc(consts, 1)
            link(pool.memset(IDENT, 0.0))
            pool.affine_select(out=IDENT, in_=IDENT, compare_op=ALU.not_equal, fill=1.0, base=0,
                               pattern=[[-1, P]], channel_multiplier=1).then_inc(consts, 1)
            pool.iota(IO32, [[1, 32]], base=0, channel_multiplier=0, allow_small_or_imprecise_dtypes=True).then_inc(consts, 1)
            link(pool.memset(ATT, 1.0))
            link(pool.affine_select(out=ATT, in_=ATT, compare_op=ALU.is_ge, fill=0.0, base=0,
                                    pattern=[[128, KC], [-D // HEADS, HEADS]], channel_multiplier=1))
            pool.affine_select(out=ATT, in_=ATT, compare_op=ALU.is_ge, fill=0.0, base=D // HEADS - 1,
                               pattern=[[-128, KC], [D // HEADS, HEADS]], channel_multiplier=-1).then_inc(consts, 1)
            def rsqrt_var(n):
                pool.wait_ge(var_ok, n + 1)
                pool.tensor_tensor(RSTD, VARE, EXPN[0:P, 0:TT], ALU.pow).then_inc(rstd_ok, 1)

            link(pool.memset(EXPN, -0.5))
            rsqrt_var(0)
            pool.wait_ge(idx_ok, 1)
            pool.wait_ge(filled, 32)

            for l in range(2):
                pool.wait_ge(rows_out, 32 * TT * (l + 1))
                if l == 0:
                    pool.wait_ge(pe_done, G["cx"] + 1)

                def scatter(t):
                    pool.wait_ge(lg_copied, (EG + 1) * l + t // RING + 2)
                    if ET * l + t:
                        pool.wait_ge(scattered, 16 * (ET * l + t))
                    pool.indirect_dma_start(
                        out=LT[l], out_offset=bass.IndirectOffsetOnAxis(ap=TIDX[:, t:t + 1], axis=0),
                        in_=LGS[:, t // RING + 1, LH[l] * (t % RING):LH[l] * (t % RING + 1)], in_offset=None,
                    ).then_inc(scattered, 16)

                for t in range(ET):
                    r = t % RING
                    if t >= LAG:
                        scatter(t - LAG)
                    if t >= RING:
                        pool.wait_ge(zt_done, 2 * (ET * l + t - RING + 1))
                    for table, k, dst in ((FS[l], 0, U), (FD[l], 1, V)):
                        pool.indirect_dma_start(
                            out=dst[:, r, :], out_offset=None, in_=table,
                            in_offset=bass.IndirectOffsetOnAxis(ap=IDX[:, k, t:t + 1], axis=0)).then_inc(gath[r], 16)
                for t in range(ET - LAG, ET):
                    scatter(t)
                rsqrt_var(l + 1)
            rsqrt_var(3)
            pool.wait_ge(feat, 3 * TT)
            link(pool.memset(at(51708, 736), 0.0))
            pool.memset(ONES, 1.0).then_inc(tbl_ok, 1)
            pool.wait_ge(bnv_ok, 1)
            pool.tensor_tensor(BNA, BNR, EXPN[:, 0:PH], ALU.pow).then_inc(bnr_ok, 1)
            rsqrt_var(4)
            rsqrt_var(5)
            pool.wait_ge(feat, 6 * TT)
            link(pool.memset(SELE, 1.0))
            link(pool.affine_select(out=SELE, in_=SELE, compare_op=ALU.is_ge, fill=0.0, base=0,
                                    pattern=[[1, XH]], channel_multiplier=-MH))
            pool.affine_select(out=SELE, in_=SELE, compare_op=ALU.is_ge, fill=0.0, base=MH - 1,
                               pattern=[[-1, XH]], channel_multiplier=MH).then_inc(sele_ok, 1)

        @block.tensor
        def _(pe):
            mm = nc.tensor.matmul

            def turn_nodes(i, src):
                pe.wait_ge(feat, TT * (i + 1))
                for c in range(KC):
                    g = G[f"xT{i}"] + c
                    claim(pe, g)
                    for t in range(TT):
                        last = nc.tensor.transpose(buf(g)[:, 128 * t:128 * t + P], src[:, t, 128 * c:128 * (c + 1)], IDENT)
                    last.then_inc(pe_done, 1)
                all_read_out(pe, f"xT{i}", KC)

            def node_rows(g, t, w):
                claim(pe, g)
                for c in range(KC):
                    for s in range(2):
                        last = mm(buf(g)[0:P, 512 * s:512 * s + HALF], XT[:, c, t * P:(t + 1) * P],
                                  w[:, c, HALF * s:HALF * (s + 1)], start=c == 0, stop=c == KC - 1)
                last.then_inc(pe_done, 1)

            def wide_rows(g, chunks, lhs, rhs, m=128):
                claim(pe, g)
                for c in range(chunks):
                    for lo, hi, at0 in ((0, 4, 0), (4, 5, 512)):
                        o = buf(g)[0:m, at0:at0 + 128 * (hi - lo)].rearrange("p (t n) -> p t n", n=128)[:, :, 0:P]
                        last = mm(o, lhs(c), rhs(c)[:, lo * P:hi * P], start=c == 0, stop=c == chunks - 1)
                last.then_inc(pe_done, 1)

            def turn_tiles(g, src, p=P):
                claim(pe, g)
                for t in range(TT):
                    last = nc.tensor.transpose(buf(g)[0:p, 128 * t:128 * t + P], src(t), IDENT)
                last.then_inc(pe_done, 1)

            counts = [(cnt_main(i), i, 0, 512) for i in range(TT)] + [(cnt_rest(i), i, 512, N) for i in range(4)]
            banks = [DB[1][0:P, 0:512], DB[1][0:P, 512:1024], DB[2][0:P, 0:512], DB[2][0:P, 512:1024],
                     DB[3][0:P, 0:512], DB[3][0:P, 512:1024]]

            pe.wait_ge(consts, 4)
            for l in range(2):
                turn_nodes(l, XN)
                pe.wait_ge(wa_in, 16 * (l + 1))
                pe.wait_ge(wb_in, 16 * (l + 1))
                for t in range(TT):
                    node_rows(G[f"proj{l}"] + 2 * t, t, WA)
                    node_rows(G[f"proj{l}"] + 2 * t + 1, t, WB)
                if l == 0:
                    claim(pe, G["cx"])
                    pe.wait_ge(cx_ready, 1)
                    for t in range(ET):
                        last = mm(buf(G["cx"])[0:P, 0:113], CXD[:, t, :], CXS[:, t, :], start=t == 0, stop=t == ET - 1)
                    last.then_inc(pe_done, 1)
                all_read_out(pe, f"proj{l}", 2 * TT)
                if l == 0:
                    read_out(pe, G["cx"])
                    for b in banks:
                        mm(b, ZERO[:, 0:P], ZERO[:, 0:512], start=True, stop=False)
                nh = LH[l]
                zps = DB[0][:, 0:384].rearrange("p (c n) -> p c n", c=3)
                mm(DB[0][0:P, 512:512 + RING * nh], IDENT, XN[:, 0, 0:RING * nh], start=True, stop=True).then_inc(lg_done, RING)
                with pe.Fori(0, ET // BODY) as g:
                    def count(r, some):
                        for o, i, lo, hi in some:
                            last = mm(o, OHD[r % 2][:, i * P:(i + 1) * P], OHS[r % 2][:, lo:hi], start=False, stop=False)
                        return last

                    def turn(r, half):
                        pe.wait_ge(zt_copied, 2 * ET * l + 2 * BODY * g + 2 * r + half + 2)
                        for c in range(3):
                            f = 128 * (3 * half + c)
                            last = nc.tensor.transpose(zps[:, c, 0:P], U[:, r % RING, f:f + 128], IDENT)
                        last.then_inc(zt_done, 1)

                    def logits(r):
                        pe.wait_ge(zt_copied, 2 * ET * l + 2 * BODY * g + 2 * r + 4)
                        if r % RING == 0:
                            pe.wait_ge(lg_copied, (EG + 1) * l + 2 * g + r // RING + 1)
                        for c in range(KC):
                            rhs = ATT[:, c, :] if l == 0 else ATO[:, c:c + 1]
                            o = 512 + nh * (r % RING)
                            last = mm(DB[0][0:P, o:o + nh], ZT[r % 2][:, c, :], rhs, start=c == 0, stop=c == KC - 1)
                        last.then_inc(lg_done, 1)

                    for r in range(BODY):
                        pe.wait_ge(z_ready, ET * l + BODY * g + r + 1)
                        turn(r, 0)
                        if l == 0:
                            pe.wait_ge(oh_ready, BODY * g + r + 1)
                            count(r, counts[:3])
                        if r:
                            logits(r - 1)
                        turn(r, 1)
                        if l == 0:
                            count(r, counts[3:]).then_inc(oh_used, 1)
                    logits(BODY - 1)
                if l == 0:
                    for b in banks:
                        last = mm(b, ZERO[:, 0:P], ZERO[:, 0:512], start=False, stop=True)
                    last.then_inc(cnt_done, 1)
                    pe.wait_ge(cnt_ok, 1)
                pe.wait_ge(lg_copied, (EG + 1) * (l + 1))

                H, HD = LH[l], D // LH[l]
                heads = [(i, h) for i in range(TT) for h in range(H)]

                def turn_head(k):
                    i, h = heads[k]
                    pe.wait_ge(p_ready, PTB[l] + k + 1)
                    view = TB[i % 2][:, 0:N * H].rearrange("p (n h) -> p h n", h=H)[:, h, :]
                    turn_tiles(G[f"pt{l}"] + k, lambda t: view[:, t * P:(t + 1) * P])

                turn_head(0)
                for k, (i, h) in enumerate(heads):
                    if k + 1 < len(heads):
                        turn_head(k + 1)
                    read_out(pe, G[f"pt{l}"] + k)
                    if h == 0:
                        claim_acc(pe, accs[f"gat{l}"] + i)
                    pieces = [(512 * (h // 4) + HD * (h % 4), h * HD, HD)] if H > 1 else [(0, 0, HALF), (512, HALF, HALF)]
                    for o, f, w in pieces:
                        for j in range(TT):
                            last = mm(ACC[0:P, o:o + w], PT[k % 2][:, j, :], NODE[:, j, f:f + w], start=j == 0, stop=j == TT - 1)
                    last.then_inc(pv_done, 1)

            turn_nodes(2, XN)
            pe.wait_ge(ffn_in, 16)
            for h in range(PH):
                wide_rows(G["q"] + h, KC, lambda c: WQ[:, c, h * 128:(h + 1) * 128], lambda c: XT[:, c, :])
            all_read_out(pe, "q", PH)
            pe.wait_ge(keys_in, 16)
            for item in sched:
                g = G[item]
                if item[0] == "sc":
                    t, h = divmod(item[1], PH)
                    claim(pe, g)
                    for s in range(2):
                        last = mm(buf(g)[0:P, 512 * s:512 * s + 400], QT[:, h, t * P:(t + 1) * P],
                                  KEYS[:, h, 400 * s:400 * (s + 1)], start=True, stop=True)
                    last.then_inc(pe_done, 1)
                elif item[0] == "z":
                    m, which = divmod(item[1], 2)
                    pe.wait_ge(swr_in[m % 4], 32 * (m // 4 + 1))
                    w = SWR[:, 2 * (m % 4) + which, :].rearrange("p (c n) -> p c n", c=KC)
                    wide_rows(g, KC, lambda c: w[:, c, :], lambda c: XT[:, c, :])
                elif item[0] == "oha":
                    _, t, half = item
                    pe.wait_ge(oha_ok, t + 1)
                    claim(pe, g)
                    for j in range(8):
                        k = 8 * half + j
                        last = nc.tensor.transpose(buf(g)[:, 128 * j:128 * j + P],
                                                   OHA[:, 4 * k:4 * k + 4, :].rearrange("p a b -> p (a b)"), IDENT)
                    last.then_inc(pe_done, 1)
                else:
                    _, t, q = item
                    read_out(pe, G[("oha", t, q // 2)])
                    pe.wait_ge(peer_in, 16 * 20)
                    claim(pe, g)
                    for j in range(4):
                        k = 4 * q + j
                        last = mm(buf(g)[0:P, 256 * j:256 * (j + 1)], OHAT[k // 8][:, k % 8, :],
                                  TBL.rearrange("p a b -> p (a b)"), start=True, stop=True)
                    last.then_inc(pe_done, 1)
            g = G["xd"]
            pe.wait_ge(xd_ok, 1)
            turn_tiles(g, lambda t: XDV[:, t, :], HK)
            read_out(pe, G["xd"])
            for pair in range(2):
                for which, w in enumerate((A1, A3)):
                    wide_rows(G["peer"] + 2 * pair + which, 1, lambda c: w[:, 88 * pair:88 * (pair + 1)], lambda c: XDT, 88)
            g = G["peer_out"]
            claim(pe, g)
            for pair in range(2):
                read_out(pe, G["peer"] + 2 * pair + 1)
            for t in range(TT):
                for pair in range(2):
                    last = mm(buf(g)[0:P, HK * t:HK * (t + 1)], ZG[:, pair, t * P:(t + 1) * P], A2[:, pair, :],
                              start=pair == 0, stop=pair == 1)
            last.then_inc(pe_done, 1)
            for m in range(8):
                read_out(pe, G[("z", 2 * m + 1)])
            pe.wait_ge(sw2_in, 16)
            for t in range(TT):
                g = G["down"] + t
                claim(pe, g)
                for m in range(8):
                    for s in range(2):
                        last = mm(buf(g)[0:P, 512 * s:512 * s + HALF], GS[:, m, t * P:(t + 1) * P],
                                  SW2[:, m, HALF * s:HALF * (s + 1)], start=m == 0, stop=m == 7)
                last.then_inc(pe_done, 1)

            for l in range(2):
                turn_nodes(3 + l, XN)
                pe.wait_ge(gw_in, 16)
                pe.wait_ge(wb_in, 48)
                for t in range(TT):
                    node_rows(G[f"h{l}"] + t, t, (WA, WB)[l])
                g = G[f"asb{l}"]
                pe.wait_ge(diag_ok, l + 1)
                claim(pe, g)
                for t in range(TT):
                    last = mm(buf(g)[0:P, 128 * t:128 * t + P], MBONES, DG[:, t, :], start=True, stop=True)
                last.then_inc(pe_done, 1)

                def turn_weights(i):
                    pe.wait_ge(p_ready, PTB[1] + TT + TT * l + i + 1)
                    turn_tiles(G[f"gt{l}"] + i, lambda t: EB[i % 2][:, t * P:(t + 1) * P])

                for i in range(TT):
                    turn_weights(i)
                    read_out(pe, G[f"gt{l}"] + i)
                    claim_acc(pe, accs[f"dense{l}"] + i)
                    for s in range(2):
                        for j in range(TT):
                            last = mm(ACC[0:P, 512 * s:512 * s + HALF], PG[i % 2][:, j, :],
                                      NODE[:, j, HALF * s:HALF * (s + 1)], start=j == 0, stop=j == TT - 1)
                    last.then_inc(pv_done, 1)

            turn_nodes(5, XN)
            g = G["route"]
            pe.wait_ge(xb_in, 64)
            claim(pe, g)
            for t in range(TT):
                for c in range(KC):
                    last = mm(buf(g)[0:P, 64 * t:64 * t + 36], XT[:, c, t * P:(t + 1) * P], WR[:, c, :], start=c == 0, stop=c == KC - 1)
            last.then_inc(pe_done, 1)
            pe.wait_ge(comb_ok, 1)
            turn_tiles(G["ct"], lambda t: COMB[:, t, :], EXP)
            pe.wait_ge(sele_ok, 1)
            read_out(pe, G["ct"])
            for m in range(XC):
                pe.wait_ge(w1_in[m % 4], 16 * (m // 4 + 1))
                w = W1R[:, m % 4, :].rearrange("p (c n) -> p c n", c=KC)
                wide_rows(G["exp"] + 2 * m, KC, lambda c: w[:, c, :], lambda c: XT[:, c, :])
                wide_rows(G["exp"] + 2 * m + 1, 1, lambda c: SELE[:, 128 * m:128 * (m + 1)], lambda c: CT)
            all_read_out(pe, "exp", 2 * XC)
            pe.wait_ge(w2_in, 48)
            for t in range(TT):
                g = G["y"] + t
                claim(pe, g)
                for m in range(XC + 1):
                    for s in range(2):
                        o = buf(g)[0:P, 512 * s:512 * s + HALF]
                        if m < XC:
                            mm(o, HS[:, m, t * P:(t + 1) * P], W2[:, m, HALF * s:HALF * (s + 1)], start=m == 0, stop=False)
                        else:
                            last = mm(o, CT[:, t * P:(t + 1) * P], B2[:, HALF * s:HALF * (s + 1)], start=False, stop=True)
                last.then_inc(pe_done, 1)

        @block.scalar
        def _(act):
            steps = [0]

            def evac(g, dst, src):
                ready(act, g)
                act.activation(dst, src, ACT.Copy).then_inc(copied[g % NPS], 1)

            def evac_nodes(i):
                for c in range(KC):
                    g = G[f"xT{i}"] + c
                    evac(g, nodes(XT[:, c, :]), tiles(buf(g)))

            for l in range(2):
                evac_nodes(l)
                act.activation(NMX[:, 0, 0:1], IDENT[:, 0:1], ACT.Copy).then_inc(zt_copied, 2) if l == 0 else None
                with act.Fori(0, ET // BODY) as g:
                    for r in range(BODY):
                        act.wait_ge(lg_done, (ET + RING) * l + BODY * g + r + RING - 1)
                        for half in range(2):
                            act.wait_ge(zt_done, 2 * ET * l + 2 * BODY * g + 2 * r + half + 1)
                            act.activation(ZT[r % 2][:, 3 * half:3 * half + 3, :],
                                           DB[0][:, 0:384].rearrange("p (c n) -> p c n", c=3)[:, :, 0:P],
                                           ACT.Copy).then_inc(zt_copied, 1)
                H = LH[l]

                def evac_head(k):
                    g = G[f"pt{l}"] + k
                    if PTB[l] + k >= 2:
                        act.wait_ge(pv_done, PTB[l] + k - 1)
                    evac(g, PT[k % 2], tiles(buf(g), P))

                def expm(i):
                    act.wait_ge(min_ok, TT * l + i + 1)
                    act.activation(MN[:, i % 2, :], MN[:, i % 2, :], ACT.Exp).then_inc(expm_ok, 1)

                for i in range(TT):
                    act.wait_ge(negmax, TT * l + i + 1)
                    for h in range(H):
                        view = TB[i % 2][:, 0:N * H].rearrange("p (n h) -> p h n", h=H)[:, h, :]
                        act.activation(view, view, ACT.Exp, bias=NMX[:, i % 2, h:h + 1]).then_inc(exped, 1)
                        if h >= 2:
                            evac_head(H * i + h - 2)
                    for h in range(max(0, H - 2), H):
                        evac_head(H * i + h)
                    if i >= 1:
                        expm(i - 1)
                expm(TT - 1)

            evac_nodes(2)
            act.wait_ge(bn_ok, 1)
            for h in range(PH):
                g = G["q"] + h
                ready(act, g)
                act.activation(nodes(QT[:, h, :]), tiles(buf(g)), ACT.Identity, bias=BNB[:, h:h + 1],
                               scale=BNA[:, h:h + 1]).then_inc(copied[g % NPS], 1)
            for item in sched:
                g = G[item]
                if item[0] == "sc":
                    if item[1] >= 2:
                        act.wait_ge(sc_used, item[1] - 1)
                    evac(g, SC[item[1] % 2].rearrange("p (a n) -> p a n", a=2),
                         buf(g)[0:P, :].rearrange("p (a n) -> p a n", a=2)[:, :, 0:400])
                elif item[0] == "z" and item[1] % 2 == 0:
                    m = item[1] // 2
                    if m >= 2:
                        read_out(act, G[("z", 2 * (m - 2) + 1)])
                    ready(act, g)
                    act.activation(nodes(SIL[m % 2]), tiles(buf(g)), ACT.Silu).then_inc(copied[g % NPS], 1)
                elif item[0] == "oha":
                    _, t, half = item
                    if t:
                        act.wait_ge(pe_done, G[("pick", t - 1, 2 * half + 1)] + 1)
                    evac(g, OHAT[half], buf(g)[:, :].rearrange("p (j n) -> p j n", j=8)[:, :, 0:P])
            evac(G["xd"], nodes(XDT), tiles(buf(G["xd"]), HK))
            for pair in range(2):
                g = G["peer"] + 2 * pair
                ready(act, g)
                read_out(act, G[("z", 13 + 2 * pair)])
                act.activation(nodes(SIL[pair][0:88, :]), tiles(buf(g), 88), ACT.Silu).then_inc(copied[g % NPS], 1)
            act.wait_ge(kgate, 1)
            act.activation(GAT, GAT, ACT.Exp).then_inc(kexp, 1)

            for l in range(2):
                evac_nodes(3 + l)
                for t in range(TT):
                    g = G[f"h{l}"] + t
                    evac(g, split(NODE[:, t, :]), halves(buf(g)))
                g = G[f"asb{l}"]
                evac(g, nodes(ASB), tiles(buf(g), P))
                for i in range(TT):
                    n = TT * (2 + l) + i
                    act.wait_ge(negmax, n + 1)
                    act.activation(EB[i % 2], EB[i % 2], ACT.Exp, bias=NMX[:, i % 2, 0:1]).then_inc(exped, 1)
                    if i >= 2:
                        act.wait_ge(pv_done, PTB[1] + TT + TT * l + i - 1)
                    g = G[f"gt{l}"] + i
                    evac(g, PG[i % 2], tiles(buf(g), P))

            evac_nodes(5)
            act.wait_ge(rt_ok, 1)
            act.activation(GV, GV, ACT.Exp).then_inc(rexp, 1)
            act.activation(EV, EV, ACT.Exp).then_inc(rexp, 1)
            evac(G["ct"], nodes(CT), tiles(buf(G["ct"]), EXP))
            for m in range(XC):
                g = G["exp"] + 2 * m
                if m >= 2:
                    read_out(act, g - 3)
                ready(act, g)
                act.activation(nodes(GT[m % 2]), tiles(buf(g)), ACT.Gelu, bias=B1C[:, m:m + 1]).then_inc(copied[g % NPS], 1)

        @block.vector
        def _(dve):
            steps = [0]

            def link(ins):
                steps[0] += 1
                ins.then_inc(dve_step, 1)
                dve.wait_ge(dve_step, steps[0])

            norms = [0]

            def norm(src, dst, *sems):
                for t in range(TT):
                    for s in range(2):
                        last = dve.bn_stats(STATS[:, 2 * t + s, :], src[:, t, HALF * s:HALF * (s + 1)])
                link(last)
                for t in range(TT):
                    last = dve.bn_aggr(MV[:, t, :], STATS[:, 2 * t:2 * t + 2, :])
                link(last)
                dve.tensor_scalar(VARE, MV[:, :, 1], EPS, None, ALU.add).then_inc(var_ok, 1)
                norms[0] += 1
                dve.wait_ge(rstd_ok, norms[0])
                for t in range(TT):
                    ins = dve.tensor_scalar(dst[:, t, :], src[:, t, :], MV[:, t, 0:1], RSTD[:, t:t + 1], ALU.subtract, ALU.mult)
                    for s in sems:
                        ins = ins.then_inc(s, 1)
                return ins

            dve.wait_ge(x_in, 16 * TT)
            norm(XRES, XN, feat)
            dve.wait_ge(idx_in, 32)
            link(dve.tensor_copy(IDF, IDX))
            link(dve.scalar_tensor_tensor(out=TIF, in0=IDF[:, 1, :], scalar=float(N), in1=IDF[:, 0, :], op0=ALU.mult, op1=ALU.add))
            dve.tensor_copy(TIDX, TIF).then_inc(idx_ok, 1)
            dve.wait_ge(consts, 7)
            dve.tensor_tensor(CXS, IDF[:, 0, :].unsqueeze(2).to_broadcast([P, ET, 113]),
                              IOTF[:, 512:N].unsqueeze(1).to_broadcast([P, ET, 113]), ALU.is_equal)
            dve.tensor_tensor(CXD, IDF[:, 1, :].unsqueeze(2).to_broadcast([P, ET, P]),
                              IOTF[:, 4 * P:N].unsqueeze(1).to_broadcast([P, ET, P]), ALU.is_equal).then_inc(cx_ready, 1)
            dve.wait_ge(cx_ready, 1)
            dve.wait_ge(att_in, 32)
            for c in range(KC):
                last = dve.tensor_scalar(ATT[:, c, :], ATT[:, c, :], ATC[:, c:c + 1], None, ALU.mult)
            link(last)
            IDG = IDF.rearrange("p a (g s) -> p a g s", s=BODY)

            for l in range(2):
                dve.wait_ge(bias_in, 32 * (l + 1))
                for t in range(TT):
                    for k, (dst, b) in enumerate(((NODE, BS), (HACC, BD))):
                        g = G[f"proj{l}"] + 2 * t + k
                        ready(dve, g)
                        dve.tensor_tensor(split(dst[:, t, :]), halves(buf(g)), split(b), ALU.add)\
                           .then_inc(copied[g % NPS], 1)
                if l == 0:
                    ready(dve, G["cx"])
                    dve.tensor_copy(CNT[:, 4, 512:N], buf(G["cx"])[0:P, 0:113]).then_inc(copied[G["cx"] % NPS], 1)
                nh = LH[l]

                def copy_logits(row):
                    return dve.tensor_scalar(row.rearrange("p a n -> p (a n)"), DB[0][0:P, 512:512 + RING * nh],
                                             1.0, None, ALU.mult).then_inc(lg_copied, 1)

                if l == 0:
                    dve.memset(OHS[0], 0.0).then_inc(oh_used, 2)
                    dve.wait_ge(oh_used, 2)
                with dve.Fori(0, ET // BODY) as g:
                    for r in range(BODY):
                        if l == 0:
                            dve.wait_ge(oh_used, BODY * g + r + 1)
                            for oh, k in ((OHS, 0), (OHD, 1)):
                                last = dve.tensor_scalar(oh[r % 2], IOTA, IDG[:, k, bass.ds(g, 1), r], None, ALU.is_equal)
                            last.then_inc(oh_ready, 1)
                        s = r % RING
                        dve.wait_ge(gath[s], 32 * EG * l + 64 * g + 32 * (r // RING) + 32)
                        dve.tensor_tensor(U[:, s, :], U[:, s, :], V[:, s, :], ALU.add).then_inc(z_sum, 1)
                        dve.wait_ge(z_sum, ET * l + BODY * g + r + 1)
                        dve.scalar_tensor_tensor(out=U[:, s, :], in0=U[:, s, :], scalar=0.2, in1=U[:, s, :],
                                                 op0=ALU.mult, op1=ALU.max).then_inc(z_ready, 1)
                        if s == 1:
                            dve.wait_ge(lg_done, (ET + RING) * l + BODY * g + r - 1 + RING)
                            copy_logits(LGS[:, bass.ds(2 * g + r // RING, 1), 0:RING * nh])
                dve.wait_ge(lg_done, (ET + RING) * (l + 1))
                copy_logits(LGS[:, EG:EG + 1, 0:RING * nh])
                if l == 0:
                    dve.wait_ge(cnt_done, 1)
                    for i in range(TT):
                        if i < 4:
                            dve.tensor_copy(CNT[:, i, 512:N], cnt_rest(i))
                        last = dve.tensor_copy(CNT[:, i, 0:512], cnt_main(i))
                    last.then_inc(cnt_ok, 1)

                H, HD = LH[l], D // LH[l]

                def elu(i):
                    dve.wait_ge(expm_ok, TT * l + i + 1)
                    if l == 0:
                        link(dve.scalar_tensor_tensor(out=MN[:, i % 2, :], in0=MN[:, i % 2, :], scalar=-1.0,
                                                      in1=XN[:, i, :], op0=ALU.add, op1=ALU.add))
                    else:
                        link(dve.tensor_scalar(MN[:, i % 2, :], MN[:, i % 2, :], -1.0, None, ALU.add))
                    link(dve.scalar_tensor_tensor(out=HACC[:, i, :], in0=HACC[:, i, :], scalar=0.0, in1=MN[:, i % 2, :],
                                                  op0=ALU.max, op1=ALU.add))

                def weigh(i, lo, hi):
                    for h in range(lo, hi):
                        dve.wait_ge(exped, PTB[l] + H * i + h + 1)
                        view = TB[i % 2][:, 0:N * H].rearrange("p (n h) -> p h n", h=H)[:, h, :]
                        dve.tensor_tensor_reduce(view, view, CNT[:, i, :], 1.0, 0.0, ALU.mult, ALU.add,
                                                 DEN[:, i % 2, h:h + 1]).then_inc(p_ready, 1)

                def peak(i):
                    dve.wait_ge(tb_in[i % 2], 16 * (3 * l + i // 2 + 1) if i % 2 == 0 else 16 * (2 * l + i // 2 + 1))
                    if H > 1:
                        link(dve.tensor_reduce(MX[:, i % 2, 0:H], TB[i % 2][:, 0:N * H].rearrange("p (n h) -> p h n", h=H), AX, ALU.max))
                    else:
                        link(dve.tensor_reduce(MX[:, i % 2, 0:1], TB[i % 2][:, 0:N], AX, ALU.max))
                    dve.tensor_scalar(NMX[:, i % 2, 0:H], MX[:, i % 2, 0:H], -1.0, None, ALU.mult).then_inc(negmax, 1)

                def out_rows(i):
                    dve.wait_ge(p_ready, PTB[l] + H * (i + 1))
                    link(dve.tensor_scalar(RDEN[:, 0:H], DEN[:, i % 2, 0:H], 1.0, None, ALU.max))
                    link(dve.reciprocal(RDEN[:, 0:H], RDEN[:, 0:H]))
                    dve.wait_ge(pv_done, PTB[l] + H * (i + 1))
                    if H > 1:
                        for s in range(2):
                            o = HACC[:, i, HALF * s:HALF * (s + 1)].rearrange("p (h d) -> p h d", h=4)
                            src = ACC[0:P, 512 * s:512 * s + HALF].rearrange("p (h d) -> p h d", h=4)
                            last = dve.tensor_tensor(o, src, RDEN[:, 4 * s:4 * s + 4].unsqueeze(2).to_broadcast([P, 4, HD]), ALU.mult)
                        last.then_inc(acc_free, 1)
                    else:
                        dve.tensor_scalar(split(HACC[:, i, :]), halves(ACC), RDEN[:, 0:1], None, ALU.mult).then_inc(acc_free, 1)
                    dve.wait_ge(acc_free, accs[f"gat{l}"] + i + 1)
                    dve.tensor_scalar(MN[:, i % 2, :], HACC[:, i, :], 0.0, None, ALU.min).then_inc(min_ok, 1)

                dve.wait_ge(rows_out, 32 * TT * (l + 1))
                peak(0)
                for i in range(TT):
                    if i + 1 < TT:
                        peak(i + 1)
                    weigh(i, 0, min(2, H))
                    if i >= 2:
                        elu(i - 2)
                    if i >= 1:
                        out_rows(i - 1)
                    weigh(i, min(2, H), H)
                elu(TT - 2)
                out_rows(TT - 1)
                elu(TT - 1)
                dve.wait_ge(lnp_in, 32 * (l + 1))
                link(norm(HACC, HACC))
                for t in range(TT):
                    last = dve.tensor_tensor(HACC[:, t, :], HACC[:, t, :], LNW, ALU.mult)
                link(last)
                for t in range(TT):
                    if l == 0:
                        dve.tensor_tensor(XN[:, t, :], HACC[:, t, :], LNB, ALU.add).then_inc(feat, 1)
                    else:
                        last = dve.tensor_tensor(HACC[:, t, :], HACC[:, t, :], LNB, ALU.add)
            link(last)
            for t in range(TT):
                last = dve.tensor_tensor(XRES[:, t, :], XRES[:, t, :], HACC[:, t, :], ALU.add)
            link(last)
            norm(XRES, XN, feat)
            dve.wait_ge(feat, 3 * TT)
            link(dve.tensor_reduce(SX, XN, AX, ALU.add))
            dve.wait_ge(bn_in, 16 * 5)
            dve.tensor_scalar(BNR, BNV[:, 4, :], EPS, None, ALU.add).then_inc(bnv_ok, 1)
            dve.wait_ge(bnr_ok, 1)
            link(dve.tensor_tensor(BNA, BNA, BNV[:, 1, :], ALU.mult))
            link(dve.tensor_tensor(BNB, BNV[:, 0, :], BNV[:, 3, :], ALU.subtract))
            link(dve.tensor_tensor(BNB, BNB, BNA, ALU.mult))
            dve.tensor_tensor(BNB, BNB, BNV[:, 2, :], ALU.add).then_inc(bn_ok, 1)

            def pick(g, t, q):
                ready(dve, g)
                prod = SELP.rearrange("p (k v b) -> p k v b", k=16, v=2)
                dve.tensor_tensor(prod, buf(g)[0:P, :].rearrange("p (k v b) -> p k v b", k=16, v=2),
                                       OHB[:, 16 * q:16 * q + 16, :].unsqueeze(2).to_broadcast([P, 16, 2, 32]), ALU.mult)\
                   .then_inc(copied[g % NPS], 1)
                read_out(dve, g)
                dve.tensor_reduce(WDC[:, t, 16 * q:16 * q + 16], prod[:, :, 0, :], AX, ALU.add)
                link(dve.tensor_reduce(WUC[:, t, 16 * q:16 * q + 16], prod[:, :, 1, :], AX, ALU.add))

            for item in sched:
                g = G[item]
                if item[0] == "sc":
                    t, h = divmod(item[1], PH)
                    s = SC[item[1] % 2]
                    read_out(dve, g)
                    v = V16[:, t, KNN * h:KNN * (h + 1)]
                    k = IDXK[:, KNN * h:KNN * (h + 1)]
                    link(dve.max(v[:, 0:8], s))
                    dve.max_index(k[:, 0:8], v[:, 0:8], s)
                    link(dve.match_replace(WK, v[:, 0:8], s, -3.0e38))
                    link(dve.max(v[:, 8:16], WK))
                    dve.max_index(k[:, 8:16], v[:, 8:16], WK).then_inc(sc_used, 1)
                    dve.wait_ge(sc_used, item[1] + 1)
                    if h == PH - 1:
                        dve.tensor_scalar(IDA, IDXK, 5, None, ALU.logical_shift_right)
                        link(dve.tensor_scalar(IDB, IDXK, 31, None, ALU.bitwise_and))
                        iota = IO32.unsqueeze(1).to_broadcast([P, HK, 32])
                        link(dve.tensor_copy(IDKF[:, 0, :], IDA))
                        if t:
                            ready(dve, G[("oha", t - 1, 1)])
                        dve.tensor_tensor(OHA, IDKF[:, 0, :].unsqueeze(2).to_broadcast([P, HK, 32]), iota, ALU.is_equal)\
                           .then_inc(oha_ok, 1)
                        dve.wait_ge(oha_ok, t + 1)
                        link(dve.tensor_copy(IDKF[:, 0, :], IDB))
                        link(dve.tensor_tensor(OHB, IDKF[:, 0, :].unsqueeze(2).to_broadcast([P, HK, 32]), iota, ALU.is_equal))
                elif item[0] == "z" and item[1] % 2 == 1:
                    m = item[1] // 2
                    ready(dve, g)
                    read_out(dve, G[("z", item[1] - 1)])
                    dve.tensor_tensor(nodes(GS[:, m, :]), nodes(SIL[m % 2]), tiles(buf(g)), ALU.mult)\
                       .then_inc(copied[g % NPS], 1)
                elif item[0] == "pick":
                    pick(g, item[1], item[2])
            for t in range(TT):
                last = dve.tensor_scalar(XDV[:, t, :], WDC[:, t, :], SX[:, t:t + 1], None, ALU.mult)
            last.then_inc(xd_ok, 1)
            v4 = V16.rearrange("p t (h k) -> p (t h) k", h=PH)
            g4 = GAT.rearrange("p t (h k) -> p (t h) k", h=PH)
            km, ks = KM.rearrange("p t h -> p (t h)"), KS.rearrange("p t h -> p (t h)")
            link(dve.tensor_reduce(km, v4, AX, ALU.max))
            dve.tensor_tensor(g4, v4, km.unsqueeze(2).to_broadcast([P, TT * PH, KNN]), ALU.subtract).then_inc(kgate, 1)
            for pair in range(2):
                g = G["peer"] + 2 * pair + 1
                ready(dve, g)
                read_out(dve, g - 1)
                dve.tensor_tensor(nodes(ZG[:, pair, :]), nodes(SIL[pair][0:88, :]), tiles(buf(g), 88), ALU.mult)\
                   .then_inc(copied[g % NPS], 1)
            dve.wait_ge(kexp, 1)
            link(dve.tensor_reduce(ks, g4, AX, ALU.add))
            link(dve.reciprocal(ks, ks))
            link(dve.tensor_tensor(g4, g4, ks.unsqueeze(2).to_broadcast([P, TT * PH, KNN]), ALU.mult))
            link(dve.tensor_tensor(GAT, GAT, WUC, ALU.mult))
            g = G["peer_out"]
            ready(dve, g)
            dve.tensor_tensor(GAT, GAT, buf(g)[0:P, 0:TT * HK].rearrange("p (t k) -> p t k", t=TT), ALU.mult)\
               .then_inc(copied[g % NPS], 1)
            read_out(dve, g)
            link(dve.tensor_reduce(CMB, GAT, AX, ALU.add))
            for t in range(TT):
                g = G["down"] + t
                ready(dve, g)
                last = dve.scalar_tensor_tensor(out=split(XRES[:, t, :]), in0=halves(buf(g)), scalar=CMB[:, t:t + 1],
                                                in1=split(XRES[:, t, :]), op0=ALU.add, op1=ALU.add)
                last.then_inc(copied[g % NPS], 1)
            all_read_out(dve, "down", TT)
            norm(XRES, XN, feat)
            for t in range(TT):
                last = dve.tensor_tensor(CNT[:, t, t * P:(t + 1) * P], CNT[:, t, t * P:(t + 1) * P], IDENT, ALU.add)
            link(last)
            dve.tensor_scalar(MB, CNT, 0.0, NEG, ALU.is_equal, ALU.mult)
            link(dve.memset(MBONES, 1.0))
            for l in range(2):
                dve.wait_ge(gb_in, 96)
                att_s, att_d, bias = GB[3 * l:3 * l + 3]
                for t in range(TT):
                    read_out(dve, G[f"h{l}"] + t)
                    link(dve.tensor_tensor_reduce(JUNK, NODE[:, t, :], att_s, 1.0, 0.0, ALU.mult, ALU.add, AS[:, t:t + 1]))
                    link(dve.tensor_tensor_reduce(JUNK, NODE[:, t, :], att_d, 1.0, 0.0, ALU.mult, ALU.add, AD[:, t:t + 1]))
                for t in range(TT):
                    last = dve.tensor_scalar(DG[:, t, :], IDENT, AS[:, t:t + 1], None, ALU.mult)
                last.then_inc(diag_ok, 1)
                read_out(dve, G[f"asb{l}"])

                def edge_logits(i):
                    e = EB[i % 2]
                    if i >= 2:
                        ready(dve, G[f"gt{l}"] + i - 2)
                    link(dve.tensor_scalar(e, ASB, AD[:, i:i + 1], None, ALU.add))
                    link(dve.scalar_tensor_tensor(out=e, in0=e, scalar=0.2, in1=e, op0=ALU.mult, op1=ALU.max))
                    link(dve.tensor_tensor(e, e, MB[:, i, :], ALU.add))
                    link(dve.tensor_reduce(MX[:, i % 2, 0:1], e, AX, ALU.max))
                    dve.tensor_scalar(NMX[:, i % 2, 0:1], MX[:, i % 2, 0:1], -1.0, None, ALU.mult).then_inc(negmax, 1)

                def edge_weights(i):
                    e = EB[i % 2]
                    dve.wait_ge(exped, PTB[1] + TT + TT * l + i + 1)
                    dve.tensor_tensor_reduce(e, e, CNT[:, i, :], 1.0, 0.0, ALU.mult, ALU.add, DEN[:, i % 2, 0:1]).then_inc(p_ready, 1)

                def node_out(i):
                    dve.wait_ge(p_ready, PTB[1] + TT + TT * l + i + 1)
                    link(dve.reciprocal(RDEN[:, 0:1], DEN[:, i % 2, 0:1]))
                    n = accs[f"dense{l}"] + i
                    dve.wait_ge(pv_done, PTB[1] + TT + TT * l + i + 1)
                    dve.scalar_tensor_tensor(out=split(HACC[:, i, :]), in0=halves(ACC), scalar=RDEN[:, 0:1], in1=split(bias),
                                             op0=ALU.mult, op1=ALU.add).then_inc(acc_free, 1)
                    dve.wait_ge(acc_free, n + 1)
                    if l == 0:
                        dve.tensor_scalar(XN[:, i, :], HACC[:, i, :], 0.0, None, ALU.max).then_inc(feat, 1)
                    else:
                        link(dve.tensor_tensor(XRES[:, i, :], XRES[:, i, :], HACC[:, i, :], ALU.add))

                edge_logits(0)
                for i in range(TT):
                    if i + 1 < TT:
                        edge_logits(i + 1)
                    edge_weights(i)
                    if i:
                        node_out(i - 1)
                node_out(TT - 1)
            norm(XRES, XN, feat)
            g = G["route"]
            ready(dve, g)
            dve.tensor_tensor(RT, buf(g)[0:P, 0:64 * TT].rearrange("p (t n) -> p t n", t=TT)[:, :, 0:36],
                                   BR.unsqueeze(1).to_broadcast([P, TT, 36]), ALU.add).then_inc(copied[g % NPS], 1)
            read_out(dve, g)
            dve.memset(RG, NEG)
            dve.memset(RE, NEG)
            dve.memset(REPG, NEG)
            link(dve.memset(REPE, NEG))
            glog = RT[:, :, 0:4]
            elog = RT[:, :, 4:36].rearrange("p t (g e) -> p t g e", g=4)
            dve.tensor_copy(RG[:, :, 0:4], glog)
            for t in range(TT):
                last = dve.tensor_copy(RE[:, 4 * t:4 * t + 4, 0:8], elog[:, t, :, :])
            link(last)
            for t in range(TT):
                dve.max(TOPG[:, t, :], RG[:, t, :])
            for j in range(4 * TT):
                last = dve.max(TOPE[:, j, :], RE[:, j, :])
            link(last)
            dve.tensor_copy(REPG[:, :, 0:2], TOPG[:, :, 0:2])
            link(dve.tensor_copy(REPE[:, :, 0:2], TOPE[:, :, 0:2]))
            for t in range(TT):
                dve.match_replace(RGO[:, t, :], REPG[:, t, :], RG[:, t, :], 3.0e38)
            for j in range(4 * TT):
                dve.match_replace(REO[:, j, :], REPE[:, j, :], RE[:, j, :], 3.0e38)
            dve.tensor_tensor(GV, RG[:, :, 0:4], TOPG[:, :, 0:1].to_broadcast([P, TT, 4]), ALU.subtract)
            link(dve.tensor_tensor(EV, RE[:, :, 0:8], TOPE[:, :, 0:1].to_broadcast([P, 4 * TT, 8]), ALU.subtract))
            dve.tensor_scalar(RGO[:, :, 0:4], RGO[:, :, 0:4], 3.0e38, None, ALU.is_equal)
            dve.tensor_scalar(REO[:, :, 0:8], REO[:, :, 0:8], 3.0e38, None, ALU.is_equal).then_inc(rt_ok, 1)
            dve.wait_ge(rexp, 2)
            dve.tensor_tensor(GV, GV, RGO[:, :, 0:4], ALU.mult)
            link(dve.tensor_tensor(EV, EV, REO[:, :, 0:8], ALU.mult))
            dve.tensor_reduce(GSM, GV, AX, ALU.add)
            link(dve.tensor_reduce(ESM, EV, AX, ALU.add))
            dve.reciprocal(GSM, GSM)
            link(dve.reciprocal(ESM, ESM))
            link(dve.tensor_tensor(GV, GV, GSM.unsqueeze(2).to_broadcast([P, TT, 4]), ALU.mult))
            gflat = GV.rearrange("p t g -> p (t g)")
            link(dve.tensor_tensor(ESM, ESM, gflat, ALU.mult))
            dve.tensor_tensor(COMB.rearrange("p t (g e) -> p (t g) e", g=4), EV,
                              ESM.unsqueeze(2).to_broadcast([P, 4 * TT, 8]), ALU.mult).then_inc(comb_ok, 1)
            for m in range(XC):
                g = G["exp"] + 2 * m + 1
                ready(dve, g)
                read_out(dve, g - 1)
                dve.tensor_tensor(nodes(HS[:, m, :]), nodes(GT[m % 2]), tiles(buf(g)), ALU.mult)\
                   .then_inc(copied[g % NPS], 1)
            for t in range(TT):
                g = G["y"] + t
                ready(dve, g)
                dve.tensor_tensor(split(XRES[:, t, :]), halves(buf(g)), split(XRES[:, t, :]), ALU.add)\
                   .then_inc(copied[g % NPS], 1)


def _layout(i):
    c = np.ascontiguousarray
    col = lambda v, k: c(v.reshape(k, 128).T)
    r = {n: i[n] for n in ("x", "src", "dst")}
    for n in ("W1s", "b1s", "W1d", "b1d", "ln1_w", "ln1_b", "Wos", "bos", "Wod", "bod", "lno_w", "lno_b"):
        r[n] = i["L0_gnn_" + n]
    r["attn1"], r["attno"] = col(i["L0_gnn_attn1"].reshape(-1), 6), col(i["L0_gnn_attno"].reshape(-1), 6)
    f = "L0_ffn_"
    r["wqT"] = c(i[f + "wq"].T)
    for n in ("bq", "bn_gamma", "bn_beta", "bn_mean", "bn_var"):
        r[n] = col(i[f + n], 4)
    r["keysT"] = c(i[f + "keys"].transpose(0, 2, 1))
    r["w_down"], r["w_up"] = i[f + "w_down_tab"], i[f + "w_up_tab"]
    for n in ("a_w1", "a_w2", "a_w3", "s_w1", "s_w2", "s_w3"):
        r[n + "T"] = c(i[f + n].T)
    f = "L1_gnn_"
    for n, m in (("G1", "W1"), ("as1", "att_src1"), ("ad1", "att_dst1"), ("gb1", "b1"),
                 ("G2", "W2"), ("as2", "att_src2"), ("ad2", "att_dst2"), ("gb2", "b2")):
        r[n] = i[f + m]
    f = "L1_ffn_"
    wr = np.concatenate([i[f + "Wg"], i[f + "Wge"].transpose(1, 0, 2).reshape(768, 32)], axis=1)
    r["Wr"] = c(wr.reshape(6, 128, 36).transpose(1, 0, 2).reshape(128, 216))
    r["br"] = np.concatenate([i[f + "bg"], i[f + "bge"].reshape(-1)])
    r["W1c"] = c(i[f + "W1"].transpose(1, 0, 2).reshape(768, 3072))
    r["b1c"] = col(i[f + "b1"].reshape(-1), 24)
    r["W2"] = i[f + "W2"].reshape(3072, 768)
    r["b2"] = i[f + "b2"]
    return r


def kernel(**inputs):
    import concourse.bacc as _bacc
    from concourse.bass_utils import run_bass_kernel_spmd as _run

    nc = _bacc.Bacc("TRN2", target_bir_lowering=False, num_devices=1)
    arrays, args = {}, {}
    for name, v in _layout({k: np.asarray(v) for k, v in inputs.items()}).items():
        v = np.ascontiguousarray(v)
        if v.dtype == np.int32:
            v = v.view(np.uint32)
        arrays["in_" + name] = v
        args[name] = nc.dram_tensor("in_" + name, v.shape, mybir.dt.from_np(v.dtype), kind="ExternalInput").ap()
    out = nc.dram_tensor("out_0", (N, D), F32, kind="ExternalOutput").ap()
    emit(nc, args, out)
    r = _run(nc, [arrays], core_ids=[0])
    return r.results[0]["out_0"]
```

```python
from contextlib import ExitStack

import numpy as np
import concourse.bass as bass
from concourse import mybir

F32 = mybir.dt.float32
BF16 = mybir.dt.bfloat16
FP16 = mybir.dt.float16
U32 = mybir.dt.uint32
ALU = mybir.AluOpType
ACT = mybir.ActivationFunctionType
AX = mybir.AxisListType.X

N, E, D = 625, 10000, 768
P = 125
TT = N // P
ET = E // P
KC = D // 128
HALF = D // 2
RING = 5
EG = ET // RING
BODY = 2 * RING
LAG = (11, 9)
HEADS = 8
TROWS = 128 * 3052
FILLW = 1526
KNN, PH, NKEY = 16, 4, 800
HK = PH * KNN
HIDA = 44
HIDS = 1024
EXP, MH = 32, 96
XH = EXP * MH
XC = XH // 128
NEG = -1.0e30
EPS = 1e-5
NCOL = 10
NPS = 3


def emit(nc, a, out):
    ctx = ExitStack()
    with ctx:
        arena = ctx.enter_context(nc.sbuf_tensor("arena", [128, 52900], F32))
        DB = [ctx.enter_context(nc.psum_tensor(f"DB{i}", [128, 1024], F32)) for i in range(4)]
        ACC = DB[3]

        def sem(name):
            return ctx.enter_context(nc.semaphore(name))

        def at(off, n, p=128):
            return arena[0:p, off:off + n]

        def at3(off, x, y, p=128):
            return arena[0:p, off:off + x * y].rearrange("p (x y) -> p x y", x=x)

        XRES = at3(0, TT, D, P)
        XN = at3(3840, TT, D, P)
        XT = at3(7680, KC, N)
        CNT = at3(11520, TT, N, P)
        NODE = at3(14720, TT, D, P)
        HACC = at3(18560, TT, D, P)
        WA = at3(22400, KC, D)
        WB = at3(27008, KC, D)
        BS, BD, LNW, LNB = (at(31616 + D * i, D, P) for i in range(4))
        PT = [at3(34688 + N * i, TT, P, P) for i in range(2)]
        LGS = at3(35938, EG + 1, RING * HEADS, P)
        TB = [at(36640 + 5000 * i, 5000, P) for i in range(2)]
        TC = [at(36640 + N * i, N, P) for i in range(TT)]
        U = at3(36640, RING, D, P)
        V = at3(36640 + RING * D, RING, D, P)
        ZT = [at3(44320 + 750 * i, KC, P) for i in range(2)]
        OHS = [arena[0:P, 46640 + 313 * i:46640 + 313 * (i + 1)].bitcast(BF16)[:, 0:N] for i in range(2)]
        OHD = [arena[0:P, 47266 + 313 * i:47266 + 313 * (i + 1)].bitcast(BF16)[:, 0:N] for i in range(2)]
        IOTA = arena[0:P, 34688:34688 + 313].bitcast(FP16)[:, 0:N]
        IOTF = at(18560, N, P)
        CXS = arena[0:P, 36640:36640 + 4520].bitcast(BF16).rearrange("p (t n) -> p t n", t=ET)
        CXD = arena[0:P, 41160:41160 + 5000].bitcast(BF16).rearrange("p (t n) -> p t n", t=ET)
        MN = at3(46640, 2, D, P)
        FILL = at(48176, FILLW)
        ATR = at(48176, D, P)
        LGD = at(48176 + D, BODY, P)
        ATT = at3(49702, KC, HEADS)
        ATC = at(49750, KC)
        IDX = arena[0:P, 49760:49920].bitcast(U32).rearrange("p (a t) -> p a t", a=2)
        TIDX = arena[0:P, 49920:50000].bitcast(U32)
        IDF = at3(50000, 2, ET, P)
        TIF = at(50160, ET, P)
        ZERO = arena[0:P, 50250:50570].bitcast(BF16)
        WQ = at3(22400, KC, PH * 128)
        SW2 = at3(25472, 8, D)
        KEYS = at3(14720, PH, NKEY)
        SIL = [at(17920, N), at(51083, N)]
        OHB = at3(18560, HK, 32, P)
        V16, XDV, GAT, WDC, WUC = (at3(20608 + 320 * i, TT, HK, P) for i in range(5))
        GS = at3(31616, 8, N)
        SWR = at3(36616, 8, D)
        SC = [at(42760 + NKEY * i, NKEY, P) for i in range(2)]
        WK = at(44360, NKEY, P)
        OHA = at3(45160, HK, 32, P)
        OHAT = [at3(47208 + 1000 * i, 8, P) for i in range(2)]
        ZG = at3(49208, 2, N, 88)
        XDT = at(50458, N, HK)
        A1 = at(51708, 176, HK)
        A3 = at(51884, 176, HK)
        A2 = at3(52060, 2, HK, 88)
        TBL = at3(52188, 4, 64)
        QT = at3(3840, PH, N)
        SELP = at(6340, 1024, P)
        IDXK = arena[0:P, 7364:7428].bitcast(U32)
        IDA = arena[0:P, 7428:7492].bitcast(U32)
        IDB = arena[0:P, 7492:7556].bitcast(U32)
        IDKF = at3(7556, 1, HK, P)
        BNV = at3(52826, 5, PH)
        BNA = at(52846, PH)
        BNB = at(52850, PH)
        GB = [at(31616 + D * i, D, P) for i in range(6)]
        ASB = at(36224, N, P)
        EB = [at(o, N, P) for o in (36864, 37504, 44200, 50450, 39424)]
        PG = [at3(38144 + 640 * i, TT, P, P) for i in range(2)]
        DG = at3(39424, TT, P, P)
        MB = at3(40100, TT, N, P)
        JUNK = at(43300, D, P)
        HS = at3(11520, XC, N)
        W2 = at3(26520, XC, D)
        W1R = at3(44952, 4, D)
        SELE = arena[0:3 * EXP, 48024:48024 + XH // 2].bitcast(BF16)
        CTB = arena[0:3 * EXP, 49560:49873].bitcast(BF16)[:, 0:N]
        C3 = at3(49880, TT, 3 * EXP, P)
        CPB = arena[0:P, 50360:50440].bitcast(BF16).rearrange("p (t e) -> p t e", t=TT)
        B2 = at(51096, D, 3 * EXP)
        GT = [at(o, N) for o in (3840, 3840 + N, 50450)]
        CT = at(5090, N, 3 * EXP)
        RT = at3(5720, TT, 36, P)
        RG = at3(5900, TT, 12, P)
        RE = at3(5960, TT * 4, 14, P)
        RGO = at3(6240, TT, 12, P)
        REO = at3(6300, TT * 4, 14, P)
        TOPG = at3(6580, TT, 8, P)
        TOPE = at3(6620, TT * 4, 8, P)
        REPG = at3(6780, TT, 8, P)
        REPE = at3(6820, TT * 4, 8, P)
        GV = at3(6980, TT, 4, P)
        EV = at3(7000, TT * 4, 8, P)
        GSM = at(7160, TT, P)
        ESM = at(7165, TT * 4, P)
        COMB = at3(7185, TT, EXP, P)
        BR = at(52080, 36, P)
        B1C = at(52116, XC)
        WR = at3(51864, KC, 36)
        IDENT = at(52444, P, P)
        IO32 = at(52570, 32, P)
        STATS = at3(52602, TT * 2, 6, P)
        MV = at3(52662, TT, 2, P)
        MX = at3(52810, 2, HEADS, P)
        NMX = at3(52686, 2, HEADS, P)
        DEN = at3(52702, 2, HEADS, P)
        RDEN = at(52718, HEADS, P)
        SX = at(52726, TT, P)
        CMB = at(52731, TT, P)
        AS = at(52736, TT, P)
        AD = at(52741, TT, P)
        KM = at3(52746, TT, PH, P)
        KS = at3(52766, TT, PH, P)
        ONES = at(52786, 2, P)
        VARE, NMU, RSTD, NMR = (at(52856 + NCOL * i, NCOL, P) for i in range(4))
        EXPN = at(52794, 6)
        BNR = at(52800, PH)
        MBONES = at(43225 + 843, P, P)

        FS = [nc.dram_tensor(f"src_rows{l}", (N, D), F32, kind="Internal").ap() for l in range(2)]
        FD = [nc.dram_tensor(f"dst_rows{l}", (N, D), F32, kind="Internal").ap() for l in range(2)]
        LT = [nc.dram_tensor(f"logits{l}", (TROWS, h), F32, kind="Internal").ap() for l, h in enumerate((HEADS, 1))]

        pe_done = sem("pe_done")
        copied = [sem(f"copied{i}") for i in range(NPS)]
        acc_free = sem("acc_free")
        dve_step, act_step, pool_step = sem("dve_step"), sem("act_step"), sem("pool_step")
        x_in, idx_in = [sem(f"x_in{t}") for t in range(TT)], sem("idx_in")
        wa_in, wb_in, bias_in, lnp_in, att_in = sem("wa_in"), sem("wb_in"), sem("bias_in"), sem("lnp_in"), sem("att_in")
        filled = sem("filled")
        consts = sem("consts")
        var_ok, rstd_ok = sem("var_ok"), sem("rstd_ok")
        bnv_ok, bnr_ok = sem("bnv_ok"), sem("bnr_ok")
        idx_ok = sem("idx_ok")
        atr_in, dotted = sem("atr_in"), sem("dotted")
        oh_ready, oh_used = sem("oh_ready"), sem("oh_used")
        cx_ready = sem("cx_ready")
        cnt_done, cnt_ok = sem("cnt_done"), sem("cnt_ok")
        feat = sem("feat")
        rows_out = sem("rows_out")
        gath = [sem(f"gath{r}") for r in range(RING)]
        z_sum, z_ready = sem("z_sum"), sem("z_ready")
        zt_done, zt_copied = sem("zt_done"), sem("zt_copied")
        lg_done, lg_copied = sem("lg_done"), sem("lg_copied")
        scattered = sem("scattered")
        tb_in = [sem("tb_in0"), sem("tb_in1")]
        tc_in = [sem(f"tc_in{i}") for i in range(TT)]
        negmax, exped, p_ready, pv_done = (sem(s) for s in ("negmax", "exped", "p_ready", "pv_done"))
        min_ok, expm_ok = sem("min_ok"), sem("expm_ok")
        bn_in, ffn_in, keys_in, sw2_in, peer_in = sem("bn_in"), sem("ffn_in"), sem("keys_in"), sem("sw2_in"), sem("peer_in")
        swr_in = [sem(f"swr_in{i}") for i in range(4)]
        tbl_ok = sem("tbl_ok")
        sc_used, oha_ok = sem("sc_used"), sem("oha_ok")
        kgate, kexp = sem("kgate"), sem("kexp")
        xd_ok, bn_ok = sem("xd_ok"), sem("bn_ok")
        gw_in, gb_in = sem("gw_in"), sem("gb_in")
        diag_ok = sem("diag_ok")
        w1_in = [sem(f"w1_in{i}") for i in range(4)]
        w2_in, xb_in = sem("w2_in"), sem("xb_in")
        sele_ok, rt_ok, rexp, comb_ok, ctb_ok = (sem(s) for s in ("sele_ok", "rt_ok", "rexp", "comb_ok", "ctb_ok"))
        y_out = sem("y_out")
        out_v = out.rearrange("(t p) d -> p t d", p=P)

        G, ngroups = {}, [0]

        def take(name, count):
            G[name] = ngroups[0]
            ngroups[0] += count

        def take_weights(turned, rows):
            for i in range(TT):
                take((turned, i), 1)
                if i:
                    take((rows, i - 1), 1)
            take((rows, TT - 1), 1)

        def rows_order(i, names):
            order = [("xT", i, 0)]
            for t in range(TT):
                if t + 1 < TT:
                    order.append(("xT", i, t + 1))
                order += [(name, t) for name in names]
            return order

        def take_all(order):
            for item in order:
                take(item, 1)

        proj_order = [rows_order(l, (("src", l), ("dst", l))) for l in range(2)]
        h_order = [rows_order(3 + l, (("h", l),)) for l in range(2)]
        for l in range(2):
            take_all(proj_order[l])
            if l == 0:
                take("cx", 1)
                take("pt0", TT * HEADS)
            else:
                take_weights("pt1", "pv1")
        take_all([("xT", 2, t) for t in range(TT)])
        take("q", PH)
        sched = []
        for t in range(TT):
            for h in range(PH):
                s = t * PH + h
                sched.append(("sc", s))
                if s < 16:
                    sched.append(("z", s))
            if t == TT - 1:
                sched += [("down", 0), ("down", 1)]
            sched += [("oha", t, 0), ("oha", t, 1)] + [("pick", t, q) for q in range(4)]
        take_all(sched)
        take_all([("down", 2), "xd", ("down", 3)])
        take("peer", 4)
        take_all([("down", 4), "peer_out"])
        for l in range(2):
            take_all(h_order[l])
            take(f"asb{l}", 1)
            take_weights(f"gt{l}", f"gv{l}")
        take_all([("xT", 5, t) for t in range(TT)])
        take("route", 1)
        moe = [("up", m) for m in range(3)] + ["ct"]
        for m in range(XC):
            moe.append(("cb", m))
            if m + 3 < XC:
                moe.append(("up", m + 3))
        take_all(moe)
        take("y", TT)

        norms = [("x", t) for t in range(TT)] + [("ln0", t) for t in range(TT)]
        for t in range(TT):
            norms += [("ln1", t)] + ([("ffn", t - 1)] if t else [])
        norms += [("ffn", TT - 1)] + [("gat", t) for t in range(TT)] + [("moe", t) for t in range(TT)]
        norm_no = {name: k for k, name in enumerate(norms)}

        def buf(g):
            return DB[g % NPS]

        def halves(b):
            return b[0:P, :].rearrange("p (a n) -> p a n", a=2)[:, :, 0:HALF]

        def split(ap):
            return ap.rearrange("p (a n) -> p a n", a=2)

        def tiles(b, p=128):
            return b[0:p, 0:640].rearrange("p (t n) -> p t n", t=TT)[:, :, 0:P]

        def nodes(ap):
            return ap.rearrange("p (t n) -> p t n", t=TT)

        def ready(eng, g):
            eng.wait_ge(pe_done, g + 1)

        def read_out(eng, g):
            eng.wait_ge(copied[g % NPS], g // NPS + 1)

        def all_read_out(eng, last):
            for g in range(last - NPS + 1, last + 1):
                read_out(eng, g)

        def col(i):
            return i % 2, i // 2

        def claim(pe, g):
            if g >= NPS:
                pe.wait_ge(copied[g % NPS], g // NPS)

        def claim_acc(pe, n):
            if n:
                pe.wait_ge(acc_free, n)

        LH = (HEADS, 1)
        p_first = [TT * n for n in (0, HEADS, HEADS + 1, HEADS + 2)]

        def cnt_main(i):
            return DB[1 + i // 2][0:P, 512 * (i % 2):512 * (i % 2) + 512] if i < 4 else DB[3][0:P, 0:512]

        def cnt_rest(i):
            return DB[3][0:P, 512 + 113 * i:512 + 113 * (i + 1)]

        block = ctx.enter_context(nc.Block())

        @block.sync
        def _(sp):
            def rows(w):
                return w.rearrange("(c p) n -> p c n", p=128)

            def bcast(v):
                return v.rearrange("(o n) -> o n", o=1).broadcast_to([P, v.shape[0]])

            for t in range(TT):
                sp.dma_start(XRES[:, t, :], a["x"][t * P:(t + 1) * P, :]).then_inc(x_in[t], 16)
            sp.dma_start(IDX[:, 0, :], a["src"].rearrange("(p t) -> p t", p=P)).then_inc(idx_in, 16)
            sp.dma_start(IDX[:, 1, :], a["dst"].rearrange("(p t) -> p t", p=P)).then_inc(idx_in, 16)
            sp.dma_start(WA, rows(a["W1s"])).then_inc(wa_in, 16)
            sp.dma_start(WB, rows(a["W1d"])).then_inc(wb_in, 16)
            sp.dma_start(BS, bcast(a["b1s"])).then_inc(bias_in, 16)
            sp.dma_start(BD, bcast(a["b1d"])).then_inc(bias_in, 16)
            sp.dma_start(LNW, bcast(a["ln1_w"])).then_inc(lnp_in, 16)
            sp.dma_start(LNB, bcast(a["ln1_b"])).then_inc(lnp_in, 16)
            sp.dma_start(ATC, a["attn1"]).then_inc(att_in, 16)
            sp.wait_ge(consts, 1)
            wide = LT[0].rearrange("(p n) h -> p (n h)", p=128).rearrange("p (a n) -> p a n", a=16)
            sp.dma_start(wide, FILL.unsqueeze(1).to_broadcast([128, 16, FILLW])).then_inc(filled, 16)
            thin = LT[1].rearrange("(p n) h -> p (n h)", p=128).rearrange("p (a n) -> p a n", a=2)
            sp.dma_start(thin, FILL.unsqueeze(1).to_broadcast([128, 2, FILLW])).then_inc(filled, 16)
            for l in range(2):
                for t in range(TT):
                    read_out(sp, G[(("src", l), t)])
                    read_out(sp, G[(("dst", l), t)])
                    sp.dma_start(FS[l][t * P:(t + 1) * P, :], NODE[:, t, :]).then_inc(rows_out, 16)
                    sp.dma_start(FD[l][t * P:(t + 1) * P, :], HACC[:, t, :]).then_inc(rows_out, 16)
                sp.wait_ge(lg_copied, (EG + 1) * l + 2)
                if l == 0:
                    sp.dma_start(WA, rows(a["Wos"])).then_inc(wa_in, 16)
                    sp.dma_start(WB, rows(a["Wod"])).then_inc(wb_in, 16)
                    sp.wait_ge(filled, 32)
                    sp.dma_start(ATR, bcast(a["attno"])).then_inc(atr_in, 16)
                    sp.dma_start(BS, bcast(a["bos"])).then_inc(bias_in, 16)
                    sp.dma_start(BD, bcast(a["bod"])).then_inc(bias_in, 16)
                else:
                    sp.dma_start(WQ, rows(a["wqT"])).then_inc(ffn_in, 16)
                    sp.dma_start(SW2, rows(a["s_w2T"])).then_inc(sw2_in, 16)
                sp.wait_ge(scattered, 16 * ET * (l + 1))
                for i in range(TT):
                    if l == 0 and i >= 2:
                        sp.wait_ge(pe_done, G["pt0"] + HEADS * (i - 1))
                    table = LT[l][i * P * N:(i + 1) * P * N, :].rearrange("(p n) h -> p (n h)", p=P)
                    if l == 0:
                        sp.dma_start(TB[i % 2], table).then_inc(tb_in[i % 2], 16)
                    else:
                        sp.dma_start(TC[i], table).then_inc(tc_in[i], 16)
                if l == 0:
                    sp.wait_ge(feat, 2 * TT)
                    sp.dma_start(LNW, bcast(a["lno_w"])).then_inc(lnp_in, 16)
                    sp.dma_start(LNB, bcast(a["lno_b"])).then_inc(lnp_in, 16)
            sp.wait_ge(feat, 3 * TT)
            sp.dma_start(KEYS, a["keysT"].rearrange("h k n -> k h n")).then_inc(keys_in, 16)
            for v, name in enumerate(("bq", "bn_gamma", "bn_beta", "bn_mean", "bn_var")):
                sp.dma_start(BNV[:, v, :], a[name]).then_inc(bn_in, 16)
            sw = [a["s_w1T"], a["s_w3T"]]
            for z in range(16):
                m, which = z // 2, z % 2
                if z >= 8:
                    sp.wait_ge(pe_done, G[("z", 2 * (m - 4) + 1)] + 1)
                sp.dma_start(SWR[:, 2 * (m % 4) + which, :].rearrange("p (c n) -> p c n", c=KC),
                             rows(sw[which])[:, :, m * 128:(m + 1) * 128]).then_inc(swr_in[m % 4], 16)
                if z == 7:
                    sp.wait_ge(tbl_ok, 1)
                    for g in range(PH):
                        for v, name in enumerate(("w_down", "w_up")):
                            sp.dma_start(TBL[32 * g:32 * g + 25, g, 32 * v:32 * v + 32],
                                         a[name].rearrange("(x y) o -> x (y o)", y=32)).then_inc(peer_in, 16)
                        sp.dma_start(A1[KNN * g:KNN * (g + 1), HIDA * g:HIDA * (g + 1)], a["a_w1T"]).then_inc(peer_in, 16)
                        sp.dma_start(A3[KNN * g:KNN * (g + 1), HIDA * g:HIDA * (g + 1)], a["a_w3T"]).then_inc(peer_in, 16)
                        sp.dma_start(A2[HIDA * (g % 2):HIDA * (g % 2 + 1), g // 2, KNN * g:KNN * (g + 1)],
                                     a["a_w2T"]).then_inc(peer_in, 16)
            sp.wait_ge(feat, 3 * TT + 1)
            sp.dma_start(WA, rows(a["G1"])).then_inc(gw_in, 16)
            for i, name in enumerate(("as1", "ad1", "gb1", "as2", "ad2", "gb2")):
                sp.dma_start(GB[i], bcast(a[name])).then_inc(gb_in, 16)
            sp.dma_start(WB, rows(a["G2"])).then_inc(wb_in, 16)
            for k in range(3):
                sp.dma_start(B2[EXP * k:EXP * (k + 1), :], a["b2"]).then_inc(xb_in, 16)
            sp.dma_start(WR, a["Wr"].rearrange("p (c n) -> p c n", c=KC)).then_inc(xb_in, 16)
            sp.dma_start(BR, bcast(a["br"])).then_inc(xb_in, 16)
            sp.dma_start(B1C, a["b1c"]).then_inc(xb_in, 16)
            for m in range(XC):
                if m == 4:
                    sp.wait_ge(feat, 6 * TT)
                    for c in range(3):
                        sp.dma_start(W2[:, 8 * c:8 * c + 8, :], rows(a["W2"])[:, 8 * c:8 * c + 8, :]).then_inc(w2_in, 16)
                if m >= 4:
                    sp.wait_ge(pe_done, G[("up", m - 4)] + 1)
                sp.dma_start(W1R[:, m % 4, :].rearrange("p (c n) -> p c n", c=KC),
                             rows(a["W1c"])[:, :, m * 128:(m + 1) * 128]).then_inc(w1_in[m % 4], 16)
            for t in range(TT):
                read_out(sp, G["y"] + t)
                sp.dma_start(out_v[:, t, :], XRES[:, t, :]).then_inc(y_out, 16)
            sp.wait_ge(y_out, 16 * TT)

        @block.gpsimd
        def _(pool):
            steps = [0]

            def link(ins):
                steps[0] += 1
                ins.then_inc(pool_step, 1)
                pool.wait_ge(pool_step, steps[0])

            pool.memset(FILL, NEG).then_inc(consts, 1)
            pool.iota(IOTF, [[1, N]], base=0, channel_multiplier=0, allow_small_or_imprecise_dtypes=True).then_inc(consts, 1)
            pool.iota(IOTA, [[1, N]], base=0, channel_multiplier=0, allow_small_or_imprecise_dtypes=True).then_inc(consts, 1)
            pool.memset(ZERO, 0.0).then_inc(consts, 1)
            link(pool.memset(IDENT, 0.0))
            pool.affine_select(out=IDENT, in_=IDENT, compare_op=ALU.not_equal, fill=1.0, base=0,
                               pattern=[[-1, P]], channel_multiplier=1).then_inc(consts, 1)
            pool.iota(IO32, [[1, 32]], base=0, channel_multiplier=0, allow_small_or_imprecise_dtypes=True).then_inc(consts, 1)
            link(pool.memset(ATT, 1.0))
            link(pool.affine_select(out=ATT, in_=ATT, compare_op=ALU.is_ge, fill=0.0, base=0,
                                    pattern=[[128, KC], [-D // HEADS, HEADS]], channel_multiplier=1))
            pool.affine_select(out=ATT, in_=ATT, compare_op=ALU.is_ge, fill=0.0, base=D // HEADS - 1,
                               pattern=[[-128, KC], [D // HEADS, HEADS]], channel_multiplier=-1).then_inc(consts, 1)
            def rsqrt_var(name):
                for k in [k for k, (n, t) in enumerate(norms) if n in name]:
                    c = k % NCOL
                    pool.wait_ge(var_ok, k + 1)
                    link(pool.tensor_tensor(RSTD[:, c:c + 1], VARE[:, c:c + 1], EXPN[0:P, 0:1], ALU.pow))
                    pool.tensor_tensor(NMR[:, c:c + 1], NMU[:, c:c + 1], RSTD[:, c:c + 1], ALU.mult).then_inc(rstd_ok, 1)

            link(pool.memset(EXPN, -0.5))
            rsqrt_var(("x",))
            pool.wait_ge(idx_ok, 1)
            pool.wait_ge(filled, 32)

            for l in range(2):
                pool.wait_ge(rows_out, 32 * TT * (l + 1))
                if l == 0:
                    pool.wait_ge(pe_done, G["cx"] + 1)

                lag = LAG[l]

                def scatter(t):
                    pool.wait_ge(lg_copied, t // RING + 2 if l == 0 else EG + 1 + t // RING + 1)
                    if ET * l + t:
                        pool.wait_ge(scattered, 16 * (ET * l + t))
                    pool.indirect_dma_start(
                        out=LT[l], out_offset=bass.IndirectOffsetOnAxis(ap=TIDX[:, t:t + 1], axis=0),
                        in_=LGS[:, t // RING + 1 - l, LH[l] * (t % RING):LH[l] * (t % RING + 1)], in_offset=None,
                    ).then_inc(scattered, 16)

                for t in range(ET):
                    r = t % RING
                    if t >= lag:
                        scatter(t - lag)
                    if t >= RING and l == 0:
                        pool.wait_ge(zt_done, 2 * (t - RING + 1))
                    if t >= RING and l == 1:
                        pool.wait_ge(dotted, t - RING + 1)
                    for table, k, dst in ((FS[l], 0, U), (FD[l], 1, V)):
                        pool.indirect_dma_start(
                            out=dst[:, r, :], out_offset=None, in_=table,
                            in_offset=bass.IndirectOffsetOnAxis(ap=IDX[:, k, t:t + 1], axis=0)).then_inc(gath[r], 16)
                for t in range(ET - lag, ET):
                    scatter(t)
                rsqrt_var((("ln0",), ("ln1", "ffn"))[l])
            pool.wait_ge(feat, 3 * TT)
            link(pool.memset(at(51708, 736), 0.0))
            pool.memset(ONES, 1.0).then_inc(tbl_ok, 1)
            pool.wait_ge(bnv_ok, 1)
            pool.tensor_tensor(BNA, BNR, EXPN[:, 0:PH], ALU.pow).then_inc(bnr_ok, 1)
            rsqrt_var(("gat",))
            pool.wait_ge(feat, 4 * TT)
            link(pool.memset(SELE, 1.0))
            for k in range(3):
                part = SELE[EXP * k:EXP * (k + 1), :]
                link(pool.affine_select(out=part, in_=part, compare_op=ALU.is_ge, fill=0.0, base=0,
                                        pattern=[[1, XH]], channel_multiplier=-MH))
                pool.affine_select(out=part, in_=part, compare_op=ALU.is_ge, fill=0.0, base=MH - 1,
                                   pattern=[[-1, XH]], channel_multiplier=MH).then_inc(sele_ok, 1)
            pool.wait_ge(sele_ok, 3)
            rsqrt_var(("moe",))

        @block.tensor
        def _(pe):
            mm = nc.tensor.matmul

            def turn_node_tile(i, t):
                pe.wait_ge(feat, TT * i + t + 1)
                g = G[("xT", i, t)]
                claim(pe, g)
                for c in range(KC):
                    last = nc.tensor.transpose(buf(g)[:, 128 * c:128 * c + P], XN[:, t, 128 * c:128 * (c + 1)], IDENT)
                last.then_inc(pe_done, 1)

            def turn_nodes(i):
                for t in range(TT):
                    turn_node_tile(i, t)
                all_read_out(pe, G[("xT", i, TT - 1)])

            def node_rows(g, t, w):
                claim(pe, g)
                for c in range(KC):
                    for s in range(2):
                        last = mm(buf(g)[0:P, 512 * s:512 * s + HALF], XT[:, c, t * P:(t + 1) * P],
                                  w[:, c, HALF * s:HALF * (s + 1)], start=c == 0, stop=c == KC - 1)
                last.then_inc(pe_done, 1)

            def wide_rows(g, chunks, lhs, rhs, m=128):
                claim(pe, g)
                for c in range(chunks):
                    for lo, hi, at0 in ((0, 4, 0), (4, 5, 512)):
                        o = buf(g)[0:m, at0:at0 + 128 * (hi - lo)].rearrange("p (t n) -> p t n", n=128)[:, :, 0:P]
                        last = mm(o, lhs(c), rhs(c)[:, lo * P:hi * P], start=c == 0, stop=c == chunks - 1)
                last.then_inc(pe_done, 1)

            def turn_tiles(g, src, p=P):
                claim(pe, g)
                for t in range(TT):
                    last = nc.tensor.transpose(buf(g)[0:p, 128 * t:128 * t + P], src(t), IDENT)
                last.then_inc(pe_done, 1)

            def weighted_rows(turned, rows, first, weights, slots):
                def turn_weights(i):
                    pe.wait_ge(p_ready, first + i + 1)
                    turn_tiles(G[(turned, i)], lambda t: weights(i)[:, t * P:(t + 1) * P])

                turn_weights(0)
                for i in range(TT):
                    if i + 1 < TT:
                        turn_weights(i + 1)
                    read_out(pe, G[(turned, i)])
                    g = G[(rows, i)]
                    claim(pe, g)
                    for s in range(2):
                        for j in range(TT):
                            last = mm(buf(g)[0:P, 512 * s:512 * s + HALF], slots[i % 2][:, j, :],
                                      NODE[:, j, HALF * s:HALF * (s + 1)], start=j == 0, stop=j == TT - 1)
                    last.then_inc(pe_done, 1)

            counts = [(cnt_main(i), i, 0, 512) for i in range(TT)] + [(cnt_rest(i), i, 512, N) for i in range(4)]
            banks = [DB[1][0:P, 0:512], DB[1][0:P, 512:1024], DB[2][0:P, 0:512], DB[2][0:P, 512:1024],
                     DB[3][0:P, 0:512], DB[3][0:P, 512:1024]]

            pe.wait_ge(consts, 4)
            for l in range(2):
                for item in proj_order[l]:
                    if item[0] == "xT":
                        turn_node_tile(l, item[2])
                        continue
                    (side, _), t = item
                    if side == "src":
                        pe.wait_ge(wa_in, 16 * (l + 1))
                        read_out(pe, G[("xT", l, t)])
                    else:
                        pe.wait_ge(wb_in, 16 * (l + 1))
                    node_rows(G[item], t, WA if side == "src" else WB)
                if l == 0:
                    claim(pe, G["cx"])
                    pe.wait_ge(cx_ready, 1)
                    for t in range(ET):
                        last = mm(buf(G["cx"])[0:P, 0:113], CXD[:, t, :], CXS[:, t, :], start=t == 0, stop=t == ET - 1)
                    last.then_inc(pe_done, 1)
                if l == 0:
                    all_read_out(pe, G["cx"])
                    for b in banks:
                        mm(b, ZERO[:, 0:P], ZERO[:, 0:512], start=True, stop=False)
                    nh = HEADS
                    zps = DB[0][:, 0:384].rearrange("p (c n) -> p c n", c=3)
                    mm(DB[0][0:P, 512:512 + RING * nh], IDENT, XN[:, 0, 0:RING * nh], start=True, stop=True).then_inc(lg_done, RING)
                    with pe.Fori(0, ET // BODY) as g:
                        def count(r, some):
                            for o, i, lo, hi in some:
                                last = mm(o, OHD[r % 2][:, i * P:(i + 1) * P], OHS[r % 2][:, lo:hi], start=False, stop=False)
                            return last

                        def turn(r, half):
                            pe.wait_ge(zt_copied, 2 * BODY * g + 2 * r + half + 2)
                            for c in range(3):
                                f = 128 * (3 * half + c)
                                last = nc.tensor.transpose(zps[:, c, 0:P], U[:, r % RING, f:f + 128], IDENT)
                            last.then_inc(zt_done, 1)

                        def logits(r):
                            pe.wait_ge(zt_copied, 2 * BODY * g + 2 * r + 4)
                            if r % RING == 0:
                                pe.wait_ge(lg_copied, 2 * g + r // RING + 1)
                            for c in range(KC):
                                o = 512 + nh * (r % RING)
                                last = mm(DB[0][0:P, o:o + nh], ZT[r % 2][:, c, :], ATT[:, c, :], start=c == 0, stop=c == KC - 1)
                            last.then_inc(lg_done, 1)

                        for r in range(BODY):
                            pe.wait_ge(z_ready, BODY * g + r + 1)
                            turn(r, 0)
                            pe.wait_ge(oh_ready, BODY * g + r + 1)
                            count(r, counts[:3])
                            if r:
                                logits(r - 1)
                            turn(r, 1)
                            count(r, counts[3:]).then_inc(oh_used, 1)
                        logits(BODY - 1)
                    for b in banks:
                        last = mm(b, ZERO[:, 0:P], ZERO[:, 0:512], start=False, stop=True)
                    last.then_inc(cnt_done, 1)
                    pe.wait_ge(cnt_ok, 1)
                    pe.wait_ge(lg_copied, EG + 1)

                if l == 1:
                    weighted_rows("pt1", "pv1", p_first[1], lambda i: TC[i], PT)
                    continue
                HD = D // HEADS
                heads = [(i, h) for i in range(TT) for h in range(HEADS)]

                def turn_head(k):
                    i, h = heads[k]
                    pe.wait_ge(p_ready, k + 1)
                    view = TB[i % 2].rearrange("p (n h) -> p h n", h=HEADS)[:, h, :]
                    turn_tiles(G["pt0"] + k, lambda t: view[:, t * P:(t + 1) * P])

                turn_head(0)
                for k, (i, h) in enumerate(heads):
                    if k + 1 < len(heads):
                        turn_head(k + 1)
                    read_out(pe, G["pt0"] + k)
                    if h == 0:
                        claim_acc(pe, i)
                    o, f = 512 * (h // 4) + HD * (h % 4), h * HD
                    for j in range(TT):
                        last = mm(ACC[0:P, o:o + HD], PT[k % 2][:, j, :], NODE[:, j, f:f + HD], start=j == 0, stop=j == TT - 1)
                    last.then_inc(pv_done, 1)

            turn_nodes(2)
            pe.wait_ge(ffn_in, 16)
            for h in range(PH):
                wide_rows(G["q"] + h, KC, lambda c: WQ[:, c, h * 128:(h + 1) * 128], lambda c: XT[:, c, :])
            all_read_out(pe, G["q"] + PH - 1)
            pe.wait_ge(keys_in, 16)

            def down(t):
                if t == 0:
                    for m in range(8):
                        read_out(pe, G[("z", 2 * m + 1)])
                    pe.wait_ge(sw2_in, 16)
                g = G[("down", t)]
                claim(pe, g)
                for m in range(8):
                    for s in range(2):
                        last = mm(buf(g)[0:P, 512 * s:512 * s + HALF], GS[:, m, t * P:(t + 1) * P],
                                  SW2[:, m, HALF * s:HALF * (s + 1)], start=m == 0, stop=m == 7)
                last.then_inc(pe_done, 1)

            for item in sched:
                g = G[item]
                if item[0] == "sc":
                    t, h = divmod(item[1], PH)
                    claim(pe, g)
                    for s in range(2):
                        last = mm(buf(g)[0:P, 512 * s:512 * s + 400], QT[:, h, t * P:(t + 1) * P],
                                  KEYS[:, h, 400 * s:400 * (s + 1)], start=True, stop=True)
                    last.then_inc(pe_done, 1)
                elif item[0] == "z":
                    m, which = divmod(item[1], 2)
                    pe.wait_ge(swr_in[m % 4], 32 * (m // 4 + 1))
                    w = SWR[:, 2 * (m % 4) + which, :].rearrange("p (c n) -> p c n", c=KC)
                    wide_rows(g, KC, lambda c: w[:, c, :], lambda c: XT[:, c, :])
                elif item[0] == "oha":
                    _, t, half = item
                    pe.wait_ge(oha_ok, t + 1)
                    claim(pe, g)
                    for j in range(8):
                        k = 8 * half + j
                        last = nc.tensor.transpose(buf(g)[:, 128 * j:128 * j + P],
                                                   OHA[:, 4 * k:4 * k + 4, :].rearrange("p a b -> p (a b)"), IDENT)
                    last.then_inc(pe_done, 1)
                elif item[0] == "pick":
                    _, t, q = item
                    read_out(pe, G[("oha", t, q // 2)])
                    pe.wait_ge(peer_in, 16 * 20)
                    claim(pe, g)
                    for j in range(4):
                        k = 4 * q + j
                        last = mm(buf(g)[0:P, 256 * j:256 * (j + 1)], OHAT[k // 8][:, k % 8, :],
                                  TBL.rearrange("p a b -> p (a b)"), start=True, stop=True)
                    last.then_inc(pe_done, 1)
                else:
                    down(item[1])
            down(2)
            pe.wait_ge(xd_ok, 1)
            turn_tiles(G["xd"], lambda t: XDV[:, t, :], HK)
            down(3)
            read_out(pe, G["xd"])
            for pair in range(2):
                for which, w in enumerate((A1, A3)):
                    wide_rows(G["peer"] + 2 * pair + which, 1, lambda c: w[:, 88 * pair:88 * (pair + 1)], lambda c: XDT, 88)
            down(4)
            g = G["peer_out"]
            claim(pe, g)
            for pair in range(2):
                read_out(pe, G["peer"] + 2 * pair + 1)
            for t in range(TT):
                for pair in range(2):
                    last = mm(buf(g)[0:P, HK * t:HK * (t + 1)], ZG[:, pair, t * P:(t + 1) * P], A2[:, pair, :],
                              start=pair == 0, stop=pair == 1)
            last.then_inc(pe_done, 1)

            for l in range(2):
                for item in h_order[l]:
                    if item[0] == "xT":
                        turn_node_tile(3 + l, item[2])
                        continue
                    t = item[1]
                    if l == 0:
                        pe.wait_ge(gw_in, 16)
                    else:
                        pe.wait_ge(wb_in, 48)
                    read_out(pe, G[("xT", 3 + l, t)])
                    node_rows(G[item], t, (WA, WB)[l])
                g = G[f"asb{l}"]
                pe.wait_ge(diag_ok, l + 1)
                claim(pe, g)
                for t in range(TT):
                    last = mm(buf(g)[0:P, 128 * t:128 * t + P], MBONES, DG[:, t, :], start=True, stop=True)
                last.then_inc(pe_done, 1)

                weighted_rows(f"gt{l}", f"gv{l}", p_first[2 + l], lambda i: EB[i], PG)

            turn_nodes(5)
            g = G["route"]
            pe.wait_ge(xb_in, 96)
            claim(pe, g)
            for t in range(TT):
                for c in range(KC):
                    last = mm(buf(g)[0:P, 64 * t:64 * t + 36], XT[:, c, t * P:(t + 1) * P], WR[:, c, :], start=c == 0, stop=c == KC - 1)
            last.then_inc(pe_done, 1)
            for item in moe:
                if item == "ct":
                    pe.wait_ge(comb_ok, 1)
                    turn_tiles(G["ct"], lambda t: C3[:, t, :], 3 * EXP)
                    pe.wait_ge(sele_ok, 3)
                    read_out(pe, G["ct"])
                    pe.wait_ge(ctb_ok, 1)
                elif item[0] == "up":
                    m = item[1]
                    pe.wait_ge(w1_in[m % 4], 16 * (m // 4 + 1))
                    w = W1R[:, m % 4, :].rearrange("p (c n) -> p c n", c=KC)
                    wide_rows(G[item], KC, lambda c: w[:, c, :], lambda c: XT[:, c, :])
                else:
                    m = item[1]
                    wide_rows(G[item], 1, lambda c: SELE[:, 128 * m:128 * (m + 1)], lambda c: CTB)
            all_read_out(pe, G[("cb", XC - 1)])
            pe.wait_ge(w2_in, 48)
            for t in range(TT):
                g = G["y"] + t
                claim(pe, g)
                for m in range(XC + 1):
                    for s in range(2):
                        o = buf(g)[0:P, 512 * s:512 * s + HALF]
                        if m < XC:
                            mm(o, HS[:, m, t * P:(t + 1) * P], W2[:, m, HALF * s:HALF * (s + 1)], start=m == 0, stop=False)
                        else:
                            last = mm(o, CT[:, t * P:(t + 1) * P], B2[:, HALF * s:HALF * (s + 1)], start=False, stop=True)
                last.then_inc(pe_done, 1)

        @block.scalar
        def _(act):
            steps = [0]

            def evac(g, dst, src):
                ready(act, g)
                act.activation(dst, src, ACT.Copy).then_inc(copied[g % NPS], 1)

            def evac_tile(i, t):
                g = G[("xT", i, t)]
                evac(g, XT[:, :, t * P:(t + 1) * P], buf(g)[:, 0:128 * KC].rearrange("p (c n) -> p c n", c=KC)[:, :, 0:P])

            def apply_norm(name, t):
                k = norm_no[(name, t)]
                c = k % NCOL
                act.wait_ge(rstd_ok, k + 1)
                act.activation(XN[:, t, :], XRES[:, t, :], ACT.Identity, bias=NMR[:, c:c + 1],
                               scale=RSTD[:, c:c + 1]).then_inc(feat, 1)

            def evac_h(l, t):
                g = G[(("h", l), t)]
                evac(g, split(NODE[:, t, :]), halves(buf(g)))

            for l in range(2):
                for t in range(TT + 1):
                    if l == 0 and t < TT:
                        apply_norm("x", t)
                    if t:
                        evac_tile(l, t - 1)
                if l == 0:
                    act.activation(NMX[:, 0, 0:1], IDENT[:, 0:1], ACT.Copy).then_inc(zt_copied, 2)
                    with act.Fori(0, ET // BODY) as g:
                        for r in range(BODY):
                            act.wait_ge(lg_done, BODY * g + r + RING - 1)
                            for half in range(2):
                                act.wait_ge(zt_done, 2 * BODY * g + 2 * r + half + 1)
                                act.activation(ZT[r % 2][:, 3 * half:3 * half + 3, :],
                                               DB[0][:, 0:384].rearrange("p (c n) -> p c n", c=3)[:, :, 0:P],
                                               ACT.Copy).then_inc(zt_copied, 1)
                H = LH[l]

                def expm(i):
                    act.wait_ge(min_ok, TT * l + i + 1)
                    act.activation(MN[:, i % 2, :], MN[:, i % 2, :], ACT.Exp).then_inc(expm_ok, 1)

                if l == 1:
                    for i in range(TT + 7):
                        if i < TT:
                            act.wait_ge(negmax, TT + i + 1)
                            j, n = col(i)
                            act.activation(TC[i], TC[i], ACT.Exp, bias=NMX[:, j, n:n + 1]).then_inc(exped, 1)
                        if 0 <= i - 1 < TT:
                            if i - 1 >= 2:
                                ready(act, G[("pv1", i - 3)])
                            g = G[("pt1", i - 1)]
                            evac(g, PT[(i - 1) % 2], tiles(buf(g), P))
                        if 0 <= i - 4 < TT:
                            expm(i - 4)
                        if 0 <= i - 6 < TT:
                            apply_norm("ffn", i - 6)
                        if 0 <= i - 7 < TT:
                            evac_tile(2, i - 7)
                    continue

                def evac_head(k):
                    if k >= 2:
                        act.wait_ge(pv_done, k - 1)
                    g = G["pt0"] + k
                    evac(g, PT[k % 2], tiles(buf(g), P))

                for i in range(TT):
                    act.wait_ge(negmax, i + 1)
                    for h in range(H):
                        view = TB[i % 2].rearrange("p (n h) -> p h n", h=H)[:, h, :]
                        act.activation(view, view, ACT.Exp, bias=NMX[:, i % 2, h:h + 1]).then_inc(exped, 1)
                        if h >= 2:
                            evac_head(H * i + h - 2)
                    for h in range(H - 2, H):
                        evac_head(H * i + h)
                    if i >= 1:
                        expm(i - 1)
                expm(TT - 1)

            act.wait_ge(bn_ok, 1)
            for h in range(PH):
                g = G["q"] + h
                ready(act, g)
                act.activation(nodes(QT[:, h, :]), tiles(buf(g)), ACT.Identity, bias=BNB[:, h:h + 1],
                               scale=BNA[:, h:h + 1]).then_inc(copied[g % NPS], 1)
            for item in sched:
                g = G[item]
                if item[0] == "sc":
                    if item[1] >= 2:
                        act.wait_ge(sc_used, item[1] - 1)
                    evac(g, SC[item[1] % 2].rearrange("p (a n) -> p a n", a=2),
                         buf(g)[0:P, :].rearrange("p (a n) -> p a n", a=2)[:, :, 0:400])
                elif item[0] == "z" and item[1] % 2 == 0:
                    m = item[1] // 2
                    if m >= 2:
                        read_out(act, G[("z", 2 * (m - 2) + 1)])
                    ready(act, g)
                    act.activation(nodes(SIL[m % 2]), tiles(buf(g)), ACT.Silu).then_inc(copied[g % NPS], 1)
                elif item[0] == "oha":
                    _, t, half = item
                    if t:
                        act.wait_ge(pe_done, G[("pick", t - 1, 2 * half + 1)] + 1)
                    evac(g, OHAT[half], buf(g)[:, :].rearrange("p (j n) -> p j n", j=8)[:, :, 0:P])
            evac(G["xd"], nodes(XDT), tiles(buf(G["xd"]), HK))
            for pair in range(2):
                g = G["peer"] + 2 * pair
                ready(act, g)
                read_out(act, G[("z", 13 + 2 * pair)])
                act.activation(nodes(SIL[pair][0:88, :]), tiles(buf(g), 88), ACT.Silu).then_inc(copied[g % NPS], 1)
            act.wait_ge(kgate, 1)
            act.activation(GAT, GAT, ACT.Exp).then_inc(kexp, 1)

            for l in range(2):
                for t in range(TT + 2):
                    if l == 0 and t < TT:
                        apply_norm("gat", t)
                    if 0 <= t - 1 < TT:
                        evac_tile(3 + l, t - 1)
                    if 0 <= t - 2 < TT:
                        evac_h(l, t - 2)
                g = G[f"asb{l}"]
                evac(g, nodes(ASB), tiles(buf(g), P))
                for i in range(TT + 1):
                    if i < TT:
                        j, n = col(i)
                        act.wait_ge(negmax, TT * (2 + l) + i + 1)
                        act.activation(EB[i], EB[i], ACT.Exp, bias=NMX[:, j, n:n + 1]).then_inc(exped, 1)
                    if i:
                        if i >= 3:
                            ready(act, G[(f"gv{l}", i - 3)])
                        g = G[(f"gt{l}", i - 1)]
                        evac(g, PG[(i - 1) % 2], tiles(buf(g), P))

            for t in range(TT + 1):
                if t < TT:
                    apply_norm("moe", t)
                if t:
                    evac_tile(5, t - 1)

            def hidden(m):
                g = G[("up", m)]
                if m >= 3:
                    read_out(act, G[("cb", m - 3)])
                ready(act, g)
                act.activation(nodes(GT[m % 3]), tiles(buf(g)), ACT.Gelu, bias=B1C[:, m:m + 1]).then_inc(copied[g % NPS], 1)

            for m in range(3):
                hidden(m)
            act.wait_ge(rt_ok, 1)
            act.activation(GV, GV, ACT.Exp).then_inc(rexp, 1)
            act.activation(EV, EV, ACT.Exp).then_inc(rexp, 1)
            evac(G["ct"], nodes(CT), tiles(buf(G["ct"]), 3 * EXP))
            read_out(act, G["ct"])
            act.activation(CTB, CT, ACT.Copy).then_inc(ctb_ok, 1)
            for m in range(3, XC):
                hidden(m)

        @block.vector
        def _(dve):
            steps = [0]

            def link(ins):
                steps[0] += 1
                ins.then_inc(dve_step, 1)
                dve.wait_ge(dve_step, steps[0])

            norms_taken = [0]

            def stats(name, src, t):
                k = norms_taken[0]
                assert norms[k] == (name, t)
                norms_taken[0] += 1
                c = k % NCOL
                for s in range(2):
                    last = dve.bn_stats(STATS[:, 2 * (k % TT) + s, :], src[:, t, HALF * s:HALF * (s + 1)])
                link(last)
                link(dve.bn_aggr(MV[:, k % TT, :], STATS[:, 2 * (k % TT):2 * (k % TT) + 2, :]))
                dve.tensor_scalar(NMU[:, c:c + 1], MV[:, k % TT, 0:1], -1.0, None, ALU.mult)
                dve.tensor_scalar(VARE[:, c:c + 1], MV[:, k % TT, 1:2], EPS, None, ALU.add).then_inc(var_ok, 1)

            for t in range(TT):
                dve.wait_ge(x_in[t], 16)
                stats("x", XRES, t)
            dve.wait_ge(idx_in, 32)
            link(dve.tensor_copy(IDF, IDX))
            link(dve.scalar_tensor_tensor(out=TIF, in0=IDF[:, 1, :], scalar=float(N), in1=IDF[:, 0, :], op0=ALU.mult, op1=ALU.add))
            dve.tensor_copy(TIDX, TIF).then_inc(idx_ok, 1)
            dve.wait_ge(consts, 7)
            dve.tensor_tensor(CXS, IDF[:, 0, :].unsqueeze(2).to_broadcast([P, ET, 113]),
                              IOTF[:, 512:N].unsqueeze(1).to_broadcast([P, ET, 113]), ALU.is_equal)
            dve.tensor_tensor(CXD, IDF[:, 1, :].unsqueeze(2).to_broadcast([P, ET, P]),
                              IOTF[:, 4 * P:N].unsqueeze(1).to_broadcast([P, ET, P]), ALU.is_equal).then_inc(cx_ready, 1)
            dve.wait_ge(cx_ready, 1)
            dve.wait_ge(att_in, 16)
            for c in range(KC):
                last = dve.tensor_scalar(ATT[:, c, :], ATT[:, c, :], ATC[:, c:c + 1], None, ALU.mult)
            link(last)
            IDG = IDF.rearrange("p a (g s) -> p a g s", s=BODY)

            for l in range(2):
                dve.wait_ge(bias_in, 32 * (l + 1))
                for t in range(TT):
                    for k, (dst, b) in enumerate(((NODE, BS), (HACC, BD))):
                        g = G[((("src", "dst")[k], l), t)]
                        ready(dve, g)
                        dve.tensor_tensor(split(dst[:, t, :]), halves(buf(g)), split(b), ALU.add)\
                           .then_inc(copied[g % NPS], 1)
                if l == 0:
                    ready(dve, G["cx"])
                    dve.tensor_copy(CNT[:, 4, 512:N], buf(G["cx"])[0:P, 0:113]).then_inc(copied[G["cx"] % NPS], 1)
                nh = LH[l]

                def copy_logits(row):
                    return dve.tensor_scalar(row.rearrange("p a n -> p (a n)"), DB[0][0:P, 512:512 + RING * nh],
                                             1.0, None, ALU.mult).then_inc(lg_copied, 1)

                if l == 0:
                    dve.memset(OHS[0], 0.0).then_inc(oh_used, 2)
                    dve.wait_ge(oh_used, 2)
                else:
                    dve.wait_ge(atr_in, 16)
                with dve.Fori(0, ET // BODY) as g:
                    for r in range(BODY):
                        if l == 0:
                            dve.wait_ge(oh_used, BODY * g + r + 1)
                            for oh, k in ((OHS, 0), (OHD, 1)):
                                last = dve.tensor_scalar(oh[r % 2], IOTA, IDG[:, k, bass.ds(g, 1), r], None, ALU.is_equal)
                            last.then_inc(oh_ready, 1)
                        s = r % RING
                        dve.wait_ge(gath[s], 32 * EG * l + 64 * g + 32 * (r // RING) + 32)
                        dve.tensor_tensor(U[:, s, :], U[:, s, :], V[:, s, :], ALU.add).then_inc(z_sum, 1)
                        dve.wait_ge(z_sum, ET * l + BODY * g + r + 1)
                        dve.scalar_tensor_tensor(out=U[:, s, :], in0=U[:, s, :], scalar=0.2, in1=U[:, s, :],
                                                 op0=ALU.mult, op1=ALU.max).then_inc(z_ready, 1)
                        if l == 0 and s == 1:
                            dve.wait_ge(lg_done, BODY * g + r - 1 + RING)
                            copy_logits(LGS[:, bass.ds(2 * g + r // RING, 1), 0:RING * nh])
                        if l == 1:
                            dve.wait_ge(z_ready, ET + BODY * g + r + 1)
                            dve.tensor_tensor_reduce(V[:, s, :], U[:, s, :], ATR, 1.0, 0.0, ALU.mult, ALU.add,
                                                     LGD[:, r:r + 1]).then_inc(dotted, 1)
                            if s == RING - 1:
                                dve.wait_ge(dotted, BODY * g + r + 1)
                                dve.tensor_scalar(LGS[:, bass.ds(2 * g + r // RING, 1), 0:RING].rearrange("p a n -> p (a n)"),
                                                  LGD[:, r - s:r + 1], 1.0, None, ALU.mult).then_inc(lg_copied, 1)
                if l == 0:
                    dve.wait_ge(lg_done, ET + RING)
                    copy_logits(LGS[:, EG:EG + 1, 0:RING * nh])
                if l == 0:
                    dve.wait_ge(cnt_done, 1)
                    for i in range(TT):
                        if i < 4:
                            dve.tensor_copy(CNT[:, i, 512:N], cnt_rest(i))
                        last = dve.tensor_copy(CNT[:, i, 0:512], cnt_main(i))
                    last.then_inc(cnt_ok, 1)

                H, HD = LH[l], D // LH[l]

                def elu(i):
                    dve.wait_ge(expm_ok, TT * l + i + 1)
                    if l == 0:
                        link(dve.scalar_tensor_tensor(out=MN[:, i % 2, :], in0=MN[:, i % 2, :], scalar=-1.0,
                                                      in1=XN[:, i, :], op0=ALU.add, op1=ALU.add))
                    else:
                        link(dve.tensor_scalar(MN[:, i % 2, :], MN[:, i % 2, :], -1.0, None, ALU.add))
                    link(dve.scalar_tensor_tensor(out=HACC[:, i, :], in0=HACC[:, i, :], scalar=0.0, in1=MN[:, i % 2, :],
                                                  op0=ALU.max, op1=ALU.add))

                def logit_head(i, h):
                    return TB[i % 2].rearrange("p (n h) -> p h n", h=HEADS)[:, h, :] if l == 0 else TC[i]

                def place(i):
                    return (i % 2, 0) if l == 0 else col(i)

                def weigh(i, lo, hi):
                    j, n = place(i)
                    for h in range(lo, hi):
                        dve.wait_ge(exped, p_first[l] + H * i + h + 1)
                        view = logit_head(i, h)
                        dve.tensor_tensor_reduce(view, view, CNT[:, i, :], 1.0, 0.0, ALU.mult, ALU.add,
                                                 DEN[:, j, n + h:n + h + 1]).then_inc(p_ready, 1)

                def peak(i):
                    j, n = place(i)
                    if l == 0:
                        dve.wait_ge(tb_in[i % 2], 16 * (i // 2 + 1))
                        src = TB[i % 2].rearrange("p (n h) -> p h n", h=H)
                    else:
                        dve.wait_ge(tc_in[i], 16)
                        src = TC[i]
                    link(dve.tensor_reduce(MX[:, j, n:n + H], src, AX, ALU.max))
                    dve.tensor_scalar(NMX[:, j, n:n + H], MX[:, j, n:n + H], -1.0, None, ALU.mult).then_inc(negmax, 1)

                def out_rows(i):
                    j, n = place(i)
                    dve.wait_ge(p_ready, p_first[l] + H * (i + 1))
                    link(dve.tensor_scalar(RDEN[:, 0:H], DEN[:, j, n:n + H], 1.0, None, ALU.max))
                    link(dve.reciprocal(RDEN[:, 0:H], RDEN[:, 0:H]))
                    if l == 0:
                        dve.wait_ge(pv_done, H * (i + 1))
                        for s in range(2):
                            o = HACC[:, i, HALF * s:HALF * (s + 1)].rearrange("p (h d) -> p h d", h=4)
                            src = ACC[0:P, 512 * s:512 * s + HALF].rearrange("p (h d) -> p h d", h=4)
                            last = dve.tensor_tensor(o, src, RDEN[:, 4 * s:4 * s + 4].unsqueeze(2).to_broadcast([P, 4, HD]), ALU.mult)
                        last.then_inc(acc_free, 1)
                        dve.wait_ge(acc_free, i + 1)
                    else:
                        g = G[("pv1", i)]
                        ready(dve, g)
                        dve.tensor_scalar(split(HACC[:, i, :]), halves(buf(g)), RDEN[:, 0:1], None, ALU.mult)\
                           .then_inc(copied[g % NPS], 1)
                        read_out(dve, g)
                    dve.tensor_scalar(MN[:, i % 2, :], HACC[:, i, :], 0.0, None, ALU.min).then_inc(min_ok, 1)

                def affine(i):
                    k = norm_no[(f"ln{l}", i)]
                    c = k % NCOL
                    dve.wait_ge(lnp_in, 32 * (l + 1))
                    dve.wait_ge(rstd_ok, k + 1)
                    link(dve.scalar_tensor_tensor(out=HACC[:, i, :], in0=HACC[:, i, :], scalar=NMU[:, c:c + 1], in1=LNW,
                                                  op0=ALU.add, op1=ALU.mult))
                    last = dve.scalar_tensor_tensor(out=XN[:, i, :] if l == 0 else HACC[:, i, :], in0=HACC[:, i, :],
                                                    scalar=RSTD[:, c:c + 1], in1=LNB, op0=ALU.mult, op1=ALU.add)
                    if l == 0:
                        last.then_inc(feat, 1)
                    else:
                        link(last)
                        link(dve.tensor_tensor(XRES[:, i, :], XRES[:, i, :], HACC[:, i, :], ALU.add))

                dve.wait_ge(rows_out, 32 * TT * (l + 1))
                if l == 0:
                    peak(0)
                    for i in range(TT):
                        weigh(i, 0, 2)
                        if i >= 2:
                            elu(i - 2)
                        if i >= 1:
                            out_rows(i - 1)
                        weigh(i, 2, 6)
                        if i + 1 < TT:
                            peak(i + 1)
                        weigh(i, 6, 8)
                        if i >= 2:
                            stats("ln0", HACC, i - 2)
                    affine(0)
                    elu(TT - 2)
                    out_rows(TT - 1)
                    stats("ln0", HACC, TT - 2)
                    affine(1)
                    affine(2)
                    elu(TT - 1)
                    stats("ln0", HACC, TT - 1)
                    affine(3)
                    affine(4)
                else:
                    for i in range(TT + 5):
                        if i < TT:
                            peak(i)
                        if 0 <= i - 1 < TT:
                            weigh(i - 1, 0, 1)
                        if 0 <= i - 3 < TT:
                            out_rows(i - 3)
                        if 0 <= i - 4 < TT:
                            elu(i - 4)
                            stats("ln1", HACC, i - 4)
                        if 0 <= i - 5 < TT:
                            affine(i - 5)
                            stats("ffn", XRES, i - 5)
            dve.wait_ge(feat, 3 * TT)
            link(dve.tensor_reduce(SX, XN, AX, ALU.add))
            dve.wait_ge(bn_in, 16 * 5)
            dve.tensor_scalar(BNR, BNV[:, 4, :], EPS, None, ALU.add).then_inc(bnv_ok, 1)
            dve.wait_ge(bnr_ok, 1)
            link(dve.tensor_tensor(BNA, BNA, BNV[:, 1, :], ALU.mult))
            link(dve.tensor_tensor(BNB, BNV[:, 0, :], BNV[:, 3, :], ALU.subtract))
            link(dve.tensor_tensor(BNB, BNB, BNA, ALU.mult))
            dve.tensor_tensor(BNB, BNB, BNV[:, 2, :], ALU.add).then_inc(bn_ok, 1)

            def pick(g, t, q):
                ready(dve, g)
                prod = SELP.rearrange("p (k v b) -> p k v b", k=16, v=2)
                dve.tensor_tensor(prod, buf(g)[0:P, :].rearrange("p (k v b) -> p k v b", k=16, v=2),
                                       OHB[:, 16 * q:16 * q + 16, :].unsqueeze(2).to_broadcast([P, 16, 2, 32]), ALU.mult)\
                   .then_inc(copied[g % NPS], 1)
                read_out(dve, g)
                dve.tensor_reduce(WDC[:, t, 16 * q:16 * q + 16], prod[:, :, 0, :], AX, ALU.add)
                link(dve.tensor_reduce(WUC[:, t, 16 * q:16 * q + 16], prod[:, :, 1, :], AX, ALU.add))

            def add_down(t):
                g = G[("down", t)]
                ready(dve, g)
                dve.tensor_tensor(split(XRES[:, t, :]), halves(buf(g)), split(XRES[:, t, :]), ALU.add)\
                   .then_inc(copied[g % NPS], 1)

            for item in sched:
                g = G[item]
                if item[0] == "sc":
                    t, h = divmod(item[1], PH)
                    s = SC[item[1] % 2]
                    read_out(dve, g)
                    v = V16[:, t, KNN * h:KNN * (h + 1)]
                    k = IDXK[:, KNN * h:KNN * (h + 1)]
                    link(dve.max(v[:, 0:8], s))
                    dve.max_index(k[:, 0:8], v[:, 0:8], s)
                    link(dve.match_replace(WK, v[:, 0:8], s, -3.0e38))
                    link(dve.max(v[:, 8:16], WK))
                    dve.max_index(k[:, 8:16], v[:, 8:16], WK).then_inc(sc_used, 1)
                    dve.wait_ge(sc_used, item[1] + 1)
                    if h == PH - 1:
                        dve.tensor_scalar(IDA, IDXK, 5, None, ALU.logical_shift_right)
                        link(dve.tensor_scalar(IDB, IDXK, 31, None, ALU.bitwise_and))
                        iota = IO32.unsqueeze(1).to_broadcast([P, HK, 32])
                        link(dve.tensor_copy(IDKF[:, 0, :], IDA))
                        if t:
                            ready(dve, G[("oha", t - 1, 1)])
                        dve.tensor_tensor(OHA, IDKF[:, 0, :].unsqueeze(2).to_broadcast([P, HK, 32]), iota, ALU.is_equal)\
                           .then_inc(oha_ok, 1)
                        dve.wait_ge(oha_ok, t + 1)
                        link(dve.tensor_copy(IDKF[:, 0, :], IDB))
                        link(dve.tensor_tensor(OHB, IDKF[:, 0, :].unsqueeze(2).to_broadcast([P, HK, 32]), iota, ALU.is_equal))
                elif item[0] == "z" and item[1] % 2 == 1:
                    m = item[1] // 2
                    ready(dve, g)
                    read_out(dve, G[("z", item[1] - 1)])
                    dve.tensor_tensor(nodes(GS[:, m, :]), nodes(SIL[m % 2]), tiles(buf(g)), ALU.mult)\
                       .then_inc(copied[g % NPS], 1)
                elif item[0] == "pick":
                    pick(g, item[1], item[2])
                elif item[0] == "down":
                    add_down(item[1])
            for t in range(TT):
                last = dve.tensor_scalar(XDV[:, t, :], WDC[:, t, :], SX[:, t:t + 1], None, ALU.mult)
            last.then_inc(xd_ok, 1)
            v4 = V16.rearrange("p t (h k) -> p (t h) k", h=PH)
            g4 = GAT.rearrange("p t (h k) -> p (t h) k", h=PH)
            km, ks = KM.rearrange("p t h -> p (t h)"), KS.rearrange("p t h -> p (t h)")
            link(dve.tensor_reduce(km, v4, AX, ALU.max))
            dve.tensor_tensor(g4, v4, km.unsqueeze(2).to_broadcast([P, TT * PH, KNN]), ALU.subtract).then_inc(kgate, 1)
            for t in range(TT):
                last = dve.tensor_tensor(CNT[:, t, t * P:(t + 1) * P], CNT[:, t, t * P:(t + 1) * P], IDENT, ALU.add)
            link(last)
            dve.tensor_scalar(MB, CNT, 0.0, NEG, ALU.is_equal, ALU.mult)
            link(dve.memset(MBONES, 1.0))
            add_down(2)
            add_down(3)
            for pair in range(2):
                g = G["peer"] + 2 * pair + 1
                ready(dve, g)
                read_out(dve, g - 1)
                dve.tensor_tensor(nodes(ZG[:, pair, :]), nodes(SIL[pair][0:88, :]), tiles(buf(g), 88), ALU.mult)\
                   .then_inc(copied[g % NPS], 1)
            dve.wait_ge(kexp, 1)
            link(dve.tensor_reduce(ks, g4, AX, ALU.add))
            link(dve.reciprocal(ks, ks))
            link(dve.tensor_tensor(g4, g4, ks.unsqueeze(2).to_broadcast([P, TT * PH, KNN]), ALU.mult))
            link(dve.tensor_tensor(GAT, GAT, WUC, ALU.mult))
            add_down(4)
            g = G["peer_out"]
            ready(dve, g)
            dve.tensor_tensor(GAT, GAT, buf(g)[0:P, 0:TT * HK].rearrange("p (t k) -> p t k", t=TT), ALU.mult)\
               .then_inc(copied[g % NPS], 1)
            read_out(dve, g)
            link(dve.tensor_reduce(CMB, GAT, AX, ALU.add))
            for t in range(TT):
                last = dve.tensor_scalar(XRES[:, t, :], XRES[:, t, :], CMB[:, t:t + 1], None, ALU.add)
                link(last)
                stats("gat", XRES, t)
            for l in range(2):
                dve.wait_ge(gb_in, 96)
                att_s, att_d, bias = GB[3 * l:3 * l + 3]
                for t in range(TT):
                    read_out(dve, G[(("h", l), t)])
                    link(dve.tensor_tensor_reduce(JUNK, NODE[:, t, :], att_s, 1.0, 0.0, ALU.mult, ALU.add, AS[:, t:t + 1]))
                    link(dve.tensor_tensor_reduce(JUNK, NODE[:, t, :], att_d, 1.0, 0.0, ALU.mult, ALU.add, AD[:, t:t + 1]))
                for t in range(TT):
                    last = dve.tensor_scalar(DG[:, t, :], IDENT, AS[:, t:t + 1], None, ALU.mult)
                last.then_inc(diag_ok, 1)
                read_out(dve, G[f"asb{l}"])

                def edge_logits(i):
                    e = EB[i]
                    j, n = col(i)
                    link(dve.tensor_scalar(e, ASB, AD[:, i:i + 1], None, ALU.add))
                    link(dve.scalar_tensor_tensor(out=e, in0=e, scalar=0.2, in1=e, op0=ALU.mult, op1=ALU.max))
                    link(dve.tensor_tensor(e, e, MB[:, i, :], ALU.add))
                    link(dve.tensor_reduce(MX[:, j, n:n + 1], e, AX, ALU.max))
                    dve.tensor_scalar(NMX[:, j, n:n + 1], MX[:, j, n:n + 1], -1.0, None, ALU.mult).then_inc(negmax, 1)

                def edge_weights(i):
                    e = EB[i]
                    j, n = col(i)
                    dve.wait_ge(exped, p_first[2 + l] + i + 1)
                    dve.tensor_tensor_reduce(e, e, CNT[:, i, :], 1.0, 0.0, ALU.mult, ALU.add, DEN[:, j, n:n + 1]).then_inc(p_ready, 1)

                def node_out(i):
                    j, n = col(i)
                    dve.wait_ge(p_ready, p_first[2 + l] + i + 1)
                    link(dve.reciprocal(RDEN[:, 0:1], DEN[:, j, n:n + 1]))
                    g = G[(f"gv{l}", i)]
                    ready(dve, g)
                    dve.scalar_tensor_tensor(out=split(HACC[:, i, :]), in0=halves(buf(g)), scalar=RDEN[:, 0:1], in1=split(bias),
                                             op0=ALU.mult, op1=ALU.add).then_inc(copied[g % NPS], 1)
                    read_out(dve, g)
                    if l == 0:
                        dve.tensor_scalar(XN[:, i, :], HACC[:, i, :], 0.0, None, ALU.max).then_inc(feat, 1)
                    else:
                        link(dve.tensor_tensor(XRES[:, i, :], XRES[:, i, :], HACC[:, i, :], ALU.add))
                        stats("moe", XRES, i)

                for i in range(TT + 3):
                    if i < TT:
                        edge_logits(i)
                    if 0 <= i - 1 < TT:
                        edge_weights(i - 1)
                    if 0 <= i - 3 < TT:
                        node_out(i - 3)
            g = G["route"]
            ready(dve, g)
            dve.tensor_tensor(RT, buf(g)[0:P, 0:64 * TT].rearrange("p (t n) -> p t n", t=TT)[:, :, 0:36],
                                   BR.unsqueeze(1).to_broadcast([P, TT, 36]), ALU.add).then_inc(copied[g % NPS], 1)
            read_out(dve, g)
            dve.memset(RG, NEG)
            dve.memset(RE, NEG)
            dve.memset(REPG, NEG)
            link(dve.memset(REPE, NEG))
            glog = RT[:, :, 0:4]
            elog = RT[:, :, 4:36].rearrange("p t (g e) -> p t g e", g=4)
            dve.tensor_copy(RG[:, :, 0:4], glog)
            for t in range(TT):
                last = dve.tensor_copy(RE[:, 4 * t:4 * t + 4, 0:8], elog[:, t, :, :])
            link(last)
            for t in range(TT):
                dve.max(TOPG[:, t, :], RG[:, t, :])
            for j in range(4 * TT):
                last = dve.max(TOPE[:, j, :], RE[:, j, :])
            link(last)
            dve.tensor_copy(REPG[:, :, 0:2], TOPG[:, :, 0:2])
            link(dve.tensor_copy(REPE[:, :, 0:2], TOPE[:, :, 0:2]))
            for t in range(TT):
                dve.match_replace(RGO[:, t, :], REPG[:, t, :], RG[:, t, :], 3.0e38)
            for j in range(4 * TT):
                dve.match_replace(REO[:, j, :], REPE[:, j, :], RE[:, j, :], 3.0e38)
            dve.tensor_tensor(GV, RG[:, :, 0:4], TOPG[:, :, 0:1].to_broadcast([P, TT, 4]), ALU.subtract)
            link(dve.tensor_tensor(EV, RE[:, :, 0:8], TOPE[:, :, 0:1].to_broadcast([P, 4 * TT, 8]), ALU.subtract))
            dve.tensor_scalar(RGO[:, :, 0:4], RGO[:, :, 0:4], 3.0e38, None, ALU.is_equal)
            dve.tensor_scalar(REO[:, :, 0:8], REO[:, :, 0:8], 3.0e38, None, ALU.is_equal).then_inc(rt_ok, 1)
            dve.wait_ge(rexp, 2)
            dve.tensor_tensor(GV, GV, RGO[:, :, 0:4], ALU.mult)
            link(dve.tensor_tensor(EV, EV, REO[:, :, 0:8], ALU.mult))
            dve.tensor_reduce(GSM, GV, AX, ALU.add)
            link(dve.tensor_reduce(ESM, EV, AX, ALU.add))
            dve.reciprocal(GSM, GSM)
            link(dve.reciprocal(ESM, ESM))
            link(dve.tensor_tensor(GV, GV, GSM.unsqueeze(2).to_broadcast([P, TT, 4]), ALU.mult))
            gflat = GV.rearrange("p t g -> p (t g)")
            link(dve.tensor_tensor(ESM, ESM, gflat, ALU.mult))
            link(dve.tensor_tensor(COMB.rearrange("p t (g e) -> p (t g) e", g=4), EV,
                                   ESM.unsqueeze(2).to_broadcast([P, 4 * TT, 8]), ALU.mult))
            for k in range(3):
                link(dve.tensor_copy(CPB, COMB))
                last = dve.tensor_copy(C3[:, :, EXP * k:EXP * (k + 1)], CPB)
                if k < 2:
                    link(last)
                    link(dve.tensor_tensor(COMB, COMB, C3[:, :, EXP * k:EXP * (k + 1)], ALU.subtract))
            last.then_inc(comb_ok, 1)
            for m in range(XC):
                g = G[("cb", m)]
                ready(dve, g)
                read_out(dve, G[("up", m)])
                dve.tensor_tensor(nodes(HS[:, m, :]), nodes(GT[m % 3]), tiles(buf(g)), ALU.mult)\
                   .then_inc(copied[g % NPS], 1)
            for t in range(TT):
                g = G["y"] + t
                ready(dve, g)
                dve.tensor_tensor(split(XRES[:, t, :]), halves(buf(g)), split(XRES[:, t, :]), ALU.add)\
                   .then_inc(copied[g % NPS], 1)


def _layout(i):
    c = np.ascontiguousarray
    col = lambda v, k: c(v.reshape(k, 128).T)
    r = {n: i[n] for n in ("x", "src", "dst")}
    for n in ("W1s", "b1s", "W1d", "b1d", "ln1_w", "ln1_b", "Wos", "bos", "Wod", "bod", "lno_w", "lno_b"):
        r[n] = i["L0_gnn_" + n]
    r["attn1"], r["attno"] = col(i["L0_gnn_attn1"].reshape(-1), 6), i["L0_gnn_attno"].reshape(-1)
    f = "L0_ffn_"
    r["wqT"] = c(i[f + "wq"].T)
    for n in ("bq", "bn_gamma", "bn_beta", "bn_mean", "bn_var"):
        r[n] = col(i[f + n], 4)
    r["keysT"] = c(i[f + "keys"].transpose(0, 2, 1))
    r["w_down"], r["w_up"] = i[f + "w_down_tab"], i[f + "w_up_tab"]
    for n in ("a_w1", "a_w2", "a_w3", "s_w1", "s_w2", "s_w3"):
        r[n + "T"] = c(i[f + n].T)
    f = "L1_gnn_"
    for n, m in (("G1", "W1"), ("as1", "att_src1"), ("ad1", "att_dst1"), ("gb1", "b1"),
                 ("G2", "W2"), ("as2", "att_src2"), ("ad2", "att_dst2"), ("gb2", "b2")):
        r[n] = i[f + m]
    f = "L1_ffn_"
    wr = np.concatenate([i[f + "Wg"], i[f + "Wge"].transpose(1, 0, 2).reshape(768, 32)], axis=1)
    r["Wr"] = c(wr.reshape(6, 128, 36).transpose(1, 0, 2).reshape(128, 216))
    r["br"] = np.concatenate([i[f + "bg"], i[f + "bge"].reshape(-1)])
    r["W1c"] = c(i[f + "W1"].transpose(1, 0, 2).reshape(768, 3072))
    r["b1c"] = col(i[f + "b1"].reshape(-1), 24)
    r["W2"] = i[f + "W2"].reshape(3072, 768)
    r["b2"] = i[f + "b2"]
    return r


def kernel(**inputs):
    import concourse.bacc as _bacc
    from concourse.bass_utils import run_bass_kernel_spmd as _run

    nc = _bacc.Bacc("TRN2", target_bir_lowering=False, num_devices=1)
    arrays, args = {}, {}
    for name, v in _layout({k: np.asarray(v) for k, v in inputs.items()}).items():
        v = np.ascontiguousarray(v)
        if v.dtype == np.int32:
            v = v.view(np.uint32)
        arrays["in_" + name] = v
        args[name] = nc.dram_tensor("in_" + name, v.shape, mybir.dt.from_np(v.dtype), kind="ExternalInput").ap()
    out = nc.dram_tensor("out_0", (N, D), F32, kind="ExternalOutput").ap()
    emit(nc, args, out)
    r = _run(nc, [arrays], core_ids=[0])
    return r.results[0]["out_0"]
```

```python
from contextlib import ExitStack

import numpy as np
import concourse.bass as bass
from concourse import mybir

F32 = mybir.dt.float32
BF16 = mybir.dt.bfloat16
FP16 = mybir.dt.float16
F32R = mybir.dt.float32r
U32 = mybir.dt.uint32
ALU = mybir.AluOpType
ACT = mybir.ActivationFunctionType
AX = mybir.AxisListType.X

N, E, D = 625, 10000, 768
P = 125
TT = N // P
ET = E // P
KC = D // 128
HALF = D // 2
RING = 5
EG = ET // RING
BODY = 2 * RING
LAG = (10, 5)
HEADS = 8
TROWS = 128 * 3052
FILLW = 1526
KNN, PH, NKEY = 16, 4, 800
HK = PH * KNN
HIDA = 44
EXP, MH = 32, 96
XH = EXP * MH
XC = XH // 128
NEG = -1.0e30
EPS = 1e-5
NCOL = 10
CUT = 314
NPS = 3


def emit(nc, a, out):
    ctx = ExitStack()
    with ctx:
        def overlay(name, off, n, dtype):
            with nc.sbuf_tensor(f"{name}_before", [128, off], F32):
                with nc.sbuf_tensor(name, [128, n], dtype) as t:
                    return t

        def over3(name, off, x, y, dtype=F32R):
            return overlay(name, off, x * y, dtype)[:, :].rearrange("p (x y) -> p x y", x=x)

        HSH, HSL = over3("hidden_high", 11520, XC, N), over3("hidden_low", 11520 + XC * N, XC, N)
        XHP, XLP = overlay("x_high_part", 41520, KC * N + 2, F32R), overlay("x_low_part", 7680, KC * N + 2, F32R)
        XTH, XTL = (t[:, 0:KC * N].rearrange("p (c n) -> p c n", c=KC) for t in (XHP, XLP))
        XTS = over3("x_whole", 7680, KC, N, F32)
        GT = over3("hidden_whole", 3840, 2, N, F32)
        B1C = overlay("hidden_bias", 51981, XC, F32)
        WRAW = [overlay(f"w_raw{i}", o, D, F32)[:, :] for i, o in enumerate((45272, 46040, 5720, 6488))]
        WHI = [overlay(f"w_high_part{i}", 46808 + D * i, D, F32R)[:, :] for i in range(2)]
        WLO = [overlay(f"w_low_part{i}", 48344 + D * i, D, F32R)[:, :] for i in range(2)]
        arena = ctx.enter_context(nc.sbuf_tensor("arena", [128, 52900], F32))
        DB = [ctx.enter_context(nc.psum_tensor(f"DB{i}", [128, 1024], F32)) for i in range(4)]
        ACC = DB[3]

        def sem(name):
            return ctx.enter_context(nc.semaphore(name))

        def at(off, n, p=128):
            return arena[0:p, off:off + n]

        def at3(off, x, y, p=128):
            return arena[0:p, off:off + x * y].rearrange("p (x y) -> p x y", x=x)

        XRES = at3(0, TT, D, P)
        XN = at3(3840, TT, D, P)
        XT = at3(7680, KC, N)
        CNT = at3(11520, TT, N, P)
        NODE = at3(14720, TT, D, P)
        HACC = at3(18560, TT, D, P)
        WA = at3(22400, KC, D)
        WB = at3(27008, KC, D)
        BS, BD, LNW, LNB = (at(31616 + D * i, D, P) for i in range(4))
        PT = [at3(34688 + N * i, TT, P, P) for i in range(2)]
        LGS = at3(35938, EG + 1, RING * HEADS, P)
        TB = [at(36640 + 5000 * i, 5000, P) for i in range(2)]
        TC = [at(36640 + N * i, N, P) for i in range(TT)]
        U = at3(36640, RING, D, P)
        V = at3(36640 + RING * D, RING, D, P)
        ZT = [at3(44320 + 750 * i, KC, P) for i in range(2)]
        OHS = [arena[0:P, 46640 + 313 * i:46640 + 313 * (i + 1)].bitcast(BF16)[:, 0:N] for i in range(2)]
        OHD = [arena[0:P, 47266 + 313 * i:47266 + 313 * (i + 1)].bitcast(BF16)[:, 0:N] for i in range(2)]
        IOTA = arena[0:P, 34688:34688 + 313].bitcast(FP16)[:, 0:N]
        IOTF = at(18560, N, P)
        CXS = arena[0:P, 36640:36640 + 4520].bitcast(BF16).rearrange("p (t n) -> p t n", t=ET)
        CXD = arena[0:P, 41160:41160 + 5000].bitcast(BF16).rearrange("p (t n) -> p t n", t=ET)
        MN = at3(46640, 2, D, P)
        FILL = at(48176, FILLW)
        ATR = at(48176, D, P)
        LGD = at(48176 + D, BODY, P)
        ATT = at3(49702, KC, HEADS)
        ATC = at(49750, KC)
        IDX = arena[0:P, 49760:49920].bitcast(U32).rearrange("p (a t) -> p a t", a=2)
        TIDX = arena[0:P, 49920:50000].bitcast(U32)
        IDF = at3(50000, 2, ET, P)
        TIF = at(50160, ET, P)
        ZERO = arena[0:P, 50250:50570].bitcast(BF16)
        WQ = at3(22400, KC, PH * 128)
        SW2 = at3(25472, 8, D)
        KEYS = at3(14720, PH, NKEY)
        SIL = [at(17920, N), at(51083, N)]
        OHB = at3(18560, HK, 32, P)
        V16, XDV, GAT, WDC, WUC = (at3(20608 + 320 * i, TT, HK, P) for i in range(5))
        GS = at3(31616, 8, N)
        SWR = at3(36616, 8, D)
        SC = [at(42760 + NKEY * i, NKEY, P) for i in range(2)]
        WK = at(44360, NKEY, P)
        OHA = at3(45160, HK, 32, P)
        OHAT = [at3(47208 + 1000 * i, 8, P) for i in range(2)]
        ZG = at3(49208, 2, N, 88)
        XDT = at(50458, N, HK)
        A1 = at(51708, 176, HK)
        A3 = at(51884, 176, HK)
        A2 = at3(52060, 2, HK, 88)
        TBL = at3(52188, 4, 64)
        QT = at3(3840, PH, N)
        SELP = at(6340, 1024, P)
        IDXK = arena[0:P, 7364:7428].bitcast(U32)
        IDA = arena[0:P, 7428:7492].bitcast(U32)
        IDB = arena[0:P, 7492:7556].bitcast(U32)
        IDKF = at3(7556, 1, HK, P)
        BNV = at3(52826, 5, PH)
        BNA = at(52846, PH)
        BNB = at(52850, PH)
        GB = [at(31616 + D * i, D, P) for i in range(6)]
        ASB = at(36224, N, P)
        G1 = at3(36616, KC, D)
        EB = [at(27008 + N * i, N, P) for i in range(TT)]
        PG = [at3(30133 + N * i, TT, P, P) for i in range(2)]
        DG = at3(44500, TT, P, P)
        MB = at3(41224, TT, N, P)
        SELE = arena[0:3 * EXP, 49880:49880 + XH // 2].bitcast(BF16)
        CTB = arena[0:3 * EXP, 51416:51729].bitcast(BF16)[:, 0:N]
        C3 = at3(5720, TT, 3 * EXP, P)
        CPB = arena[0:P, 7400:7480].bitcast(BF16).rearrange("p (t e) -> p t e", t=TT)
        B2 = at(41520, D, 3 * EXP)
        CT = at(5090, N, 3 * EXP)
        RT = at3(5720, TT, 36, P)
        RG = at3(5900, TT, 12, P)
        RE = at3(5960, TT * 4, 14, P)
        RGO = at3(6240, TT, 12, P)
        REO = at3(6300, TT * 4, 14, P)
        TOPG = at3(6580, TT, 8, P)
        TOPE = at3(6620, TT * 4, 8, P)
        REPG = at3(6780, TT, 8, P)
        REPE = at3(6820, TT * 4, 8, P)
        GV = at3(6980, TT, 4, P)
        EV = at3(7000, TT * 4, 8, P)
        GSM = at(7160, TT, P)
        ESM = at(7165, TT * 4, P)
        COMB = at3(7185, TT, EXP, P)
        BR = at(51945, 36, P)
        ZEROS = arena[0:P, 52010:52330].bitcast(BF16)
        WR = at3(51729, KC, 36)
        IDENT = at(52444, P, P)
        IO32 = at(52570, 32, P)
        STATS = at3(52602, TT * 2, 6, P)
        MV = at3(52662, TT, 2, P)
        MX = at3(52810, 2, HEADS, P)
        NMX = at3(52686, 2, HEADS, P)
        DEN = at3(52702, 2, HEADS, P)
        RDEN = at(52718, HEADS, P)
        SX = at(52726, TT, P)
        CMB = at(52731, TT, P)
        AS = at(52736, TT, P)
        AD = at(52741, TT, P)
        KM = at3(52746, TT, PH, P)
        KS = at3(52766, TT, PH, P)
        VARE, NMU, RSTD, NMR = (at(52856 + NCOL * i, NCOL, P) for i in range(4))
        EXPN = at(52794, 6)
        BNR = at(52800, PH)
        ONES = at(44360, P, P)

        FS = [nc.dram_tensor(f"src_rows{l}", (N, D), F32, kind="Internal").ap() for l in range(2)]
        FD = [nc.dram_tensor(f"dst_rows{l}", (N, D), F32, kind="Internal").ap() for l in range(2)]
        LT = [nc.dram_tensor(f"logits{l}", (TROWS, h), F32, kind="Internal").ap() for l, h in enumerate((HEADS, 1))]

        pe_done = sem("pe_done")
        copied = [sem(f"copied{i}") for i in range(NPS)]
        acc_free = sem("acc_free")
        dve_step, act_step, pool_step = sem("dve_step"), sem("act_step"), sem("pool_step")
        x_in, idx_in = [sem(f"x_in{t}") for t in range(TT)], sem("idx_in")
        wa_in, wb_in, bias_in, lnp_in, att_in = sem("wa_in"), sem("wb_in"), sem("bias_in"), sem("lnp_in"), sem("att_in")
        filled, filled_thin = sem("filled"), sem("filled_thin")
        consts = sem("consts")
        var_ok, rstd_ok = sem("var_ok"), sem("rstd_ok")
        bnv_ok, bnr_ok = sem("bnv_ok"), sem("bnr_ok")
        idx_ok = sem("idx_ok")
        atr_in, dotted = sem("atr_in"), sem("dotted")
        oh_ready, oh_used = sem("oh_ready"), sem("oh_used")
        cx_ready = sem("cx_ready")
        cnt_done, cnt_ok = sem("cnt_done"), sem("cnt_ok")
        feat = sem("feat")
        rows_out = sem("rows_out")
        gath = [sem(f"gath{r}") for r in range(RING)]
        z_sum, z_ready = sem("z_sum"), sem("z_ready")
        zt_done, zt_copied = sem("zt_done"), sem("zt_copied")
        lg_done, lg_copied = sem("lg_done"), sem("lg_copied")
        scattered = sem("scattered")
        tb_in = [sem("tb_in0"), sem("tb_in1")]
        tc_in = [sem(f"tc_in{i}") for i in range(TT)]
        negmax, exped, p_ready, pv_done = (sem(s) for s in ("negmax", "exped", "p_ready", "pv_done"))
        min_ok, expm_ok = sem("min_ok"), sem("expm_ok")
        bn_in, ffn_in, keys_in, sw2_in, peer_in = sem("bn_in"), sem("ffn_in"), sem("keys_in"), sem("sw2_in"), sem("peer_in")
        swr_in = [sem(f"swr_in{i}") for i in range(4)]
        tbl_ok = sem("tbl_ok")
        sc_used, oha_ok = sem("sc_used"), sem("oha_ok")
        kgate, kexp = sem("kgate"), sem("kexp")
        xd_ok, bn_ok = sem("xd_ok"), sem("bn_ok")
        gw_in, gb_in = [sem("gw_in0"), sem("gw_in1")], sem("gb_in")
        diag_ok = sem("diag_ok")
        w_in = [sem(f"w_in{i}") for i in range(4)]
        b2_in, xb_in = sem("b2_in"), sem("xb_in")
        x_high, x_low = sem("x_high"), sem("x_low")
        w_high, w_low = sem("w_high"), sem("w_low")
        zeros_ok = sem("zeros_ok")
        h_high, h_low = sem("h_high"), sem("h_low")
        chunk_done, y_ready = sem("chunk_done"), sem("y_ready")
        sele_ok, rt_ok, rexp, comb_ok, ctb_ok = (sem(s) for s in ("sele_ok", "rt_ok", "rexp", "comb_ok", "ctb_ok"))
        y_added, y_out = sem("y_added"), sem("y_out")
        out_v = out.rearrange("(t p) d -> p t d", p=P)

        G, ngroups = {}, [0]

        def take(name, count):
            G[name] = ngroups[0]
            ngroups[0] += count

        def take_weights(turned, rows):
            for i in range(TT):
                take((turned, i), 1)
                if i:
                    take((rows, i - 1), 1)
            take((rows, TT - 1), 1)

        def rows_order(i, names):
            order = [("xT", i, 0)]
            for t in range(TT):
                if t + 1 < TT:
                    order.append(("xT", i, t + 1))
                order += [(name, t) for name in names]
            return order

        def take_all(order):
            for item in order:
                take(item, 1)

        proj_order = [rows_order(l, (("src", l), ("dst", l))) for l in range(2)]
        h_order = [rows_order(3 + l, (("h", l),)) for l in range(2)]
        for l in range(2):
            take_all(proj_order[l])
            if l == 0:
                take("cx", 1)
                take("pt0", TT * HEADS)
            else:
                take_weights("pt1", "pv1")
        take_all([("xT", 2, t) for t in range(TT)])
        take("q", PH)
        sched = []
        for t in range(TT):
            for h in range(PH):
                s = t * PH + h
                sched.append(("sc", s))
                if s < 16:
                    sched.append(("z", s))
            if t == TT - 1:
                sched += [("down", 0), ("down", 1)]
            sched += [("oha", t, 0), ("oha", t, 1)] + [("pick", t, q) for q in range(4)]
        take_all(sched)
        take_all([("down", 2), "xd", ("down", 3)])
        take("peer", 4)
        take_all([("down", 4), "peer_out"])
        for l in range(2):
            take_all(h_order[l])
            take(f"asb{l}", 1)
            take_weights(f"gt{l}", f"gv{l}")
        take_all([("xT", 5, t) for t in range(TT)])
        take("route", 1)
        moe = [("up", m) for m in range(3)] + ["ct"]
        for m in range(XC):
            if m >= 3:
                moe.append(("up", m))
            moe.append(("cb", m))
        take_all(moe)

        norms = [("x", t) for t in range(TT)] + [("ln0", t) for t in range(TT)]
        for t in range(TT):
            norms += [("ln1", t)] + ([("ffn", t - 1)] if t else [])
        norms += [("ffn", TT - 1)] + [("gat", t) for t in range(TT)] + [("moe", t) for t in range(TT)]
        norm_no = {name: k for k, name in enumerate(norms)}

        def buf(g):
            return DB[g % NPS]

        def halves(b):
            return b[0:P, :].rearrange("p (a n) -> p a n", a=2)[:, :, 0:HALF]

        def split(ap):
            return ap.rearrange("p (a n) -> p a n", a=2)

        def tiles(b, p=128):
            return b[0:p, 0:640].rearrange("p (t n) -> p t n", t=TT)[:, :, 0:P]

        def nodes(ap):
            return ap.rearrange("p (t n) -> p t n", t=TT)

        def ready(eng, g):
            eng.wait_ge(pe_done, g + 1)

        def read_out(eng, g):
            eng.wait_ge(copied[g % NPS], g // NPS + 1)

        def all_read_out(eng, last):
            for g in range(last - NPS + 1, last + 1):
                read_out(eng, g)

        def wraw(n):
            if n < XC:
                return n % 2, n // 2
            j, place = (n - XC) // 4, (2, 3, 0, 1)[n % 4]
            return place, j if place >= 2 else XC // 2 + j

        def across(b, p=128):
            return b[0:p, 512 - CUT:512 - CUT + N]

        def y_parts(t):
            rest = DB[2 + (t + 2) // 4] if t < 4 else DB[3]
            lo = (512, 768, 0, 256, 512)[t]
            return DB[t // 2][0:P, 512 * (t % 2):512 * (t % 2) + 512], rest[0:P, lo:lo + 256]

        def col(i):
            return i % 2, i // 2

        def claim(pe, g):
            if g >= NPS:
                pe.wait_ge(copied[g % NPS], g // NPS)

        def claim_acc(pe, n):
            if n:
                pe.wait_ge(acc_free, n)

        LH = (HEADS, 1)
        p_first = [TT * n for n in (0, HEADS, HEADS + 1, HEADS + 2)]

        def cnt_main(i):
            return DB[1 + i // 2][0:P, 512 * (i % 2):512 * (i % 2) + 512] if i < 4 else DB[3][0:P, 0:512]

        def cnt_rest(i):
            return DB[3][0:P, 512 + 113 * i:512 + 113 * (i + 1)]

        block = ctx.enter_context(nc.Block())

        @block.sync
        def _(sp):
            def rows(w):
                return w.rearrange("(c p) n -> p c n", p=128)

            def bcast(v):
                return v.rearrange("(o n) -> o n", o=1).broadcast_to([P, v.shape[0]])

            for t in range(TT):
                sp.dma_start(XRES[:, t, :], a["x"][t * P:(t + 1) * P, :]).then_inc(x_in[t], 16)
            sp.dma_start(IDX[:, 0, :], a["src"].rearrange("(p t) -> p t", p=P)).then_inc(idx_in, 16)
            sp.dma_start(IDX[:, 1, :], a["dst"].rearrange("(p t) -> p t", p=P)).then_inc(idx_in, 16)
            sp.dma_start(WA, rows(a["W1s"])).then_inc(wa_in, 16)
            sp.dma_start(WB, rows(a["W1d"])).then_inc(wb_in, 16)
            sp.dma_start(BS, bcast(a["b1s"])).then_inc(bias_in, 16)
            sp.dma_start(BD, bcast(a["b1d"])).then_inc(bias_in, 16)
            sp.dma_start(LNW, bcast(a["ln1_w"])).then_inc(lnp_in, 16)
            sp.dma_start(LNB, bcast(a["ln1_b"])).then_inc(lnp_in, 16)
            sp.dma_start(ATC, a["attn1"]).then_inc(att_in, 16)
            sp.wait_ge(consts, 1)
            wide = LT[0].rearrange("(p n) h -> p (n h)", p=128).rearrange("p (a n) -> p a n", a=16)
            sp.dma_start(wide, FILL.unsqueeze(1).to_broadcast([128, 16, FILLW])).then_inc(filled, 16)
            for l in range(2):
                for t in range(TT):
                    read_out(sp, G[(("src", l), t)])
                    read_out(sp, G[(("dst", l), t)])
                    sp.dma_start(FS[l][t * P:(t + 1) * P, :], NODE[:, t, :]).then_inc(rows_out, 16)
                    sp.dma_start(FD[l][t * P:(t + 1) * P, :], HACC[:, t, :]).then_inc(rows_out, 16)
                if l == 0:
                    chunks = [(w[:, c, :], rows(a[name])[:, c, :], s) for w, name, s in ((WA, "Wos", wa_in), (WB, "Wod", wb_in))
                              for c in range(KC)]
                else:
                    chunks = [(WQ[:, c, :], rows(a["wqT"])[:, c, :], ffn_in) for c in range(KC)]
                    chunks += [(SW2[:, c, :], rows(a["s_w2T"])[:, c, :], sw2_in) for c in range(8)]
                if l == 0:
                    thin = LT[1].rearrange("(p n) h -> p (n h)", p=128).rearrange("p (a n) -> p a n", a=2)
                    sp.wait_ge(lg_copied, 2)
                    sp.dma_start(thin, FILL.unsqueeze(1).to_broadcast([128, 2, FILLW])).then_inc(filled_thin, 16)
                for n, (place, source, loaded) in enumerate(chunks):
                    sp.wait_ge(lg_copied, n + 2 if l == 0 else EG + 1 + RING * (n + 1))
                    sp.dma_start(place, source).then_inc(loaded, 16)
                if l == 0:
                    sp.wait_ge(filled, 16)
                    sp.wait_ge(filled_thin, 16)
                    sp.dma_start(ATR, bcast(a["attno"])).then_inc(atr_in, 16)
                    sp.dma_start(BS, bcast(a["bos"])).then_inc(bias_in, 16)
                    sp.dma_start(BD, bcast(a["bod"])).then_inc(bias_in, 16)
                sp.wait_ge(scattered, 16 * ET * (l + 1))
                for i in range(TT):
                    if l == 0 and i >= 2:
                        sp.wait_ge(pe_done, G["pt0"] + HEADS * (i - 1))
                    table = LT[l][i * P * N:(i + 1) * P * N, :].rearrange("(p n) h -> p (n h)", p=P)
                    if l == 0:
                        sp.dma_start(TB[i % 2], table).then_inc(tb_in[i % 2], 16)
                    else:
                        sp.dma_start(TC[i], table).then_inc(tc_in[i], 16)
                if l == 0:
                    sp.wait_ge(feat, 2 * TT)
                    sp.dma_start(LNW, bcast(a["lno_w"])).then_inc(lnp_in, 16)
                    sp.dma_start(LNB, bcast(a["lno_b"])).then_inc(lnp_in, 16)
            sp.wait_ge(feat, 3 * TT)
            sp.dma_start(KEYS, a["keysT"].rearrange("h k n -> k h n")).then_inc(keys_in, 16)
            for v, name in enumerate(("bq", "bn_gamma", "bn_beta", "bn_mean", "bn_var")):
                sp.dma_start(BNV[:, v, :], a[name]).then_inc(bn_in, 16)
            sw = [a["s_w1T"], a["s_w3T"]]
            for z in range(16):
                m, which = z // 2, z % 2
                if z >= 8:
                    sp.wait_ge(pe_done, G[("z", 2 * (m - 4) + 1)] + 1)
                sp.dma_start(SWR[:, 2 * (m % 4) + which, :].rearrange("p (c n) -> p c n", c=KC),
                             rows(sw[which])[:, :, m * 128:(m + 1) * 128]).then_inc(swr_in[m % 4], 16)
                if z == 7:
                    sp.wait_ge(tbl_ok, 1)
                    for g in range(PH):
                        for v, name in enumerate(("w_down", "w_up")):
                            sp.dma_start(TBL[32 * g:32 * g + 25, g, 32 * v:32 * v + 32],
                                         a[name].rearrange("(x y) o -> x (y o)", y=32)).then_inc(peer_in, 16)
                        sp.dma_start(A1[KNN * g:KNN * (g + 1), HIDA * g:HIDA * (g + 1)], a["a_w1T"]).then_inc(peer_in, 16)
                        sp.dma_start(A3[KNN * g:KNN * (g + 1), HIDA * g:HIDA * (g + 1)], a["a_w3T"]).then_inc(peer_in, 16)
                        sp.dma_start(A2[HIDA * (g % 2):HIDA * (g % 2 + 1), g // 2, KNN * g:KNN * (g + 1)],
                                     a["a_w2T"]).then_inc(peer_in, 16)
            sp.wait_ge(pe_done, G[("z", 15)] + 1)
            sp.dma_start(G1, rows(a["G1"])).then_inc(gw_in[0], 16)
            sp.wait_ge(feat, 3 * TT + 1)
            sp.dma_start(WA, rows(a["G2"])).then_inc(gw_in[1], 16)
            for i, name in enumerate(("as1", "ad1", "gb1", "as2", "ad2", "gb2")):
                sp.dma_start(GB[i], bcast(a[name])).then_inc(gb_in, 16)
            sp.dma_start(WR, a["Wr"].rearrange("p (c n) -> p c n", c=KC)).then_inc(xb_in, 16)
            sp.dma_start(BR, bcast(a["br"])).then_inc(xb_in, 16)
            sp.dma_start(B1C[:, :], a["b1c"]).then_inc(xb_in, 16)
            for n in range(2 * XC):
                place, turn = wraw(n)
                if n == XC:
                    ready(sp, G["ct"])
                    sp.wait_ge(comb_ok, 1)
                if n == XC + 6:
                    ready(sp, G[("up", XC - 1)])
                    for k in range(3):
                        sp.dma_start(B2[EXP * k:EXP * (k + 1), :], a["b2"]).then_inc(b2_in, 16)
                if turn:
                    sp.wait_ge(w_low, n - (2 if n < XC else 4) + 1)
                if n < XC:
                    sp.dma_start(WRAW[place].rearrange("p (c n) -> p c n", c=KC),
                                 rows(a["W1c"])[:, :, n * 128:(n + 1) * 128]).then_inc(w_in[place], 16)
                else:
                    m = n - XC
                    sp.dma_start(WRAW[place], a["W2"][m * 128:(m + 1) * 128, :]).then_inc(w_in[place], 16)
            for t in range(TT):
                sp.wait_ge(y_added, t + 1)
                sp.dma_start(out_v[:, t, :], XRES[:, t, :]).then_inc(y_out, 16)
            sp.wait_ge(y_out, 16 * TT)

        @block.gpsimd
        def _(pool):
            steps = [0]

            def link(ins):
                steps[0] += 1
                ins.then_inc(pool_step, 1)
                pool.wait_ge(pool_step, steps[0])

            pool.memset(FILL, NEG).then_inc(consts, 1)
            pool.iota(IOTF, [[1, N]], base=0, channel_multiplier=0, allow_small_or_imprecise_dtypes=True).then_inc(consts, 1)
            pool.iota(IOTA, [[1, N]], base=0, channel_multiplier=0, allow_small_or_imprecise_dtypes=True).then_inc(consts, 1)
            pool.memset(ZERO, 0.0).then_inc(consts, 1)
            link(pool.memset(IDENT, 0.0))
            pool.affine_select(out=IDENT, in_=IDENT, compare_op=ALU.not_equal, fill=1.0, base=0,
                               pattern=[[-1, P]], channel_multiplier=1).then_inc(consts, 1)
            pool.iota(IO32, [[1, 32]], base=0, channel_multiplier=0, allow_small_or_imprecise_dtypes=True).then_inc(consts, 1)
            link(pool.memset(ATT, 1.0))
            link(pool.affine_select(out=ATT, in_=ATT, compare_op=ALU.is_ge, fill=0.0, base=0,
                                    pattern=[[128, KC], [-D // HEADS, HEADS]], channel_multiplier=1))
            pool.affine_select(out=ATT, in_=ATT, compare_op=ALU.is_ge, fill=0.0, base=D // HEADS - 1,
                               pattern=[[-128, KC], [D // HEADS, HEADS]], channel_multiplier=-1).then_inc(consts, 1)
            def rsqrt_var(name):
                for k in [k for k, (n, t) in enumerate(norms) if n in name]:
                    c = k % NCOL
                    pool.wait_ge(var_ok, k + 1)
                    link(pool.tensor_tensor(RSTD[:, c:c + 1], VARE[:, c:c + 1], EXPN[0:P, 0:1], ALU.pow))
                    pool.tensor_tensor(NMR[:, c:c + 1], NMU[:, c:c + 1], RSTD[:, c:c + 1], ALU.mult).then_inc(rstd_ok, 1)

            link(pool.memset(EXPN, -0.5))
            rsqrt_var(("x",))
            pool.wait_ge(idx_ok, 1)
            pool.wait_ge(filled, 16)

            for l in range(2):
                pool.wait_ge(rows_out, 32 * TT * (l + 1))
                if l == 0:
                    pool.wait_ge(pe_done, G["cx"] + 1)

                if l == 1:
                    pool.wait_ge(filled_thin, 16)
                lag = LAG[l]

                def scatter(t):
                    pool.wait_ge(lg_copied, t // RING + 2 if l == 0 else EG + 1 + t + 1)
                    if ET * l + t:
                        pool.wait_ge(scattered, 16 * (ET * l + t))
                    pool.indirect_dma_start(
                        out=LT[l], out_offset=bass.IndirectOffsetOnAxis(ap=TIDX[:, t:t + 1], axis=0),
                        in_=LGS[:, t // RING + 1 - l, LH[l] * (t % RING):LH[l] * (t % RING + 1)], in_offset=None,
                    ).then_inc(scattered, 16)

                for t in range(ET):
                    r = t % RING
                    if t >= lag:
                        scatter(t - lag)
                    if t >= RING and l == 0:
                        pool.wait_ge(zt_done, 2 * (t - RING + 1))
                    if t >= RING and l == 1:
                        pool.wait_ge(dotted, t - RING + 1)
                    for table, k, dst in ((FS[l], 0, U), (FD[l], 1, V)):
                        pool.indirect_dma_start(
                            out=dst[:, r, :], out_offset=None, in_=table,
                            in_offset=bass.IndirectOffsetOnAxis(ap=IDX[:, k, t:t + 1], axis=0)).then_inc(gath[r], 16)
                for t in range(ET - lag, ET):
                    scatter(t)
                rsqrt_var((("ln0",), ("ln1", "ffn"))[l])
            pool.wait_ge(feat, 3 * TT)
            pool.memset(at(51708, 736), 0.0).then_inc(tbl_ok, 1)
            pool.wait_ge(tbl_ok, 1)
            pool.wait_ge(bnv_ok, 1)
            pool.tensor_tensor(BNA, BNR, EXPN[:, 0:PH], ALU.pow).then_inc(bnr_ok, 1)
            rsqrt_var(("gat",))
            pool.wait_ge(feat, 4 * TT)
            link(pool.memset(SELE, 1.0))
            for k in range(3):
                part = SELE[EXP * k:EXP * (k + 1), :]
                link(pool.affine_select(out=part, in_=part, compare_op=ALU.is_ge, fill=0.0, base=0,
                                        pattern=[[1, XH]], channel_multiplier=-MH))
                pool.affine_select(out=part, in_=part, compare_op=ALU.is_ge, fill=0.0, base=MH - 1,
                                   pattern=[[-1, XH]], channel_multiplier=MH).then_inc(sele_ok, 1)
            pool.wait_ge(sele_ok, 3)
            rsqrt_var(("moe",))

        @block.tensor
        def _(pe):
            mm = nc.tensor.matmul

            def turn_node_tile(i, t):
                pe.wait_ge(feat, TT * i + t + 1)
                g = G[("xT", i, t)]
                claim(pe, g)
                for c in range(KC):
                    last = nc.tensor.transpose(buf(g)[:, 128 * c:128 * c + P], XN[:, t, 128 * c:128 * (c + 1)], IDENT)
                last.then_inc(pe_done, 1)

            def turn_nodes(i):
                for t in range(TT):
                    turn_node_tile(i, t)
                all_read_out(pe, G[("xT", i, TT - 1)])

            def node_rows(g, t, w):
                claim(pe, g)
                for c in range(KC):
                    for s in range(2):
                        last = mm(buf(g)[0:P, 512 * s:512 * s + HALF], XT[:, c, t * P:(t + 1) * P],
                                  w[:, c, HALF * s:HALF * (s + 1)], start=c == 0, stop=c == KC - 1)
                last.then_inc(pe_done, 1)

            def wide_rows(g, chunks, lhs, rhs, m=128):
                claim(pe, g)
                for c in range(chunks):
                    for lo, hi, at0 in ((0, 4, 0), (4, 5, 512)):
                        o = buf(g)[0:m, at0:at0 + 128 * (hi - lo)].rearrange("p (t n) -> p t n", n=128)[:, :, 0:P]
                        last = mm(o, lhs(c), rhs(c)[:, lo * P:hi * P], start=c == 0, stop=c == chunks - 1)
                last.then_inc(pe_done, 1)

            def turn_tiles(g, src, p=P):
                claim(pe, g)
                for t in range(TT):
                    last = nc.tensor.transpose(buf(g)[0:p, 128 * t:128 * t + P], src(t), IDENT)
                last.then_inc(pe_done, 1)

            def weighted_rows(turned, rows, first, weights, slots):
                def turn_weights(i):
                    pe.wait_ge(p_ready, first + i + 1)
                    turn_tiles(G[(turned, i)], lambda t: weights(i)[:, t * P:(t + 1) * P])

                turn_weights(0)
                for i in range(TT):
                    if i + 1 < TT:
                        turn_weights(i + 1)
                    read_out(pe, G[(turned, i)])
                    g = G[(rows, i)]
                    claim(pe, g)
                    for s in range(2):
                        for j in range(TT):
                            last = mm(buf(g)[0:P, 512 * s:512 * s + HALF], slots[i % 2][:, j, :],
                                      NODE[:, j, HALF * s:HALF * (s + 1)], start=j == 0, stop=j == TT - 1)
                    last.then_inc(pe_done, 1)

            counts = [(cnt_main(i), i, 0, 512) for i in range(TT)] + [(cnt_rest(i), i, 512, N) for i in range(4)]
            banks = [DB[1][0:P, 0:512], DB[1][0:P, 512:1024], DB[2][0:P, 0:512], DB[2][0:P, 512:1024],
                     DB[3][0:P, 0:512], DB[3][0:P, 512:1024]]

            pe.wait_ge(consts, 4)
            for l in range(2):
                for item in proj_order[l]:
                    if item[0] == "xT":
                        turn_node_tile(l, item[2])
                        continue
                    (side, _), t = item
                    if side == "src":
                        pe.wait_ge(wa_in, 16 * (1 + KC * l))
                        read_out(pe, G[("xT", l, t)])
                    else:
                        pe.wait_ge(wb_in, 16 * (1 + KC * l))
                    node_rows(G[item], t, WA if side == "src" else WB)
                if l == 0:
                    claim(pe, G["cx"])
                    pe.wait_ge(cx_ready, 1)
                    for t in range(ET):
                        last = mm(buf(G["cx"])[0:P, 0:113], CXD[:, t, :], CXS[:, t, :], start=t == 0, stop=t == ET - 1)
                    last.then_inc(pe_done, 1)
                if l == 0:
                    all_read_out(pe, G["cx"])
                    for b in banks:
                        mm(b, ZERO[:, 0:P], ZERO[:, 0:512], start=True, stop=False)
                    nh = HEADS
                    zps = DB[0][:, 0:384].rearrange("p (c n) -> p c n", c=3)
                    mm(DB[0][0:P, 512:512 + RING * nh], IDENT, XN[:, 0, 0:RING * nh], start=True, stop=True).then_inc(lg_done, RING)
                    with pe.Fori(0, ET // BODY) as g:
                        def count(r, some):
                            for o, i, lo, hi in some:
                                last = mm(o, OHD[r % 2][:, i * P:(i + 1) * P], OHS[r % 2][:, lo:hi], start=False, stop=False)
                            return last

                        def turn(r, half):
                            pe.wait_ge(zt_copied, 2 * BODY * g + 2 * r + half + 2)
                            for c in range(3):
                                f = 128 * (3 * half + c)
                                last = nc.tensor.transpose(zps[:, c, 0:P], U[:, r % RING, f:f + 128], IDENT)
                            last.then_inc(zt_done, 1)

                        def logits(r):
                            pe.wait_ge(zt_copied, 2 * BODY * g + 2 * r + 4)
                            if r % RING == 0:
                                pe.wait_ge(lg_copied, 2 * g + r // RING + 1)
                            for c in range(KC):
                                o = 512 + nh * (r % RING)
                                last = mm(DB[0][0:P, o:o + nh], ZT[r % 2][:, c, :], ATT[:, c, :], start=c == 0, stop=c == KC - 1)
                            last.then_inc(lg_done, 1)

                        for r in range(BODY):
                            pe.wait_ge(z_ready, BODY * g + r + 1)
                            turn(r, 0)
                            pe.wait_ge(oh_ready, BODY * g + r + 1)
                            count(r, counts[:3])
                            if r:
                                logits(r - 1)
                            turn(r, 1)
                            count(r, counts[3:]).then_inc(oh_used, 1)
                        logits(BODY - 1)
                    for b in banks:
                        last = mm(b, ZERO[:, 0:P], ZERO[:, 0:512], start=False, stop=True)
                    last.then_inc(cnt_done, 1)
                    pe.wait_ge(cnt_ok, 1)
                    pe.wait_ge(lg_copied, EG + 1)

                if l == 1:
                    weighted_rows("pt1", "pv1", p_first[1], lambda i: TC[i], PT)
                    continue
                HD = D // HEADS
                heads = [(i, h) for i in range(TT) for h in range(HEADS)]

                def turn_head(k):
                    i, h = heads[k]
                    pe.wait_ge(p_ready, k + 1)
                    view = TB[i % 2].rearrange("p (n h) -> p h n", h=HEADS)[:, h, :]
                    turn_tiles(G["pt0"] + k, lambda t: view[:, t * P:(t + 1) * P])

                turn_head(0)
                for k, (i, h) in enumerate(heads):
                    if k + 1 < len(heads):
                        turn_head(k + 1)
                    read_out(pe, G["pt0"] + k)
                    if h == 0:
                        claim_acc(pe, i)
                    o, f = 512 * (h // 4) + HD * (h % 4), h * HD
                    for j in range(TT):
                        last = mm(ACC[0:P, o:o + HD], PT[k % 2][:, j, :], NODE[:, j, f:f + HD], start=j == 0, stop=j == TT - 1)
                    last.then_inc(pv_done, 1)

            turn_nodes(2)
            pe.wait_ge(ffn_in, 16 * KC)
            for h in range(PH):
                wide_rows(G["q"] + h, KC, lambda c: WQ[:, c, h * 128:(h + 1) * 128], lambda c: XT[:, c, :])
            all_read_out(pe, G["q"] + PH - 1)
            pe.wait_ge(keys_in, 16)

            def down(t):
                if t == 0:
                    for m in range(8):
                        read_out(pe, G[("z", 2 * m + 1)])
                    pe.wait_ge(sw2_in, 16 * 8)
                g = G[("down", t)]
                claim(pe, g)
                for m in range(8):
                    for s in range(2):
                        last = mm(buf(g)[0:P, 512 * s:512 * s + HALF], GS[:, m, t * P:(t + 1) * P],
                                  SW2[:, m, HALF * s:HALF * (s + 1)], start=m == 0, stop=m == 7)
                last.then_inc(pe_done, 1)

            for item in sched:
                g = G[item]
                if item[0] == "sc":
                    t, h = divmod(item[1], PH)
                    claim(pe, g)
                    for s in range(2):
                        last = mm(buf(g)[0:P, 512 * s:512 * s + 400], QT[:, h, t * P:(t + 1) * P],
                                  KEYS[:, h, 400 * s:400 * (s + 1)], start=True, stop=True)
                    last.then_inc(pe_done, 1)
                elif item[0] == "z":
                    m, which = divmod(item[1], 2)
                    pe.wait_ge(swr_in[m % 4], 32 * (m // 4 + 1))
                    w = SWR[:, 2 * (m % 4) + which, :].rearrange("p (c n) -> p c n", c=KC)
                    wide_rows(g, KC, lambda c: w[:, c, :], lambda c: XT[:, c, :])
                elif item[0] == "oha":
                    _, t, half = item
                    pe.wait_ge(oha_ok, t + 1)
                    claim(pe, g)
                    for j in range(8):
                        k = 8 * half + j
                        last = nc.tensor.transpose(buf(g)[:, 128 * j:128 * j + P],
                                                   OHA[:, 4 * k:4 * k + 4, :].rearrange("p a b -> p (a b)"), IDENT)
                    last.then_inc(pe_done, 1)
                elif item[0] == "pick":
                    _, t, q = item
                    read_out(pe, G[("oha", t, q // 2)])
                    pe.wait_ge(peer_in, 16 * 20)
                    claim(pe, g)
                    for j in range(4):
                        k = 4 * q + j
                        last = mm(buf(g)[0:P, 256 * j:256 * (j + 1)], OHAT[k // 8][:, k % 8, :],
                                  TBL.rearrange("p a b -> p (a b)"), start=True, stop=True)
                    last.then_inc(pe_done, 1)
                else:
                    down(item[1])
            down(2)
            pe.wait_ge(xd_ok, 1)
            turn_tiles(G["xd"], lambda t: XDV[:, t, :], HK)
            down(3)
            read_out(pe, G["xd"])
            for pair in range(2):
                for which, w in enumerate((A1, A3)):
                    wide_rows(G["peer"] + 2 * pair + which, 1, lambda c: w[:, 88 * pair:88 * (pair + 1)], lambda c: XDT, 88)
            down(4)
            g = G["peer_out"]
            claim(pe, g)
            for pair in range(2):
                read_out(pe, G["peer"] + 2 * pair + 1)
            for t in range(TT):
                for pair in range(2):
                    last = mm(buf(g)[0:P, HK * t:HK * (t + 1)], ZG[:, pair, t * P:(t + 1) * P], A2[:, pair, :],
                              start=pair == 0, stop=pair == 1)
            last.then_inc(pe_done, 1)

            for l in range(2):
                for item in h_order[l]:
                    if item[0] == "xT":
                        turn_node_tile(3 + l, item[2])
                        continue
                    t = item[1]
                    pe.wait_ge(gw_in[l], 16)
                    read_out(pe, G[("xT", 3 + l, t)])
                    node_rows(G[item], t, (G1, WA)[l])
                g = G[f"asb{l}"]
                pe.wait_ge(diag_ok, TT * (l + 1))
                claim(pe, g)
                for t in range(TT):
                    last = mm(buf(g)[0:P, 128 * t:128 * t + P], ONES, DG[:, t, :], start=True, stop=True)
                last.then_inc(pe_done, 1)

                weighted_rows(f"gt{l}", f"gv{l}", p_first[2 + l], lambda i: EB[i], PG)

            turn_nodes(5)
            g = G["route"]
            pe.wait_ge(xb_in, 48)
            claim(pe, g)
            for t in range(TT):
                for c in range(KC):
                    last = mm(buf(g)[0:P, 64 * t:64 * t + 36], XTS[:, c, t * P:(t + 1) * P], WR[:, c, :], start=c == 0, stop=c == KC - 1)
            last.then_inc(pe_done, 1)
            for item in moe:
                if item == "ct":
                    pe.wait_ge(comb_ok, 1)
                    turn_tiles(G["ct"], lambda t: C3[:, t, :], 3 * EXP)
                    pe.wait_ge(sele_ok, 3)
                    read_out(pe, G["ct"])
                    pe.wait_ge(ctb_ok, 1)
                elif item[0] == "up":
                    m = item[1]
                    g = G[item]
                    claim(pe, g)
                    if m == 0:
                        pe.wait_ge(x_high, TT)
                    pe.wait_ge(w_low, m + 1)
                    high, low = (w[m % 2].rearrange("p (c n) -> p c n", c=KC) for w in (WHI, WLO))
                    for c in range(KC):
                        if m == 0:
                            pe.wait_ge(x_low, min(KC, c + 2) + 1)
                        for lo, hi in ((0, CUT), (CUT, N + 1)):
                            o = buf(g)[:, 512 - CUT + lo:512 - CUT + hi]
                            x_high_part, x_low_part = (x[:, N * c + lo:N * c + hi] for x in (XHP, XLP))
                            mm(o, high[:, c, :], x_high_part, start=c == 0, stop=False)
                            mm(o, high[:, c, :], x_low_part, start=False, stop=False)
                            last = mm(o, low[:, c, :], x_high_part, start=False, stop=c == KC - 1)
                    last.then_inc(pe_done, 1)
                else:
                    m = item[1]
                    g = G[item]
                    claim(pe, g)
                    for lo, hi in ((0, CUT), (CUT, N)):
                        last = mm(buf(g)[:, 512 - CUT + lo:512 - CUT + hi], SELE[:, 128 * m:128 * (m + 1)], CTB[:, lo:hi],
                                  start=True, stop=True)
                    last.then_inc(pe_done, 1)
            all_read_out(pe, G[("cb", XC - 1)])
            shared = [DB[2][0:P, 512:1024], DB[3][0:P, 0:512], DB[3][0:P, 512:1024]]
            pe.wait_ge(zeros_ok, 1)
            for b in shared:
                mm(b, ZEROS[:, 0:P], ZEROS[:, 0:512], start=True, stop=False)
            for m in range(XC):
                pe.wait_ge(w_low, XC + m + 1)
                pe.wait_ge(h_low, m + 1)
                for t in range(TT):
                    for o, lo in zip(y_parts(t), (0, 512)):
                        f = slice(lo, lo + o.shape[1])
                        n = slice(t * P, (t + 1) * P)
                        mm(o, HSH[:, m, n], WHI[m % 2][:, f], start=m == 0 and lo == 0, stop=False)
                        mm(o, HSH[:, m, n], WLO[m % 2][:, f], start=False, stop=False)
                        last = mm(o, HSL[:, m, n], WHI[m % 2][:, f], start=False, stop=False)
                    if m == XC - 1:
                        pe.wait_ge(b2_in, 48)
                        for o, lo in zip(y_parts(t), (0, 512)):
                            mm(o, CT[:, n], B2[:, lo:lo + o.shape[1]], start=False, stop=lo == 0)
                        if t in (1, 3, 4):
                            mm(shared[t // 2], ZEROS[:, 0:P], ZEROS[:, 0:512], start=False, stop=True).then_inc(y_ready, 1)
                if m < XC - 1:
                    last.then_inc(chunk_done, 1)

        @block.scalar
        def _(act):
            steps = [0]

            def evac(g, dst, src):
                ready(act, g)
                act.activation(dst, src, ACT.Copy).then_inc(copied[g % NPS], 1)

            def evac_tile(i, t):
                g = G[("xT", i, t)]
                evac(g, (XTS if i == 5 else XT)[:, :, t * P:(t + 1) * P], buf(g)[:, 0:128 * KC].rearrange("p (c n) -> p c n", c=KC)[:, :, 0:P])

            def apply_norm(name, t):
                k = norm_no[(name, t)]
                c = k % NCOL
                act.wait_ge(rstd_ok, k + 1)
                act.activation(XN[:, t, :], XRES[:, t, :], ACT.Identity, bias=NMR[:, c:c + 1],
                               scale=RSTD[:, c:c + 1]).then_inc(feat, 1)

            def evac_h(l, t):
                g = G[(("h", l), t)]
                evac(g, split(NODE[:, t, :]), halves(buf(g)))

            for l in range(2):
                for t in range(TT + 1):
                    if l == 0 and t < TT:
                        apply_norm("x", t)
                    if t:
                        evac_tile(l, t - 1)
                if l == 0:
                    act.activation(NMX[:, 0, 0:1], IDENT[:, 0:1], ACT.Copy).then_inc(zt_copied, 2)
                    with act.Fori(0, ET // BODY) as g:
                        for r in range(BODY):
                            act.wait_ge(lg_done, BODY * g + r + RING - 1)
                            for half in range(2):
                                act.wait_ge(zt_done, 2 * BODY * g + 2 * r + half + 1)
                                act.activation(ZT[r % 2][:, 3 * half:3 * half + 3, :],
                                               DB[0][:, 0:384].rearrange("p (c n) -> p c n", c=3)[:, :, 0:P],
                                               ACT.Copy).then_inc(zt_copied, 1)
                H = LH[l]

                def expm(i):
                    act.wait_ge(min_ok, TT * l + i + 1)
                    act.activation(MN[:, i % 2, :], MN[:, i % 2, :], ACT.Exp).then_inc(expm_ok, 1)

                if l == 1:
                    for i in range(TT + 7):
                        if i < TT:
                            act.wait_ge(negmax, TT + i + 1)
                            j, n = col(i)
                            act.activation(TC[i], TC[i], ACT.Exp, bias=NMX[:, j, n:n + 1]).then_inc(exped, 1)
                        if 0 <= i - 1 < TT:
                            if i - 1 >= 2:
                                ready(act, G[("pv1", i - 3)])
                            g = G[("pt1", i - 1)]
                            evac(g, PT[(i - 1) % 2], tiles(buf(g), P))
                        if 0 <= i - 4 < TT:
                            expm(i - 4)
                        if 0 <= i - 6 < TT:
                            apply_norm("ffn", i - 6)
                        if 0 <= i - 7 < TT:
                            evac_tile(2, i - 7)
                    continue

                def evac_head(k):
                    if k >= 2:
                        act.wait_ge(pv_done, k - 1)
                    g = G["pt0"] + k
                    evac(g, PT[k % 2], tiles(buf(g), P))

                for i in range(TT):
                    act.wait_ge(negmax, i + 1)
                    for h in range(H):
                        view = TB[i % 2].rearrange("p (n h) -> p h n", h=H)[:, h, :]
                        act.activation(view, view, ACT.Exp, bias=NMX[:, i % 2, h:h + 1]).then_inc(exped, 1)
                        if H * i + h >= 2:
                            evac_head(H * i + h - 2)
                        if h == 4 and i:
                            expm(i - 1)
                for k in range(H * TT - 2, H * TT):
                    evac_head(k)
                expm(TT - 1)

            act.wait_ge(bn_ok, 1)
            for h in range(PH):
                g = G["q"] + h
                ready(act, g)
                act.activation(nodes(QT[:, h, :]), tiles(buf(g)), ACT.Identity, bias=BNB[:, h:h + 1],
                               scale=BNA[:, h:h + 1]).then_inc(copied[g % NPS], 1)
            for item in sched:
                g = G[item]
                if item[0] == "sc":
                    if item[1] >= 2:
                        act.wait_ge(sc_used, item[1] - 1)
                    evac(g, SC[item[1] % 2].rearrange("p (a n) -> p a n", a=2),
                         buf(g)[0:P, :].rearrange("p (a n) -> p a n", a=2)[:, :, 0:400])
                elif item[0] == "z" and item[1] % 2 == 0:
                    m = item[1] // 2
                    if m >= 2:
                        read_out(act, G[("z", 2 * (m - 2) + 1)])
                    ready(act, g)
                    act.activation(nodes(SIL[m % 2]), tiles(buf(g)), ACT.Silu).then_inc(copied[g % NPS], 1)
                elif item[0] == "oha":
                    _, t, half = item
                    if t:
                        act.wait_ge(pe_done, G[("pick", t - 1, 2 * half + 1)] + 1)
                    evac(g, OHAT[half], buf(g)[:, :].rearrange("p (j n) -> p j n", j=8)[:, :, 0:P])
            evac(G["xd"], nodes(XDT), tiles(buf(G["xd"]), HK))
            for pair in range(2):
                g = G["peer"] + 2 * pair
                ready(act, g)
                read_out(act, G[("z", 13 + 2 * pair)])
                act.activation(nodes(SIL[pair][0:88, :]), tiles(buf(g), 88), ACT.Silu).then_inc(copied[g % NPS], 1)
            act.wait_ge(kgate, 1)
            act.activation(GAT, GAT, ACT.Exp).then_inc(kexp, 1)

            for l in range(2):
                for t in range(TT + 2):
                    if l == 0 and t < TT:
                        apply_norm("gat", t)
                    if 0 <= t - 1 < TT:
                        evac_tile(3 + l, t - 1)
                    if 0 <= t - 2 < TT:
                        evac_h(l, t - 2)
                g = G[f"asb{l}"]
                evac(g, nodes(ASB), tiles(buf(g), P))
                for i in range(TT + 1):
                    if i < TT:
                        j, n = col(i)
                        act.wait_ge(negmax, TT * (2 + l) + i + 1)
                        act.activation(EB[i], EB[i], ACT.Exp, bias=NMX[:, j, n:n + 1]).then_inc(exped, 1)
                    if i:
                        if i >= 3:
                            ready(act, G[(f"gv{l}", i - 3)])
                        g = G[(f"gt{l}", i - 1)]
                        evac(g, PG[(i - 1) % 2], tiles(buf(g), P))

            def high_weights(n):
                place, turn = wraw(n)
                act.wait_ge(w_in[place], 16 * (turn + 1))
                if 2 <= n < XC + 2:
                    ready(act, G[("up", n - 2)])
                elif n >= XC + 2:
                    act.wait_ge(chunk_done, n - XC - 1)
                act.activation(WHI[n % 2], WRAW[place], ACT.Copy).then_inc(w_high, 1)

            for t in range(TT + 2):
                if t < TT:
                    apply_norm("moe", t)
                if 1 <= t <= TT:
                    evac_tile(5, t - 1)
                if t >= 2:
                    read_out(act, G[("xT", 5, t - 2)])
                    n = slice((t - 2) * P, (t - 1) * P)
                    act.activation(XTH[:, :, n], XTS[:, :, n], ACT.Copy).then_inc(x_high, 1)
            high_weights(0)
            high_weights(1)

            def hidden(m):
                g = G[("up", m)]
                if m >= 2:
                    act.wait_ge(h_low, m - 1)
                ready(act, g)
                act.activation(GT[:, m % 2, :], across(buf(g)), ACT.Gelu, bias=B1C[:, m:m + 1]).then_inc(copied[g % NPS], 1)

            hidden(0)
            high_weights(2)
            act.wait_ge(rt_ok, 1)
            act.activation(GV, GV, ACT.Exp).then_inc(rexp, 1)
            act.activation(EV, EV, ACT.Exp).then_inc(rexp, 1)
            hidden(1)
            high_weights(3)
            evac(G["ct"], nodes(CT), tiles(buf(G["ct"]), 3 * EXP))
            read_out(act, G["ct"])
            act.activation(CTB, CT, ACT.Copy).then_inc(ctb_ok, 1)

            def high_hidden(m):
                read_out(act, G[("cb", m)])
                act.activation(HSH[:, m, :], GT[:, m % 2, :], ACT.Copy).then_inc(h_high, 1)

            high_hidden(0)
            for m in range(2, XC):
                hidden(m)
                high_weights(m + 2)
                if m == 2:
                    high_hidden(1)
                high_hidden(m)
            for n in range(XC + 2, 2 * XC):
                high_weights(n)

        @block.vector
        def _(dve):
            steps = [0]

            def link(ins):
                steps[0] += 1
                ins.then_inc(dve_step, 1)
                dve.wait_ge(dve_step, steps[0])

            norms_taken = [0]

            def stats(name, src, t):
                k = norms_taken[0]
                assert norms[k] == (name, t)
                norms_taken[0] += 1
                c = k % NCOL
                for s in range(2):
                    last = dve.bn_stats(STATS[:, 2 * (k % TT) + s, :], src[:, t, HALF * s:HALF * (s + 1)])
                link(last)
                link(dve.bn_aggr(MV[:, k % TT, :], STATS[:, 2 * (k % TT):2 * (k % TT) + 2, :]))
                dve.tensor_scalar(NMU[:, c:c + 1], MV[:, k % TT, 0:1], -1.0, None, ALU.mult)
                dve.tensor_scalar(VARE[:, c:c + 1], MV[:, k % TT, 1:2], EPS, None, ALU.add).then_inc(var_ok, 1)

            for t in range(TT):
                dve.wait_ge(x_in[t], 16)
                stats("x", XRES, t)
            dve.wait_ge(idx_in, 32)
            link(dve.tensor_copy(IDF, IDX))
            link(dve.scalar_tensor_tensor(out=TIF, in0=IDF[:, 1, :], scalar=float(N), in1=IDF[:, 0, :], op0=ALU.mult, op1=ALU.add))
            dve.tensor_copy(TIDX, TIF).then_inc(idx_ok, 1)
            dve.wait_ge(consts, 7)
            dve.tensor_tensor(CXS, IDF[:, 0, :].unsqueeze(2).to_broadcast([P, ET, 113]),
                              IOTF[:, 512:N].unsqueeze(1).to_broadcast([P, ET, 113]), ALU.is_equal)
            dve.tensor_tensor(CXD, IDF[:, 1, :].unsqueeze(2).to_broadcast([P, ET, P]),
                              IOTF[:, 4 * P:N].unsqueeze(1).to_broadcast([P, ET, P]), ALU.is_equal).then_inc(cx_ready, 1)
            dve.wait_ge(cx_ready, 1)
            dve.wait_ge(att_in, 16)
            for c in range(KC):
                last = dve.tensor_scalar(ATT[:, c, :], ATT[:, c, :], ATC[:, c:c + 1], None, ALU.mult)
            link(last)
            IDG = IDF.rearrange("p a (g s) -> p a g s", s=BODY)

            for l in range(2):
                dve.wait_ge(bias_in, 32 * (l + 1))
                for t in range(TT):
                    for k, (dst, b) in enumerate(((NODE, BS), (HACC, BD))):
                        g = G[((("src", "dst")[k], l), t)]
                        ready(dve, g)
                        dve.tensor_tensor(split(dst[:, t, :]), halves(buf(g)), split(b), ALU.add)\
                           .then_inc(copied[g % NPS], 1)
                if l == 0:
                    ready(dve, G["cx"])
                    dve.tensor_copy(CNT[:, 4, 512:N], buf(G["cx"])[0:P, 0:113]).then_inc(copied[G["cx"] % NPS], 1)
                nh = LH[l]

                def copy_logits(row):
                    return dve.tensor_scalar(row.rearrange("p a n -> p (a n)"), DB[0][0:P, 512:512 + RING * nh],
                                             1.0, None, ALU.mult).then_inc(lg_copied, 1)

                if l == 0:
                    dve.memset(OHS[0], 0.0).then_inc(oh_used, 2)
                    dve.wait_ge(oh_used, 2)
                else:
                    dve.wait_ge(atr_in, 16)
                with dve.Fori(0, ET // BODY) as g:
                    for r in range(BODY):
                        if l == 0:
                            dve.wait_ge(oh_used, BODY * g + r + 1)
                            for oh, k in ((OHS, 0), (OHD, 1)):
                                last = dve.tensor_scalar(oh[r % 2], IOTA, IDG[:, k, bass.ds(g, 1), r], None, ALU.is_equal)
                            last.then_inc(oh_ready, 1)
                        s = r % RING
                        dve.wait_ge(gath[s], 32 * EG * l + 64 * g + 32 * (r // RING) + 32)
                        dve.tensor_tensor(U[:, s, :], U[:, s, :], V[:, s, :], ALU.add).then_inc(z_sum, 1)
                        dve.wait_ge(z_sum, ET * l + BODY * g + r + 1)
                        dve.scalar_tensor_tensor(out=U[:, s, :], in0=U[:, s, :], scalar=0.2, in1=U[:, s, :],
                                                 op0=ALU.mult, op1=ALU.max).then_inc(z_ready, 1)
                        if l == 0 and s == 1:
                            dve.wait_ge(lg_done, BODY * g + r - 1 + RING)
                            copy_logits(LGS[:, bass.ds(2 * g + r // RING, 1), 0:RING * nh])
                        if l == 1:
                            dve.wait_ge(z_ready, ET + BODY * g + r + 1)
                            dve.tensor_tensor_reduce(V[:, s, :], U[:, s, :], ATR, 1.0, 0.0, ALU.mult, ALU.add,
                                                     LGD[:, r:r + 1]).then_inc(dotted, 1)
                            dve.wait_ge(dotted, BODY * g + r + 1)
                            dve.tensor_scalar(LGS[:, bass.ds(2 * g + r // RING, 1), s:s + 1].rearrange("p a n -> p (a n)"),
                                              LGD[:, r:r + 1], 1.0, None, ALU.mult).then_inc(lg_copied, 1)
                if l == 0:
                    dve.wait_ge(lg_done, ET + RING)
                    copy_logits(LGS[:, EG:EG + 1, 0:RING * nh])
                if l == 0:
                    dve.wait_ge(cnt_done, 1)
                    for i in range(TT):
                        if i < 4:
                            dve.tensor_copy(CNT[:, i, 512:N], cnt_rest(i))
                        last = dve.tensor_copy(CNT[:, i, 0:512], cnt_main(i))
                    last.then_inc(cnt_ok, 1)

                H, HD = LH[l], D // LH[l]

                def elu(i):
                    dve.wait_ge(expm_ok, TT * l + i + 1)
                    if l == 0:
                        link(dve.scalar_tensor_tensor(out=MN[:, i % 2, :], in0=MN[:, i % 2, :], scalar=-1.0,
                                                      in1=XN[:, i, :], op0=ALU.add, op1=ALU.add))
                    else:
                        link(dve.tensor_scalar(MN[:, i % 2, :], MN[:, i % 2, :], -1.0, None, ALU.add))
                    link(dve.scalar_tensor_tensor(out=HACC[:, i, :], in0=HACC[:, i, :], scalar=0.0, in1=MN[:, i % 2, :],
                                                  op0=ALU.max, op1=ALU.add))

                def logit_head(i, h):
                    return TB[i % 2].rearrange("p (n h) -> p h n", h=HEADS)[:, h, :] if l == 0 else TC[i]

                def place(i):
                    return (i % 2, 0) if l == 0 else col(i)

                def weigh(i, lo, hi):
                    j, n = place(i)
                    for h in range(lo, hi):
                        dve.wait_ge(exped, p_first[l] + H * i + h + 1)
                        view = logit_head(i, h)
                        dve.tensor_tensor_reduce(view, view, CNT[:, i, :], 1.0, 0.0, ALU.mult, ALU.add,
                                                 DEN[:, j, n + h:n + h + 1]).then_inc(p_ready, 1)

                def peak(i):
                    j, n = place(i)
                    if l == 0:
                        dve.wait_ge(tb_in[i % 2], 16 * (i // 2 + 1))
                        src = TB[i % 2].rearrange("p (n h) -> p h n", h=H)
                    else:
                        dve.wait_ge(tc_in[i], 16)
                        src = TC[i]
                    link(dve.tensor_reduce(MX[:, j, n:n + H], src, AX, ALU.max))
                    dve.tensor_scalar(NMX[:, j, n:n + H], MX[:, j, n:n + H], -1.0, None, ALU.mult).then_inc(negmax, 1)

                def out_rows(i):
                    j, n = place(i)
                    dve.wait_ge(p_ready, p_first[l] + H * (i + 1))
                    link(dve.tensor_scalar(RDEN[:, 0:H], DEN[:, j, n:n + H], 1.0, None, ALU.max))
                    link(dve.reciprocal(RDEN[:, 0:H], RDEN[:, 0:H]))
                    if l == 0:
                        dve.wait_ge(pv_done, H * (i + 1))
                        for s in range(2):
                            o = HACC[:, i, HALF * s:HALF * (s + 1)].rearrange("p (h d) -> p h d", h=4)
                            src = ACC[0:P, 512 * s:512 * s + HALF].rearrange("p (h d) -> p h d", h=4)
                            last = dve.tensor_tensor(o, src, RDEN[:, 4 * s:4 * s + 4].unsqueeze(2).to_broadcast([P, 4, HD]), ALU.mult)
                        last.then_inc(acc_free, 1)
                        dve.wait_ge(acc_free, i + 1)
                    else:
                        g = G[("pv1", i)]
                        ready(dve, g)
                        dve.tensor_scalar(split(HACC[:, i, :]), halves(buf(g)), RDEN[:, 0:1], None, ALU.mult)\
                           .then_inc(copied[g % NPS], 1)
                        read_out(dve, g)
                    dve.tensor_scalar(MN[:, i % 2, :], HACC[:, i, :], 0.0, None, ALU.min).then_inc(min_ok, 1)

                def affine(i):
                    k = norm_no[(f"ln{l}", i)]
                    c = k % NCOL
                    dve.wait_ge(lnp_in, 32 * (l + 1))
                    dve.wait_ge(rstd_ok, k + 1)
                    link(dve.scalar_tensor_tensor(out=HACC[:, i, :], in0=HACC[:, i, :], scalar=NMU[:, c:c + 1], in1=LNW,
                                                  op0=ALU.add, op1=ALU.mult))
                    if l == 0:
                        dve.scalar_tensor_tensor(out=XN[:, i, :], in0=HACC[:, i, :], scalar=RSTD[:, c:c + 1], in1=LNB,
                                                 op0=ALU.mult, op1=ALU.add).then_inc(feat, 1)
                    else:
                        link(dve.scalar_tensor_tensor(out=XRES[:, i, :], in0=HACC[:, i, :], scalar=RSTD[:, c:c + 1],
                                                      in1=XRES[:, i, :], op0=ALU.mult, op1=ALU.add))

                dve.wait_ge(rows_out, 32 * TT * (l + 1))
                if l == 0:
                    peak(0)
                    for i in range(TT):
                        weigh(i, 0, 2)
                        if i >= 2:
                            elu(i - 2)
                        if i >= 1:
                            out_rows(i - 1)
                        weigh(i, 2, 6)
                        if i + 1 < TT:
                            peak(i + 1)
                        weigh(i, 6, 8)
                        if i >= 2:
                            stats("ln0", HACC, i - 2)
                    affine(0)
                    elu(TT - 2)
                    out_rows(TT - 1)
                    stats("ln0", HACC, TT - 2)
                    affine(1)
                    affine(2)
                    elu(TT - 1)
                    stats("ln0", HACC, TT - 1)
                    affine(3)
                    affine(4)
                else:
                    dve.wait_ge(lnp_in, 64)
                    for t in range(TT):
                        last = dve.tensor_tensor(XRES[:, t, :], XRES[:, t, :], LNB, ALU.add)
                    link(last)
                    for i in range(TT + 5):
                        if i < TT:
                            peak(i)
                        if 0 <= i - 1 < TT:
                            weigh(i - 1, 0, 1)
                        if 0 <= i - 3 < TT:
                            out_rows(i - 3)
                        if 0 <= i - 4 < TT:
                            elu(i - 4)
                            stats("ln1", HACC, i - 4)
                        if 0 <= i - 5 < TT:
                            affine(i - 5)
                            stats("ffn", XRES, i - 5)
            dve.wait_ge(feat, 3 * TT)
            link(dve.tensor_reduce(SX, XN, AX, ALU.add))
            dve.wait_ge(bn_in, 16 * 5)
            dve.tensor_scalar(BNR, BNV[:, 4, :], EPS, None, ALU.add).then_inc(bnv_ok, 1)
            dve.wait_ge(bnr_ok, 1)
            link(dve.tensor_tensor(BNA, BNA, BNV[:, 1, :], ALU.mult))
            link(dve.tensor_tensor(BNB, BNV[:, 0, :], BNV[:, 3, :], ALU.subtract))
            link(dve.tensor_tensor(BNB, BNB, BNA, ALU.mult))
            dve.tensor_tensor(BNB, BNB, BNV[:, 2, :], ALU.add).then_inc(bn_ok, 1)

            def pick(g, t, q):
                ready(dve, g)
                prod = SELP.rearrange("p (k v b) -> p k v b", k=16, v=2)
                dve.tensor_tensor(prod, buf(g)[0:P, :].rearrange("p (k v b) -> p k v b", k=16, v=2),
                                       OHB[:, 16 * q:16 * q + 16, :].unsqueeze(2).to_broadcast([P, 16, 2, 32]), ALU.mult)\
                   .then_inc(copied[g % NPS], 1)
                read_out(dve, g)
                dve.tensor_reduce(WDC[:, t, 16 * q:16 * q + 16], prod[:, :, 0, :], AX, ALU.add)
                link(dve.tensor_reduce(WUC[:, t, 16 * q:16 * q + 16], prod[:, :, 1, :], AX, ALU.add))

            def add_down(t):
                g = G[("down", t)]
                ready(dve, g)
                dve.tensor_tensor(split(XRES[:, t, :]), halves(buf(g)), split(XRES[:, t, :]), ALU.add)\
                   .then_inc(copied[g % NPS], 1)

            for item in sched:
                g = G[item]
                if item[0] == "sc":
                    t, h = divmod(item[1], PH)
                    s = SC[item[1] % 2]
                    read_out(dve, g)
                    v = V16[:, t, KNN * h:KNN * (h + 1)]
                    k = IDXK[:, KNN * h:KNN * (h + 1)]
                    link(dve.max(v[:, 0:8], s))
                    dve.max_index(k[:, 0:8], v[:, 0:8], s)
                    link(dve.match_replace(WK, v[:, 0:8], s, -3.0e38))
                    link(dve.max(v[:, 8:16], WK))
                    dve.max_index(k[:, 8:16], v[:, 8:16], WK).then_inc(sc_used, 1)
                    dve.wait_ge(sc_used, item[1] + 1)
                    if h == PH - 1:
                        dve.tensor_scalar(IDA, IDXK, 5, None, ALU.logical_shift_right)
                        link(dve.tensor_scalar(IDB, IDXK, 31, None, ALU.bitwise_and))
                        iota = IO32.unsqueeze(1).to_broadcast([P, HK, 32])
                        link(dve.tensor_copy(IDKF[:, 0, :], IDA))
                        if t:
                            ready(dve, G[("oha", t - 1, 1)])
                        dve.tensor_tensor(OHA, IDKF[:, 0, :].unsqueeze(2).to_broadcast([P, HK, 32]), iota, ALU.is_equal)\
                           .then_inc(oha_ok, 1)
                        dve.wait_ge(oha_ok, t + 1)
                        link(dve.tensor_copy(IDKF[:, 0, :], IDB))
                        link(dve.tensor_tensor(OHB, IDKF[:, 0, :].unsqueeze(2).to_broadcast([P, HK, 32]), iota, ALU.is_equal))
                elif item[0] == "z" and item[1] % 2 == 1:
                    m = item[1] // 2
                    ready(dve, g)
                    read_out(dve, G[("z", item[1] - 1)])
                    dve.tensor_tensor(nodes(GS[:, m, :]), nodes(SIL[m % 2]), tiles(buf(g)), ALU.mult)\
                       .then_inc(copied[g % NPS], 1)
                elif item[0] == "pick":
                    pick(g, item[1], item[2])
                elif item[0] == "down":
                    add_down(item[1])
            for t in range(TT):
                last = dve.tensor_scalar(XDV[:, t, :], WDC[:, t, :], SX[:, t:t + 1], None, ALU.mult)
            last.then_inc(xd_ok, 1)
            v4 = V16.rearrange("p t (h k) -> p (t h) k", h=PH)
            g4 = GAT.rearrange("p t (h k) -> p (t h) k", h=PH)
            km, ks = KM.rearrange("p t h -> p (t h)"), KS.rearrange("p t h -> p (t h)")
            link(dve.tensor_reduce(km, v4, AX, ALU.max))
            dve.tensor_tensor(g4, v4, km.unsqueeze(2).to_broadcast([P, TT * PH, KNN]), ALU.subtract).then_inc(kgate, 1)
            for t in range(TT):
                last = dve.tensor_tensor(CNT[:, t, t * P:(t + 1) * P], CNT[:, t, t * P:(t + 1) * P], IDENT, ALU.add)
            link(last)
            dve.tensor_scalar(MB, CNT, 0.0, NEG, ALU.is_equal, ALU.mult)
            link(dve.memset(ONES, 1.0))
            add_down(2)
            add_down(3)
            for pair in range(2):
                g = G["peer"] + 2 * pair + 1
                ready(dve, g)
                read_out(dve, g - 1)
                dve.tensor_tensor(nodes(ZG[:, pair, :]), nodes(SIL[pair][0:88, :]), tiles(buf(g), 88), ALU.mult)\
                   .then_inc(copied[g % NPS], 1)
            dve.wait_ge(kexp, 1)
            link(dve.tensor_reduce(ks, g4, AX, ALU.add))
            link(dve.reciprocal(ks, ks))
            link(dve.tensor_tensor(g4, g4, ks.unsqueeze(2).to_broadcast([P, TT * PH, KNN]), ALU.mult))
            link(dve.tensor_tensor(GAT, GAT, WUC, ALU.mult))
            add_down(4)
            g = G["peer_out"]
            ready(dve, g)
            dve.tensor_tensor(GAT, GAT, buf(g)[0:P, 0:TT * HK].rearrange("p (t k) -> p t k", t=TT), ALU.mult)\
               .then_inc(copied[g % NPS], 1)
            read_out(dve, g)
            link(dve.tensor_reduce(CMB, GAT, AX, ALU.add))
            for t in range(TT):
                last = dve.tensor_scalar(XRES[:, t, :], XRES[:, t, :], CMB[:, t:t + 1], None, ALU.add)
                link(last)
                stats("gat", XRES, t)
            for l in range(2):
                dve.wait_ge(gb_in, 96)
                att_s, att_d, bias = GB[3 * l:3 * l + 3]
                if l == 1:
                    for t in range(TT):
                        last = dve.tensor_tensor(XRES[:, t, :], XRES[:, t, :], bias, ALU.add)
                    link(last)
                for t in range(TT):
                    read_out(dve, G[(("h", l), t)])
                    link(dve.tensor_tensor_reduce(HACC[:, 0, :], NODE[:, t, :], att_s, 1.0, 0.0, ALU.mult, ALU.add, AS[:, t:t + 1]))
                    dve.tensor_scalar(DG[:, t, :], IDENT, AS[:, t:t + 1], None, ALU.mult).then_inc(diag_ok, 1)
                    link(dve.tensor_tensor_reduce(HACC[:, 0, :], NODE[:, t, :], att_d, 1.0, 0.0, ALU.mult, ALU.add, AD[:, t:t + 1]))
                read_out(dve, G[f"asb{l}"])

                def edge_logits(i):
                    e = EB[i]
                    j, n = col(i)
                    link(dve.tensor_scalar(e, ASB, AD[:, i:i + 1], None, ALU.add))
                    link(dve.scalar_tensor_tensor(out=e, in0=e, scalar=0.2, in1=e, op0=ALU.mult, op1=ALU.max))
                    link(dve.tensor_tensor(e, e, MB[:, i, :], ALU.add))
                    link(dve.tensor_reduce(MX[:, j, n:n + 1], e, AX, ALU.max))
                    dve.tensor_scalar(NMX[:, j, n:n + 1], MX[:, j, n:n + 1], -1.0, None, ALU.mult).then_inc(negmax, 1)

                def edge_weights(i):
                    e = EB[i]
                    j, n = col(i)
                    dve.wait_ge(exped, p_first[2 + l] + i + 1)
                    dve.tensor_tensor_reduce(e, e, CNT[:, i, :], 1.0, 0.0, ALU.mult, ALU.add, DEN[:, j, n:n + 1]).then_inc(p_ready, 1)

                def node_out(i):
                    j, n = col(i)
                    dve.wait_ge(p_ready, p_first[2 + l] + i + 1)
                    link(dve.reciprocal(RDEN[:, 0:1], DEN[:, j, n:n + 1]))
                    g = G[(f"gv{l}", i)]
                    ready(dve, g)
                    dst = HACC if l == 0 else XRES
                    dve.scalar_tensor_tensor(out=split(dst[:, i, :]), in0=halves(buf(g)), scalar=RDEN[:, 0:1],
                                             in1=split(bias if l == 0 else XRES[:, i, :]),
                                             op0=ALU.mult, op1=ALU.add).then_inc(copied[g % NPS], 1)
                    read_out(dve, g)
                    if l == 0:
                        dve.tensor_scalar(XN[:, i, :], HACC[:, i, :], 0.0, None, ALU.max).then_inc(feat, 1)
                    else:
                        stats("moe", XRES, i)

                for i in range(TT + 3):
                    if i < TT:
                        edge_logits(i)
                    if 0 <= i - 1 < TT:
                        edge_weights(i - 1)
                    if 0 <= i - 3 < TT:
                        node_out(i - 3)
            def low_weights(n):
                dve.wait_ge(w_high, n + 1)
                dve.tensor_tensor(WLO[n % 2], WRAW[wraw(n)[0]], WHI[n % 2], ALU.subtract).then_inc(w_low, 1)

            dve.memset(ZEROS, 0.0).then_inc(zeros_ok, 1)
            low_weights(0)
            g = G["route"]
            ready(dve, g)
            dve.wait_ge(x_high, TT)
            dve.tensor_scalar(XLP[:, KC * N:KC * N + 2], BNA[:, 0:2], 0.0, None, ALU.mult)
            dve.tensor_scalar(XHP[:, KC * N:KC * N + 2], BNA[:, 0:2], 0.0, None, ALU.mult).then_inc(x_low, 1)
            for c in range(KC):
                dve.tensor_tensor(XTL[:, c, :], XTS[:, c, :], XTH[:, c, :], ALU.subtract).then_inc(x_low, 1)
            low_weights(1)
            dve.tensor_tensor(RT, buf(g)[0:P, 0:64 * TT].rearrange("p (t n) -> p t n", t=TT)[:, :, 0:36],
                                   BR.unsqueeze(1).to_broadcast([P, TT, 36]), ALU.add).then_inc(copied[g % NPS], 1)
            read_out(dve, g)
            dve.memset(RG, NEG)
            dve.memset(RE, NEG)
            dve.memset(REPG, NEG)
            link(dve.memset(REPE, NEG))
            glog = RT[:, :, 0:4]
            elog = RT[:, :, 4:36].rearrange("p t (g e) -> p t g e", g=4)
            dve.tensor_copy(RG[:, :, 0:4], glog)
            for t in range(TT):
                last = dve.tensor_copy(RE[:, 4 * t:4 * t + 4, 0:8], elog[:, t, :, :])
            link(last)
            for t in range(TT):
                dve.max(TOPG[:, t, :], RG[:, t, :])
            for j in range(4 * TT):
                last = dve.max(TOPE[:, j, :], RE[:, j, :])
            link(last)
            dve.tensor_copy(REPG[:, :, 0:2], TOPG[:, :, 0:2])
            link(dve.tensor_copy(REPE[:, :, 0:2], TOPE[:, :, 0:2]))
            for t in range(TT):
                dve.match_replace(RGO[:, t, :], REPG[:, t, :], RG[:, t, :], 3.0e38)
            for j in range(4 * TT):
                dve.match_replace(REO[:, j, :], REPE[:, j, :], RE[:, j, :], 3.0e38)
            dve.tensor_tensor(GV, RG[:, :, 0:4], TOPG[:, :, 0:1].to_broadcast([P, TT, 4]), ALU.subtract)
            link(dve.tensor_tensor(EV, RE[:, :, 0:8], TOPE[:, :, 0:1].to_broadcast([P, 4 * TT, 8]), ALU.subtract))
            dve.tensor_scalar(RGO[:, :, 0:4], RGO[:, :, 0:4], 3.0e38, None, ALU.is_equal)
            dve.tensor_scalar(REO[:, :, 0:8], REO[:, :, 0:8], 3.0e38, None, ALU.is_equal).then_inc(rt_ok, 1)
            low_weights(2)
            dve.wait_ge(rexp, 2)
            dve.tensor_tensor(GV, GV, RGO[:, :, 0:4], ALU.mult)
            link(dve.tensor_tensor(EV, EV, REO[:, :, 0:8], ALU.mult))
            dve.tensor_reduce(GSM, GV, AX, ALU.add)
            link(dve.tensor_reduce(ESM, EV, AX, ALU.add))
            dve.reciprocal(GSM, GSM)
            link(dve.reciprocal(ESM, ESM))
            link(dve.tensor_tensor(GV, GV, GSM.unsqueeze(2).to_broadcast([P, TT, 4]), ALU.mult))
            gflat = GV.rearrange("p t g -> p (t g)")
            link(dve.tensor_tensor(ESM, ESM, gflat, ALU.mult))
            link(dve.tensor_tensor(COMB.rearrange("p t (g e) -> p (t g) e", g=4), EV,
                                   ESM.unsqueeze(2).to_broadcast([P, 4 * TT, 8]), ALU.mult))
            for k in range(3):
                link(dve.tensor_copy(CPB, COMB))
                last = dve.tensor_copy(C3[:, :, EXP * k:EXP * (k + 1)], CPB)
                if k < 2:
                    link(last)
                    link(dve.tensor_tensor(COMB, COMB, C3[:, :, EXP * k:EXP * (k + 1)], ALU.subtract))
            last.then_inc(comb_ok, 1)
            low_weights(3)
            for m in range(XC):
                g = G[("cb", m)]
                ready(dve, g)
                read_out(dve, G[("up", m)])
                dve.tensor_tensor(GT[:, m % 2, :], GT[:, m % 2, :], across(buf(g)), ALU.mult).then_inc(copied[g % NPS], 1)
                read_out(dve, g)
                if m >= 2:
                    low_weights(m + 2)
                dve.wait_ge(h_high, m + 1)
                dve.tensor_tensor(HSL[:, m, :], GT[:, m % 2, :], HSH[:, m, :], ALU.subtract).then_inc(h_low, 1)
            for n in range(XC + 2, 2 * XC):
                low_weights(n)
            for t in range(TT):
                dve.wait_ge(y_ready, t // 2 + 1)
                first, rest = y_parts(t)
                dve.tensor_tensor(XRES[:, t, 0:512], first, XRES[:, t, 0:512], ALU.add)
                dve.tensor_tensor(XRES[:, t, 512:D], rest, XRES[:, t, 512:D], ALU.add).then_inc(y_added, 1)


def _layout(i):
    c = np.ascontiguousarray
    col = lambda v, k: c(v.reshape(k, 128).T)
    r = {n: i[n] for n in ("x", "src", "dst")}
    for n in ("W1s", "b1s", "W1d", "b1d", "ln1_w", "ln1_b", "Wos", "bos", "Wod", "bod", "lno_w", "lno_b"):
        r[n] = i["L0_gnn_" + n]
    r["attn1"], r["attno"] = col(i["L0_gnn_attn1"].reshape(-1), 6), i["L0_gnn_attno"].reshape(-1)
    f = "L0_ffn_"
    r["wqT"] = c(i[f + "wq"].T)
    for n in ("bq", "bn_gamma", "bn_beta", "bn_mean", "bn_var"):
        r[n] = col(i[f + n], 4)
    r["keysT"] = c(i[f + "keys"].transpose(0, 2, 1))
    r["w_down"], r["w_up"] = i[f + "w_down_tab"], i[f + "w_up_tab"]
    for n in ("a_w1", "a_w2", "a_w3", "s_w1", "s_w2", "s_w3"):
        r[n + "T"] = c(i[f + n].T)
    f = "L1_gnn_"
    for n, m in (("G1", "W1"), ("as1", "att_src1"), ("ad1", "att_dst1"), ("gb1", "b1"),
                 ("G2", "W2"), ("as2", "att_src2"), ("ad2", "att_dst2"), ("gb2", "b2")):
        r[n] = i[f + m]
    f = "L1_ffn_"
    wr = np.concatenate([i[f + "Wg"], i[f + "Wge"].transpose(1, 0, 2).reshape(768, 32)], axis=1)
    r["Wr"] = c(wr.reshape(6, 128, 36).transpose(1, 0, 2).reshape(128, 216))
    r["br"] = np.concatenate([i[f + "bg"], i[f + "bge"].reshape(-1)])
    r["W1c"] = c(i[f + "W1"].transpose(1, 0, 2).reshape(768, 3072))
    r["b1c"] = col(i[f + "b1"].reshape(-1), 24)
    r["W2"] = i[f + "W2"].reshape(3072, 768)
    r["b2"] = i[f + "b2"]
    return r


def kernel(**inputs):
    import concourse.bacc as _bacc
    from concourse.bass_utils import run_bass_kernel_spmd as _run

    nc = _bacc.Bacc("TRN2", target_bir_lowering=False, num_devices=1)
    arrays, args = {}, {}
    for name, v in _layout({k: np.asarray(v) for k, v in inputs.items()}).items():
        v = np.ascontiguousarray(v)
        if v.dtype == np.int32:
            v = v.view(np.uint32)
        arrays["in_" + name] = v
        args[name] = nc.dram_tensor("in_" + name, v.shape, mybir.dt.from_np(v.dtype), kind="ExternalInput").ap()
    out = nc.dram_tensor("out_0", (N, D), F32, kind="ExternalOutput").ap()
    emit(nc, args, out)
    r = _run(nc, [arrays], core_ids=[0])
    return r.results[0]["out_0"]
```
